# Optimizing a Trainium2 kernel written in Bass

```python
import numpy as np
import jax
import jax.numpy as jnp

def _softmax(x, axis=-1):
    return jax.nn.softmax(x, axis=axis)

def _gelu(x):
    return jax.nn.gelu(x, approximate=True)

def _silu(x):
    return jax.nn.silu(x)

def _sigmoid(x):
    return jax.nn.sigmoid(x)

def _layernorm(x, axis=-1, eps=1e-05):
    m = jnp.mean(x, axis=axis, keepdims=True)
    v = jnp.var(x, axis=axis, keepdims=True)
    return (x - m) / jnp.sqrt(v + eps)

def _scatter_add(tgt, idx, src, axis=0):
    return tgt.at[idx].add(src)

def _segment_sum(src, seg, n):
    return jax.ops.segment_sum(src, seg, n)
kernel_name = 'mk_prb_d2_jaxref_r8_318fe0'

def setup_inputs(seed: int=0):
    np.random.seed(seed)
    _w = jnp.asarray

    def _L0_attn_setup():
        import jax, jax.numpy as jnp
        import numpy as np
        HEADS = 4
        DIM_HEAD = 32
        EPS = 1e-05
        key = jax.random.key(seed)
        ks = jax.random.split(key, 6)
        b, n, dim = (8, 512, 128)
        hidden = HEADS * DIM_HEAD
        x = jax.random.normal(ks[0], (b, n, dim), dtype=jnp.float32)
        gamma = jnp.ones((1, 1, dim), dtype=jnp.float32)
        beta = jnp.zeros((1, 1, dim), dtype=jnp.float32)
        w_qkv = jax.random.normal(ks[1], (dim, hidden * 3), dtype=jnp.float32) / np.sqrt(dim)
        w_out = jax.random.normal(ks[2], (hidden, dim), dtype=jnp.float32) / np.sqrt(hidden)
        b_out = jnp.zeros((dim,), dtype=jnp.float32)
        return {'x': x, 'gamma': gamma, 'beta': beta, 'w_qkv': w_qkv, 'w_out': w_out, 'b_out': b_out}
    _L0_attn_in = _L0_attn_setup()

    def _L0_ffn_setup():
        import jax, jax.numpy as jnp
        import numpy as np
        DIM = 128
        HIDDEN = 256
        N_EXPERTS = 8
        TOP_K = 2
        EPS = 1e-06

        def rms_norm(x, scale, eps=EPS):
            ms = jnp.mean(jnp.square(x.astype(jnp.float32)), axis=-1, keepdims=True)
            s = scale.astype(jnp.float32) * jax.lax.rsqrt(ms + eps)
            return x * s.astype(x.dtype)

        def moe_linear(xf, ids, W):
            E = W.shape[0]
            out = jnp.zeros((xf.shape[0], W.shape[1]), dtype=xf.dtype)
            for e in range(E):
                out = out + jnp.where((ids == e)[:, None], xf @ W[e].T, 0.0)
            return out
        key = jax.random.key(seed)
        k1, k2, k3, k4 = jax.random.split(key, 4)
        x = jax.random.normal(k1, (4, 512, DIM), dtype=jnp.float32)
        norm_scale = jnp.ones((DIM,), dtype=jnp.float32)
        w_router = jax.random.normal(k2, (N_EXPERTS, DIM), dtype=jnp.float32) / np.sqrt(DIM)
        lim_up = np.sqrt(6.0 / (DIM + 2 * HIDDEN))
        w_up = jax.random.uniform(k3, (N_EXPERTS, 2 * HIDDEN, DIM), dtype=jnp.float32, minval=-lim_up, maxval=lim_up)
        lim_dn = np.sqrt(6.0 / (HIDDEN + DIM))
        w_down = jax.random.uniform(k4, (N_EXPERTS, DIM, HIDDEN), dtype=jnp.float32, minval=-lim_dn, maxval=lim_dn)
        return {'x': x, 'norm_scale': norm_scale, 'w_router': w_router, 'w_up': w_up, 'w_down': w_down}
    _L0_ffn_in = _L0_ffn_setup()

    def _L1_attn_setup():
        import math
        import jax, jax.numpy as jnp
        import numpy as np
        HEADS = 16
        DIM_HEAD = 64
        NUM_NULL_KV = 2
        ATTN_SCALE = 8.0
        LN_EPS = 1e-05

        def _alibi_slopes(heads):
            start = 2.0 ** (-2.0 ** (-(math.log2(heads) - 3.0)))
            return np.array([start * start ** i for i in range(heads)], dtype=np.float32)

        def _l2norm(t):
            return t / jnp.maximum(jnp.linalg.norm(t, axis=-1, keepdims=True), 1e-12)
        key = jax.random.key(seed)
        ks = jax.random.split(key, 5)
        b, n, dim = (4, 256, 128)
        return {'x': jax.random.normal(ks[0], (b, n, dim), dtype=jnp.float32), 'gamma': jnp.ones((dim,), dtype=jnp.float32), 'w_q': jax.random.normal(ks[1], (dim, HEADS * DIM_HEAD), dtype=jnp.float32) * 0.02, 'w_kv': jax.random.normal(ks[2], (dim, 2 * HEADS * DIM_HEAD), dtype=jnp.float32) * 0.02, 'null_kv': jax.random.normal(ks[3], (HEADS, 2 * NUM_NULL_KV, DIM_HEAD), dtype=jnp.float32), 'q_scale': jnp.ones((DIM_HEAD,), dtype=jnp.float32), 'k_scale': jnp.ones((DIM_HEAD,), dtype=jnp.float32), 'w_out': jax.random.normal(ks[4], (HEADS * DIM_HEAD, dim), dtype=jnp.float32) * 0.02}
    _L1_attn_in = _L1_attn_setup()

    def _L1_ffn_setup():
        import jax, jax.numpy as jnp
        import numpy as np
        N_EXPERTS = 8
        N_GROUP = 4
        TOPK_GROUP = 2
        TOP_K = 2
        HIDDEN = 128
        INTER = 256
        B, S = (1, 128)

        def _grouped_topk(scores):
            T, E = scores.shape
            per_group = E // N_GROUP
            group_scores = scores.reshape(T, N_GROUP, per_group).max(-1)
            _, gidx = jax.lax.top_k(group_scores, TOPK_GROUP)
            gmask = jnp.zeros((T, N_GROUP), scores.dtype).at[jnp.arange(T)[:, None], gidx].set(1.0)
            smask = jnp.repeat(gmask, per_group, axis=1)
            masked = jnp.where(smask > 0, scores, 0.0)
            topk_w, topk_ids = jax.lax.top_k(masked, TOP_K)
            topk_w = topk_w / topk_w.sum(-1, keepdims=True)
            return (topk_ids, topk_w)
        key = jax.random.key(seed)
        k1, k2, k3, k4 = jax.random.split(key, 4)
        return {'hidden_states': jax.random.normal(k1, (B, S, HIDDEN), jnp.float32), 'gate_w': jax.random.normal(k2, (N_EXPERTS, HIDDEN), jnp.float32) * 0.02, 'w13_weight': jax.random.normal(k3, (N_EXPERTS, 2 * INTER, HIDDEN), jnp.float32) * 0.02, 'w2_weight': jax.random.normal(k4, (N_EXPERTS, HIDDEN, INTER), jnp.float32) * 0.02}
    _L1_ffn_in = _L1_ffn_setup()
    _d = {'L0_attn_x': _L0_attn_in['x'], 'L0_attn_gamma': _L0_attn_in['gamma'], 'L0_attn_beta': _L0_attn_in['beta'], 'L0_attn_w_qkv': _L0_attn_in['w_qkv'], 'L0_attn_w_out': _L0_attn_in['w_out'], 'L0_attn_b_out': _L0_attn_in['b_out'], 'L0_ffn_norm_scale': _L0_ffn_in['norm_scale'], 'L0_ffn_w_router': _L0_ffn_in['w_router'], 'L0_ffn_w_up': _L0_ffn_in['w_up'], 'L0_ffn_w_down': _L0_ffn_in['w_down'], 'L1_attn_gamma': _L1_attn_in['gamma'], 'L1_attn_w_q': _L1_attn_in['w_q'], 'L1_attn_w_kv': _L1_attn_in['w_kv'], 'L1_attn_null_kv': _L1_attn_in['null_kv'], 'L1_attn_q_scale': _L1_attn_in['q_scale'], 'L1_attn_k_scale': _L1_attn_in['k_scale'], 'L1_attn_w_out': _L1_attn_in['w_out'], 'L1_ffn_gate_w': _L1_ffn_in['gate_w'], 'L1_ffn_w13_weight': _L1_ffn_in['w13_weight'], 'L1_ffn_w2_weight': _L1_ffn_in['w2_weight']}
    _x0 = _d['L0_attn_x']
    _d['L0_attn_x'] = jax.random.normal(jax.random.fold_in(jax.random.key(seed), 1), (8, 256, 128), dtype=_x0.dtype)
    del _x0
    return _d

def reference(L0_attn_x, L0_attn_gamma, L0_attn_beta, L0_attn_w_qkv, L0_attn_w_out, L0_attn_b_out, L0_ffn_norm_scale, L0_ffn_w_router, L0_ffn_w_up, L0_ffn_w_down, L1_attn_gamma, L1_attn_w_q, L1_attn_w_kv, L1_attn_null_kv, L1_attn_q_scale, L1_attn_k_scale, L1_attn_w_out, L1_ffn_gate_w, L1_ffn_w13_weight, L1_ffn_w2_weight):

    def _L0_attn_ref(x, gamma, beta, w_qkv, w_out, b_out):
        import jax, jax.numpy as jnp
        import numpy as np
        HEADS = 4
        DIM_HEAD = 32
        EPS = 1e-05
        b, n, dim = x.shape
        mean = jnp.mean(x, axis=2, keepdims=True)
        var = jnp.var(x, axis=2, keepdims=True)
        xn = (x - mean) / jnp.sqrt(var + EPS) * gamma + beta
        qkv = jnp.einsum('bnc,ck->bnk', xn, w_qkv)
        q, k, v = jnp.split(qkv, 3, axis=2)

        def to_heads(t):
            return t.reshape(b, n, HEADS, DIM_HEAD)
        q, k, v = (to_heads(q), to_heads(k), to_heads(v))
        q = q * DIM_HEAD ** (-0.5)
        k = jax.nn.softmax(k, axis=1)
        context = jnp.einsum('bnhd,bnhe->bhde', k, v)
        out = jnp.einsum('bhde,bnhd->bnhe', context, q)
        out = out.reshape(b, n, HEADS * DIM_HEAD)
        out = jnp.einsum('bnk,kc->bnc', out, w_out) + b_out
        return out + x

    def _L0_ffn_ref(x, norm_scale, w_router, w_up, w_down):
        import jax, jax.numpy as jnp
        import numpy as np
        DIM = 128
        HIDDEN = 256
        N_EXPERTS = 8
        TOP_K = 2
        EPS = 1e-06

        def rms_norm(x, scale, eps=EPS):
            ms = jnp.mean(jnp.square(x.astype(jnp.float32)), axis=-1, keepdims=True)
            s = scale.astype(jnp.float32) * jax.lax.rsqrt(ms + eps)
            return x * s.astype(x.dtype)

        def moe_linear(xf, ids, W):
            E = W.shape[0]
            out = jnp.zeros((xf.shape[0], W.shape[1]), dtype=xf.dtype)
            for e in range(E):
                out = out + jnp.where((ids == e)[:, None], xf @ W[e].T, 0.0)
            return out
        B, S, D = x.shape
        skip = x
        xn = rms_norm(x, norm_scale)
        scores = (xn @ w_router.T).astype(jnp.float32)
        scores_topk, idx = jax.lax.top_k(scores, TOP_K)
        weights = jax.nn.softmax(scores_topk, axis=-1)
        xf = jnp.broadcast_to(xn[..., None, :], (B, S, TOP_K, D)).reshape(-1, D)
        ids = idx.reshape(-1)
        up = moe_linear(xf, ids, w_up)
        u, gate = jnp.split(up, 2, axis=-1)
        h = u * jax.nn.silu(gate)
        down = moe_linear(h, ids, w_down)
        down = down.reshape(B, S, TOP_K, D)
        out = jnp.sum(down * weights[..., None].astype(down.dtype), axis=-2)
        return out + skip

    def _L1_attn_ref(x, gamma, w_q, w_kv, null_kv, q_scale, k_scale, w_out):
        import math
        import jax, jax.numpy as jnp
        import numpy as np
        HEADS = 16
        DIM_HEAD = 64
        NUM_NULL_KV = 2
        ATTN_SCALE = 8.0
        LN_EPS = 1e-05

        def _alibi_slopes(heads):
            start = 2.0 ** (-2.0 ** (-(math.log2(heads) - 3.0)))
            return np.array([start * start ** i for i in range(heads)], dtype=np.float32)

        def _l2norm(t):
            return t / jnp.maximum(jnp.linalg.norm(t, axis=-1, keepdims=True), 1e-12)
        b, n, dim = x.shape
        mu = jnp.mean(x, axis=-1, keepdims=True)
        var = jnp.mean(jnp.square(x - mu), axis=-1, keepdims=True)
        xn = (x - mu) * jax.lax.rsqrt(var + LN_EPS) * gamma
        q = (xn @ w_q).reshape(b, n, HEADS, DIM_HEAD).transpose(0, 2, 1, 3)
        kv = xn @ w_kv
        k, v = jnp.split(kv, 2, axis=-1)
        k = k.reshape(b, n, HEADS, DIM_HEAD).transpose(0, 2, 1, 3)
        v = v.reshape(b, n, HEADS, DIM_HEAD).transpose(0, 2, 1, 3)
        nkv = null_kv.reshape(HEADS, NUM_NULL_KV, 2, DIM_HEAD)
        nk = jnp.broadcast_to(nkv[:, :, 0][None], (b, HEADS, NUM_NULL_KV, DIM_HEAD))
        nv = jnp.broadcast_to(nkv[:, :, 1][None], (b, HEADS, NUM_NULL_KV, DIM_HEAD))
        k = jnp.concatenate([nk, k], axis=2)
        v = jnp.concatenate([nv, v], axis=2)
        q = _l2norm(q) * q_scale
        k = _l2norm(k) * k_scale
        sim = jnp.einsum('bhid,bhjd->bhij', q, k) * ATTN_SCALE
        j = n + NUM_NULL_KV
        rows = jnp.arange(n)
        cols = jnp.arange(j)
        dist = -jnp.abs(cols[None, :] - (rows[:, None] + NUM_NULL_KV)).astype(sim.dtype)
        slopes = jnp.asarray(_alibi_slopes(HEADS))
        sim = sim + dist[None, None] * slopes[None, :, None, None]
        causal_mask = cols[None, :] > rows[:, None] + NUM_NULL_KV
        neg = -jnp.finfo(sim.dtype).max
        sim = jnp.where(causal_mask[None, None], neg, sim)
        attn = jax.nn.softmax(sim, axis=-1)
        out = jnp.einsum('bhij,bhjd->bhid', attn, v)
        out = out.transpose(0, 2, 1, 3).reshape(b, n, HEADS * DIM_HEAD)
        return out @ w_out

    def _L1_ffn_ref(hidden_states, gate_w, w13_weight, w2_weight):
        import jax, jax.numpy as jnp
        import numpy as np
        N_EXPERTS = 8
        N_GROUP = 4
        TOPK_GROUP = 2
        TOP_K = 2
        HIDDEN = 128
        INTER = 256
        B, S = (1, 128)

        def _grouped_topk(scores):
            T, E = scores.shape
            per_group = E // N_GROUP
            group_scores = scores.reshape(T, N_GROUP, per_group).max(-1)
            _, gidx = jax.lax.top_k(group_scores, TOPK_GROUP)
            gmask = jnp.zeros((T, N_GROUP), scores.dtype).at[jnp.arange(T)[:, None], gidx].set(1.0)
            smask = jnp.repeat(gmask, per_group, axis=1)
            masked = jnp.where(smask > 0, scores, 0.0)
            topk_w, topk_ids = jax.lax.top_k(masked, TOP_K)
            topk_w = topk_w / topk_w.sum(-1, keepdims=True)
            return (topk_ids, topk_w)
        Bm, Sm, H = hidden_states.shape
        x = hidden_states.reshape(-1, H)
        T = x.shape[0]
        scores = jax.nn.softmax(x @ gate_w.T, axis=-1)
        topk_ids, topk_w = _grouped_topk(scores)
        combine = jnp.zeros((T, N_EXPERTS), x.dtype).at[jnp.arange(T)[:, None], topk_ids].add(topk_w)
        gu = jnp.einsum('th,eih->tei', x, w13_weight)
        gate, up = (gu[..., :INTER], gu[..., INTER:])
        act = jax.nn.silu(gate) * up
        act = act * combine[:, :, None]
        out = jnp.einsum('tei,ehi->th', act, w2_weight)
        return out.reshape(Bm, Sm, H)
    x = L0_attn_x
    xn = _layernorm(x, axis=-1)
    x = x + _L0_attn_ref(xn, L0_attn_gamma, L0_attn_beta, L0_attn_w_qkv, L0_attn_w_out, L0_attn_b_out) + _L0_ffn_ref(xn, L0_ffn_norm_scale, L0_ffn_w_router, L0_ffn_w_up, L0_ffn_w_down)
    xn = _layernorm(x, axis=-1)
    x = x + _L1_attn_ref(xn, L1_attn_gamma, L1_attn_w_q, L1_attn_w_kv, L1_attn_null_kv, L1_attn_q_scale, L1_attn_k_scale, L1_attn_w_out) + _L1_ffn_ref(xn, L1_ffn_gate_w, L1_ffn_w13_weight, L1_ffn_w2_weight)
    return x

_drawn_inputs = setup_inputs


def setup_inputs(seed=0):
    import zlib

    import numpy as np

    out = dict(_drawn_inputs(seed))
    spreads = {'L0_attn_gamma': (1.0, 0.6),
     'L0_attn_beta': (0.0, 0.1),
     'L0_attn_b_out': (0.0, 0.1),
     'L0_ffn_norm_scale': (1.0, 0.567),
     'L1_attn_gamma': (1.0, 0.6),
     'L1_attn_q_scale': (1.0, 0.6),
     'L1_attn_k_scale': (1.0, 0.6)}
    factors = {'L1_attn_w_q': 3.581,
     'L1_attn_w_kv': 2.904,
     'L1_attn_null_kv': 3.992,
     'L1_ffn_gate_w': 8.0,
     'L1_ffn_w13_weight': 8.0,
     'L1_ffn_w2_weight': 8.0}
    for name, (base, spread) in spreads.items():
        noise = np.random.default_rng([zlib.crc32(name.encode()), seed]).standard_normal(out[name].shape)
        drawn = base * np.exp(spread * noise) if base else spread * noise
        out[name] = jnp.asarray(drawn.astype(out[name].dtype))
    for name, factor in factors.items():
        out[name] = (out[name] * factor).astype(out[name].dtype)
    return out
```

```python
from contextlib import ExitStack

import numpy as np

import concourse.bass as bass
from concourse import mybir

F32 = mybir.dt.float32
F32R = mybir.dt.float32r
U32 = mybir.dt.uint32
ALU = mybir.AluOpType
ACT = mybir.ActivationFunctionType
AX = mybir.AxisListType

P = 128
B, S, D = 8, 256, 128
T = S // P
E = 8
HID = 256
HB = HID // P
H0, DH0 = 4, 32
H1, DH1 = 16, 64
HD1 = H1 * DH1
HP = H1 // 2
NULL = 2
SIM_SCALE = 8.0
GROUPS = 4
LN_EPS, RMS_EPS = 1e-5, 1e-6
HALF = 8
STEPS = T * HP
FAR = 1e38


def slopes():
    start = 2.0 ** (-2.0 ** (-(np.log2(H1) - 3.0)))
    return [float(np.float32(start * start ** i)) for i in range(H1)]


class Progress:

    def __init__(self, sem, names):
        self.sem, self.names, self.per = sem, list(names), len(names)
        self.index = {n: i + 1 for i, n in enumerate(self.names)}
        self.next = 0

    def __call__(self, name):
        assert self.names[self.next % self.per] == name, (name, self.names[self.next % self.per])
        self.next += 1
        return self.sem, 1

    def at(self, b, name):
        if isinstance(b, int):
            b = min(b, B - 1)
        return self.sem, b * self.per + (2 * self.per + self.index[name])


def experts_at(p, m0, m1):
    first = range(E) if m0 else []
    second = [8, 10, 12, 14, 16, 17, 18, 19] if m0 else [1, 3, 5, 7, 9, 10, 11, 12]
    out = [(0, p)] if p in first else []
    return out + [(1, second.index(p))] if m1 and p in second else out


def moe_order(layer, first, second):
    out = []
    for p in range(STEPS + 6):
        out += [f"{n}{e}" for l, e in experts_at(p, True, True) if l == layer for n in first]
        out += [f"{n}{e}" for l, e in experts_at(p - 1, True, True) if l == layer for n in second]
    return out


def build(nc, x, w_small, w_up0, w_dn0, w_qkv1, w_out1, w_up1, w_dn1, null_k, null_v, consts, distance, out):
    ctx = ExitStack()
    with ctx:
        def sb(name, shape, dt=F32):
            return ctx.enter_context(nc.sbuf_tensor(name, shape, dt))

        def bank(name):
            return ctx.enter_context(nc.psum_tensor(name, [P, 512], F32))

        def sem(name):
            return ctx.enter_context(nc.semaphore(name))

        def progress(name, names):
            return Progress(sem(name), names)

        small = sb("small", [P, SMALL_COLS])
        cst = sb("cst", [P, CONST_COLS])
        up_h = [sb(f"up_h{i}", [P, E, 2 * HID], F32R) for i in range(2)]
        up_l = [sb(f"up_l{i}", [P, E, 2 * HID], F32R) for i in range(2)]
        down = [sb(f"down{i}", [P, E, HB, D]) for i in range(2)]
        qkv1 = sb("qkv1", [P, 3 * HD1])
        wout1 = sb("wout1", [P, HP, D])
        bias = sb("bias", [P, H1, S])
        nkw = sb("nkw", [NULL * H1, 2, DH1])
        nk_ss = sb("nk_ss", [NULL * H1, 4])
        nkbd = sb("nkbd", [P, HP, 2 * NULL])
        nvbd = sb("nvbd", [NULL * HALF, T, HALF * DH1])
        qscale = sb("qscale", [P, 1])
        halves = sb("halves", [P, 64])

        def cols(tile, table, name):
            at, n = table[name]
            return tile[:, at:at + n]

        ident = cols(cst, CONST, "ident")
        null_bias = cols(cst, CONST, "null_bias").rearrange("p (t n) -> p t n", t=T)
        head_mask = cols(cst, CONST, "head_mask")
        iota8 = cols(cst, CONST, "iota8")
        wq0, wk0, wv0 = (cols(small, SMALL, n) for n in ("wq0", "wk0", "wv0"))
        wout0, router0, router1 = (cols(small, SMALL, n) for n in ("wout0", "router0", "router1"))
        gamma0, beta0, rms_scale, gamma1 = (cols(small, SMALL, n) for n in ("gamma0", "beta0", "rms", "gamma1"))
        qs2, ks2 = (cols(small, SMALL, n) for n in ("qs2", "ks2"))
        b_out = cols(small, SMALL, "b_out")[0:1]
        ones_row = cols(cst, CONST, "ones")[0:1]

        x_in = sb("x_in", [P, T, D])
        xn = sb("xn", [P, T, D])
        tin = sb("tin", [P, 2 * T, D])
        stats = [sb(f"stats{i}", [P, T, 6]) for i in range(4)]
        mv = [sb(f"mv{i}", [P, T, 2]) for i in range(4)]
        var = [sb(f"var{i}", [P, 2 * T]) for i in range(4)]
        rstd = [sb(f"rstd{i}", [P, 2 * T]) for i in range(4)]
        start0 = sb("start0", [P, T, D])
        acc0 = sb("acc0", [P, T, D])
        start1 = sb("start1", [P, T, D])
        acc1 = sb("acc1", [P, T, D])
        xaT = sb("xaT", [P, S])
        xfT = sb("xfT", [P, S])
        xf_h = [sb(f"xf_h{i}", [P, S], F32R) for i in range(2)]
        xf_l = [sb(f"xf_l{i}", [P, S], F32R) for i in range(2)]
        nkmax = sb("nkmax", [P, 1])
        ksum = sb("ksum", [P, 2])
        keT = xn[:].rearrange("p t d -> p (t d)")
        qsT = sb("qsT", [P, S])
        vk = sb("vk", [P, 2, T, P])
        ctxT = sb("ctxT", [P, P])
        mix = sb("mix", [P, D])
        rt = [sb(f"rt{i}", [P, T, E]) for i in range(2)]
        prob = sb("prob", [P, T, E])
        gpad = sb("gpad", [P, T, E])
        gtop = sb("gtop", [P, T, E])
        gidx = sb("gidx", [P, T, E], U32)
        gidxf = sb("gidxf", [P, T, 2])
        gmask = sb("gmask", [P, T, 2, GROUPS])
        masked = sb("masked", [P, T, E])
        top = [sb(f"top{i}", [P, T, E]) for i in range(2)]
        topi = [sb(f"topi{i}", [P, T, E], U32) for i in range(2)]
        topf = [sb(f"topf{i}", [P, T, 2]) for i in range(2)]
        tw = [sb(f"tw{i}", [P, 8, T]) for i in range(2)]
        one = [sb(f"one{i}", [P, 2, T, E]) for i in range(2)]
        cw = [sb(f"cw{i}", [P, T, E]) for i in range(2)]
        qk = sb("qk", [P, 2, T, HD1])
        sq = sb("sq", [P, HD1 // 2])
        ss = sb("ss", [P, 2, T, H1])
        rn = sb("rn", [P, 2, T, H1])
        qkT = sb("qkT", [P, 2, HP, S])
        v = sb("v", [P, T, HD1])
        th = [sb(f"th{i}", [P, HB * S]) for i in range(2)]
        hid = [sb(f"hid{i}", [P, HB, S]) for i in range(2)]
        sn = sb("sn", [P, T, H1, NULL])
        nmin = sb("nmin", [P, T, H1])
        mneg = sb("mneg", [P, T, H1])
        lsum = sb("lsum", [P, T, H1])
        rl = sb("rl", [P, T, H1])
        prb = [sb(f"prb{i}", [P, 2, S]) for i in range(2)]
        prT = [sb(f"prT{i}", [P, 2, S]) for i in range(3)]
        pnd = sb("pnd", [P, HALF, NULL])
        pn = sb("pn", [P, HALF, NULL])
        pnT = sb("pnT", [NULL * HALF, P])
        o = sb("o", [P, HALF * DH1])
        oT = sb("oT", [P, 4, P])

        raw_up = [qkT[:].rearrange("p a b c -> p (a b c)"), qk[:].rearrange("p a b c -> p (a b c)")]
        dist = prb[0][:, 0]
        nk_sq = prT[0][0:NULL * H1, 0, 0:2 * DH1].rearrange("p (a d) -> p a d", a=2)

        b_gate, b_up, b_y = bank("b_gate"), bank("b_up"), bank("b_y")
        b_sim = [bank("b_simA"), bank("b_simB")]
        b_prT, b_pv, b_front = bank("b_prT"), bank("b_pv"), bank("b_front")
        turn_banks = [b_front, *b_sim]

        small_in, const_in, up0_in, dn0_in = (sem(n) for n in ("small_in", "const_in", "up0_in", "dn0_in"))
        qkv_in, wout_in, up1_in, dn1_in, null_in, dist_in = (sem(n) for n in ("qkv_in", "wout_in", "up1_in", "dn1_in", "null_in", "dist_in"))
        half_set = sem("half_set")
        pad_set = sem("pad_set")
        bias_set = sem("bias_set")
        qscale_set = sem("qscale_set")
        up_hi, up_lo = [sem(f"up_hi{i}") for i in range(2)], [sem(f"up_lo{i}") for i in range(2)]
        null_dve, null_pool, null_pe = sem("null_dve"), sem("null_pool"), sem("null_pe")

        x_loaded, out_stored = sem("x_loaded"), sem("out_stored")
        dve_met, pool_met = sem("dve_met"), sem("pool_met")
        QKT = [f"qkT{n}" for n in range(8)]
        PROJ = [f"proj{n}" for n in range(8)]
        VS = [f"v{n}" for n in range(4)]
        LN = lambda r: [f"stats{r}", f"aggr{r}", f"var{r}"]
        TOP = lambda r: [f"{n}{r}" for n in ("max", "idx", "idxf")]
        pe_f0 = progress("pe_f0", ["T0", "qk0", "vk0", "ctx", "mix", "out0"])
        act_f0 = progress("act_f0", ["xaT", "xfT", "kexp", "vk", "mix", "topexp", "xfh"])
        pool_f0 = progress("pool_f0", ["rstd0", "rstd1", "xfl"])
        dve_f0 = progress("dve_f0", LN(0) + ["xn0"] + LN(1) + ["msq", "ms", "tin0", "start0", "nkmax", "rksum", "qsT", "ctxT",
                                                               "out0", "rt0"] + TOP(0)
                          + ["gap", "den0", "w1_0", "w2_0", "w1h", "w2h", "one0", "cw0"])
        pe_f1 = progress("pe_f1", ["T1", "logit1"] + PROJ + QKT + VS)
        act_f1 = progress("act_f1", ["xaT1", "xfT1", "rexp0", "rexp1"] + PROJ + QKT + VS + ["xfh1"])
        pool_f1 = progress("pool_f1", ["rstd2", "rstd3", "start1"] + [f"sq{n}" for n in range(8)]
                           + ["rn", "nrm0", "nrm1", "nrm2", "nrm3", "xfl1"])
        dve_f1 = progress("dve_f1", LN(2) + ["xn1"] + LN(3) + ["tin1", "rt1", "nrmax", "rsum", "prob", "group",
                                                               "gmax", "gidx", "gidxf", "gone", "gmask", "masked", "ss0"]
                          + ["max1", "idx1", "ss1", "idxf1", "den1", "rden", "rdenh", "tw1", "ss2"]
                          + [f"ss{n}" for n in range(3, 8)] + ["floor", "one1", "cw1"])
        pe_moe = [progress(f"pe_moe{i}", moe_order(i, ["gu"], ["dn"])) for i in range(2)]
        act_moe = [progress(f"act_moe{i}", moe_order(i, ["th"], [])) for i in range(2)]
        dve_moe = [progress(f"dve_moe{i}", moe_order(i, ["ga", "hid"], ["y"])) for i in range(2)]

        def expert_before(b, layer, e):
            if e:
                return layer, b, e - 1
            return (0, b + 1, E - 1) if layer else (1, b - 2, E - 1)

        def head_order(per_step):
            return [n for p in range(STEPS + 6) for n in per_step(p)]

        def halves_at(p, late):
            return [(p - late) // 4] if p >= late and (p - late) % 4 == 0 and (p - late) // 4 < STEPS // 4 else []

        def pe_head_steps(p):
            out = [f"op{h}" for h in halves_at(p, 9)]
            if p < STEPS:
                out += [f"null{p // HP}"] * (p % HP == 0) + [f"simA{p}", f"simB{p}"]
            out += [f"prT{p - 1}"] * (1 <= p <= STEPS)
            out += [f"pnT{h}" for h in halves_at(p, 5)]
            out += [f"pv{p - 3}"] * (3 <= p < STEPS + 3)
            out += [f"pvn{h}" for h in halves_at(p, 6)]
            return out + [f"oT{h}" for h in halves_at(p, 8)]

        def dve_head_steps(p):
            out = [f"add{h}" for h in halves_at(p, 9)]
            if p < STEPS:
                out += [f"sn{p // HP}", f"nmin{p // HP}"] * (p % HP == 0) + [f"simA{p}", f"simB{p}"]
            out += [n for h in halves_at(p, 4) for n in (f"pnd{h}", f"l1_{h}", f"l2_{h}", f"rl{h}")]
            out += [f"pnT{h}" for h in halves_at(p, 5)]
            return out + [f"o{h}" for h in halves_at(p, 6)]

        def act_head_steps(p):
            out = [f"expA{p}", f"expB{p}"] if p < STEPS else []
            out += [f"pn{h}" for h in halves_at(p, 4)]
            out += [f"prT{p - 1}"] * (1 <= p <= STEPS)
            return out + [f"oT{h}" for h in halves_at(p, 8)]

        pe_heads = progress("pe_heads", head_order(pe_head_steps))
        dve_heads = progress("dve_heads", head_order(dve_head_steps))
        act_heads = progress("act_heads", head_order(act_head_steps))

        ROUND = STEPS + 6
        PIECES = 2 * ROUND

        def in_round(b, heads, experts, front0, front1, m0=True, m1=True, f0=True, f1=True, h=True):
            for p in range(ROUND):
                for piece in (2 * p, 2 * p + 1):
                    if piece == 2 * p and h:
                        heads(b, p)
                    if piece == 2 * p + 1:
                        experts(b, p, m0, m1)
                    if f0:
                        front0(b + 2, piece)
                    if f1:
                        front1(b + 1, piece)

        def all_rounds(engine, parts):
            in_round(-1, *parts, m1=False, h=False)
            with engine.Fori(0, B - 2) as b:
                in_round(b, *parts)
            in_round(B - 2, *parts, f0=False)
            in_round(B - 1, *parts, m0=False, f0=False, f1=False)

        block = ctx.enter_context(nc.Block())

        @block.sync
        def _(sp):
            sp.sem_inc(x_loaded, 16)
            sp.sem_inc(out_stored, 16)

            def load_x(b):
                sp.wait_ge(*dve_f0.at(b - 1, "start0"))
                sp.dma_start(x_in[:], x[b].rearrange("(t p) d -> p t d", p=P)).then_inc(x_loaded, 16)

            def store(b):
                sp.wait_ge(*dve_heads.at(b, f"add{STEPS // 4 - 1}"))
                sp.wait_ge(*dve_moe[1].at(b, f"y{E - 1}"))
                sp.dma_start(out[b].rearrange("(t p) d -> p t d", p=P), acc1[:]).then_inc(out_stored, 16)

            load_x(0)
            sp.dma_start(cst[:], consts).then_inc(const_in, 16)
            sp.dma_start(small[:], w_small).then_inc(small_in, 16)
            sp.dma_start(raw_up[0], w_up0).then_inc(up0_in, 16)
            sp.dma_start(down[0][:].rearrange("p e a c -> p (e a c)"), w_dn0).then_inc(dn0_in, 16)
            sp.dma_start(dist, distance).then_inc(dist_in, 16)
            sp.dma_start(nkw[:].rearrange("p a d -> p (a d)"), null_k).then_inc(null_in, 16)
            sp.dma_start(nvbd[:].rearrange("p a d -> p (a d)"), null_v).then_inc(null_in, 16)
            sp.dma_start(raw_up[1], w_up1).then_inc(up1_in, 16)
            sp.dma_start(qkv1[:], w_qkv1).then_inc(qkv_in, 16)
            sp.dma_start(wout1[:].rearrange("p h c -> p (h c)"), w_out1).then_inc(wout_in, 16)
            sp.dma_start(down[1][:].rearrange("p e a c -> p (e a c)"), w_dn1).then_inc(dn1_in, 16)
            load_x(1)
            with sp.Fori(0, B - 2) as b:
                load_x(b + 2)
                store(b)
            store(B - 2)
            store(B - 1)
            sp.wait_ge(out_stored, 16 * (B + 1))

        @block.gpsimd
        def _(pool):
            for prog in (pool_f0, pool_f1):
                pool.sem_inc(prog.sem, 2 * prog.per)
            nc.gpsimd.memset(halves[:], -0.5).then_inc(half_set, 1)

            def front0(b, k):
                if k == 0:
                    pool.wait_ge(half_set, 1)
                    pool.wait_ge(*dve_f0.at(b, "var0"))
                    nc.gpsimd.tensor_tensor(rstd[0][:, 0:T], var[0][:, 0:T], halves[:, 0:T], ALU.pow)\
                        .then_inc(*pool_f0("rstd0"))
                if k == 1:
                    pool.wait_ge(*dve_f0.at(b, "ms"))
                    nc.gpsimd.tensor_tensor(rstd[1][:], var[1][:], halves[:, 0:2 * T], ALU.pow)\
                        .then_inc(*pool_f0("rstd1"))
                if k == 16:
                    pool.wait_ge(*act_f0.at(b, "xfh"))
                    pool.wait_ge(*pe_moe[0].at(b - 1, f"gu{E - 1}"))
                    nc.gpsimd.tensor_tensor(xf_l[0][:], xfT[:], xf_h[0][:].bitcast(F32), ALU.subtract)\
                        .then_inc(*pool_f0("xfl"))

            def front1(b, k):
                if k in (17, 18):
                    r = k - 15
                    pool.wait_ge(*dve_f1.at(b, f"var{r}"))
                    nc.gpsimd.tensor_tensor(rstd[r][:, 0:T], var[r][:, 0:T], halves[:, 0:T], ALU.pow)\
                        .then_inc(*pool_f1(f"rstd{r}"))
                if k == 22:
                    pool.wait_ge(*dve_moe[0].at(b, f"y{E - 1}"))
                    pool.wait_ge(*dve_moe[1].at(b - 1, "y0"))
                    pool.wait_ge(*dve_heads.at(b - 1, "add0"))
                    pool.sem_inc(pool_met, 1)
                    nc.gpsimd.tensor_copy(start1[:], acc0[:]).then_inc(*pool_f1("start1"))
                if 22 <= k < 30:
                    n = k - 22
                    part = qk[:, n // 4, n // 2 % 2, n % 2 * 512:n % 2 * 512 + 512]
                    pool.wait_ge(*act_f1.at(b, f"proj{n}"))
                    pool.wait_ge(*(dve_f1.at(b, f"ss{n - 1}") if n else dve_f1.at(b - 1, "ss7")))
                    nc.gpsimd.tensor_tensor(sq[:], part, part, ALU.mult).then_inc(*pool_f1(f"sq{n}"))
                if k == 31:
                    pool.wait_ge(*dve_f1.at(b, "floor"))
                    flat = "p w t h -> p (w t h)"
                    nc.gpsimd.tensor_tensor(rn[:].rearrange(flat), ss[:].rearrange(flat), halves[:], ALU.pow)\
                        .then_inc(*pool_f1("rn"))
                    pool.wait_ge(*pool_f1.at(b, "rn"))
                    for n in range(2 * T):
                        t = qk[:, n // T, n % T].rearrange("p (h d) -> p h d", h=H1)
                        nc.gpsimd.tensor_tensor(t, t, rn[:, n // T, n % T].unsqueeze(2).to_broadcast([P, H1, DH1]), ALU.mult)\
                            .then_inc(*pool_f1(f"nrm{n}"))
                if k == PIECES - 1:
                    pool.wait_ge(*act_f1.at(b, "xfh1"))
                    pool.wait_ge(*pe_moe[1].at(b - 1, f"gu{E - 1}"))
                    nc.gpsimd.tensor_tensor(xf_l[1][:], xfT[:], xf_h[1][:].bitcast(F32), ALU.subtract)\
                        .then_inc(*pool_f1("xfl1"))

            for k in range(PIECES):
                front0(0, k)
            pool.wait_ge(dist_in, 16)
            for h, slope in enumerate(slopes()):
                nc.gpsimd.tensor_scalar(bias[:, h], dist, slope, None, ALU.mult).then_inc(bias_set, 1)
            pool.wait_ge(null_dve, 3)
            nc.gpsimd.tensor_tensor(nk_ss[:, 2:4], nk_ss[:, 0:2], halves[0:NULL * H1, 0:2], ALU.pow).then_inc(null_pool, 1)
            pool.wait_ge(up_hi[1], 1)
            nc.gpsimd.tensor_tensor(up_l[1][:].rearrange("p e n -> p (e n)"), raw_up[1],
                                    up_h[1][:].rearrange("p e n -> p (e n)").bitcast(F32), ALU.subtract)\
                .then_inc(up_lo[1], 1)
            nothing = lambda *_: None
            all_rounds(pool, (nothing, nothing, front0, front1))

        @block.scalar
        def _(act):
            for prog in (act_f0, act_f1, *act_moe, act_heads):
                act.sem_inc(prog.sem, 2 * prog.per)

            def front0(b, k):
                if k == 4:
                    act.wait_ge(small_in, 16)
                    act.wait_ge(*pe_f1.at(b - 2, "v3"))
                    act.wait_ge(*pe_f0.at(b, "T0"))
                    nc.scalar.activation(xaT[:], b_front[:, 0:S], ACT.Identity, bias=beta0, scale=gamma0)\
                        .then_inc(*act_f0("xaT"))
                    act.wait_ge(*pool_f1.at(b - 2, "xfl1"))
                    nc.scalar.activation(xfT[:], b_front[:, S:2 * S], ACT.Copy, scale=rms_scale).then_inc(*act_f0("xfT"))
                if k == 5:
                    act.wait_ge(*dve_f0.at(b, "nkmax"))
                    nc.scalar.activation(keT, b_front[:, S:2 * S], ACT.Exp, bias=nkmax[:], accum_out=ksum[:, 0:1])\
                        .then_inc(*act_f0("kexp"))
                if k == 6:
                    act.wait_ge(*pe_f0.at(b, "vk0"))
                    nc.scalar.activation(vk[:].rearrange("p a t d -> p (a t d)"), b_front[:], ACT.Copy).then_inc(*act_f0("vk"))
                if k == 8:
                    act.wait_ge(*pe_f0.at(b, "mix"))
                    nc.scalar.activation(mix[:], b_front[:, 0:D], ACT.Copy).then_inc(*act_f0("mix"))
                if k == 10:
                    act.wait_ge(*dve_f0.at(b, "gap"))
                    nc.scalar.activation(tw[0][:, 1], tw[0][:, 0], ACT.Exp).then_inc(*act_f0("topexp"))
                if k == 16:
                    act.wait_ge(*pe_moe[0].at(b - 1, f"gu{E - 1}"))
                    act.wait_ge(*act_f0.at(b, "xfT"))
                    nc.scalar.activation(xf_h[0][:], xfT[:], ACT.Copy).then_inc(*act_f0("xfh"))

            def front1(b, k):
                if k == 20:
                    act.wait_ge(*pe_f0.at(b + 1, "out0"))
                    act.wait_ge(*pool_f0.at(b + 1, "xfl"))
                    act.wait_ge(*pe_f1.at(b, "T1"))
                    nc.scalar.activation(xaT[:], b_front[:, 0:S], ACT.Copy, scale=gamma1).then_inc(*act_f1("xaT1"))
                    nc.scalar.activation(xfT[:], b_front[:, S:2 * S], ACT.Copy).then_inc(*act_f1("xfT1"))
                if k == 21:
                    act.wait_ge(*dve_f1.at(b, "nrmax"))
                    for t in range(T):
                        nc.scalar.activation(prob[:, t], rt[1][:, t], ACT.Exp, bias=tw[1][:, 0, t:t + 1],
                                             accum_out=tw[1][:, 1, t:t + 1]).then_inc(*act_f1(f"rexp{t}"))
                if 22 <= k < 30:
                    n = k - 22
                    act.wait_ge(*pe_f1.at(b, f"proj{n}"))
                    if n == 0:
                        act.wait_ge(*pe_f1.at(b - 1, "qkT7"))
                    nc.scalar.activation(qk[:, n // 4, n // 2 % 2, n % 2 * 512:n % 2 * 512 + 512], b_front[:], ACT.Copy)\
                        .then_inc(*act_f1(f"proj{n}"))
                if 32 <= k < 40:
                    n = k - 32
                    w, t, g = n // 4, n // 2 % 2, n % 2
                    act.wait_ge(*pe_f1.at(b, f"qkT{n}"))
                    if n == 0:
                        act.wait_ge(qscale_set, 2)
                        act.wait_ge(*pe_heads.at(b - 1, f"simB{STEPS - 1}"))
                    nc.scalar.activation(qkT[:, w, 4 * g:4 * g + 4, t * P:(t + 1) * P],
                                         turn_banks[n % 3][:].rearrange("p (h q) -> p h q", h=4), ACT.Copy,
                                         **({} if w else {"scale": qscale[:]})).then_inc(*act_f1(f"qkT{n}"))
                if 40 <= k < 44:
                    n = k - 40
                    act.wait_ge(*pe_f1.at(b, f"v{n}"))
                    if n == 0:
                        act.wait_ge(*pe_heads.at(b - 1, f"pv{STEPS - 1}"))
                    nc.scalar.activation(v[:, n // 2, n % 2 * 512:n % 2 * 512 + 512], turn_banks[(8 + n) % 3][:], ACT.Copy)\
                        .then_inc(*act_f1(f"v{n}"))
                if k == PIECES - 1:
                    act.wait_ge(*act_f1.at(b, "xfT1"))
                    act.wait_ge(*pe_moe[1].at(b - 1, f"gu{E - 1}"))
                    nc.scalar.activation(xf_h[1][:], xfT[:], ACT.Copy).then_inc(*act_f1("xfh1"))

            def experts(b, p, m0, m1):
                for layer, e in experts_at(p, m0, m1):
                    act.wait_ge(*pe_moe[layer].at(b + 1 - layer, f"gu{e}"))
                    nc.scalar.activation(th[e % 2][:], b_gate[:], ACT.Tanh, scale=0.5).then_inc(*act_moe[layer](f"th{e}"))

            def heads(b, p):
                qt = p // HP
                n = P * (qt + 1)
                if p < STEPS:
                    for i, ab in enumerate("AB"):
                        h = 2 * (p % HP) + i
                        act.wait_ge(*dve_heads.at(b, f"sim{ab}{p}"))
                        nc.scalar.activation(prb[p % 2][:, i, 0:n], prb[p % 2][:, i, 0:n], ACT.Exp, scale=-1.0,
                                             bias=mneg[:, qt, h:h + 1], accum_out=lsum[:, qt, h:h + 1])\
                            .then_inc(*act_heads(f"exp{ab}{p}"))
                for half in halves_at(p, 4):
                    act.wait_ge(*dve_heads.at(b, f"pnd{half}"))
                    nc.scalar.activation(pn[:], pnd[:], ACT.Exp).then_inc(*act_heads(f"pn{half}"))
                if 1 <= p <= STEPS:
                    p1 = p - 1
                    n1 = P * (p1 // HP + 1)
                    act.wait_ge(*pe_heads.at(b, f"prT{p1}"))
                    if p1 >= 3:
                        act.wait_ge(*pe_heads.at(b, f"pv{p1 - 3}"))
                    nc.scalar.activation(prT[p1 % 3][:, :, 0:n1], b_prT[:, 0:2 * n1].rearrange("p (a n) -> p a n", a=2),
                                         ACT.Copy).then_inc(*act_heads(f"prT{p1}"))
                for half in halves_at(p, 8):
                    act.wait_ge(*pe_heads.at(b, f"oT{half}"))
                    nc.scalar.activation(oT[:].rearrange("p a q -> p (a q)"), b_prT[:], ACT.Copy)\
                        .then_inc(*act_heads(f"oT{half}"))

            for k in range(6):
                front0(0, k)
            act.wait_ge(up0_in, 16)
            nc.scalar.activation(up_h[0][:].rearrange("p e n -> p (e n)"), raw_up[0], ACT.Copy).then_inc(up_hi[0], 1)
            for k in range(6, PIECES):
                front0(0, k)
            act.wait_ge(up1_in, 16)
            nc.scalar.activation(up_h[1][:].rearrange("p e n -> p (e n)"), raw_up[1], ACT.Copy).then_inc(up_hi[1], 1)
            act.wait_ge(up_lo[0], 1)
            act.wait_ge(up_lo[1], 1)
            all_rounds(act, (heads, experts, front0, front1))

        @block.vector
        def _(dve):
            for prog in (dve_f0, dve_f1, *dve_moe, dve_heads):
                dve.sem_inc(prog.sem, 2 * prog.per)
            nc.vector.memset(gpad[:], -1.0).then_inc(pad_set, 1)

            def layer_norm_stats(b, f, r, src, eps=LN_EPS):
                for t in range(T):
                    ins = nc.vector.bn_stats(stats[r][:, t], src[:, t])
                ins.then_inc(*f(f"stats{r}"))
                dve.wait_ge(*f.at(b, f"stats{r}"))
                dve.sem_inc(dve_met, 1)
                for t in range(T):
                    ins = nc.vector.bn_aggr(mv[r][:, t], stats[r][:, t])
                ins.then_inc(*f(f"aggr{r}"))
                dve.wait_ge(*f.at(b, f"aggr{r}"))
                nc.vector.tensor_scalar(var[r][:, 0:T], mv[r][:, :, 1], eps, None, ALU.add).then_inc(*f(f"var{r}"))

            def normalise(dst, src, r):
                for t in range(T):
                    ins = nc.vector.tensor_scalar(dst[:, t], src[:, t], mv[r][:, t, 0:1], rstd[r][:, t:t + 1],
                                                  ALU.subtract, ALU.mult)
                return ins

            def top2_max(b, f, i, src):
                for t in range(T):
                    ins = nc.vector.max(top[i][:, t], src[:, t])
                ins.then_inc(*f(f"max{i}"))
                dve.wait_ge(*f.at(b, f"max{i}"))
                dve.sem_inc(dve_met, 1)
                for t in range(T):
                    ins = nc.vector.max_index(topi[i][:, t], top[i][:, t], src[:, t])
                ins.then_inc(*f(f"idx{i}"))

            def top2_float(b, f, i):
                dve.wait_ge(*f.at(b, f"idx{i}"))
                nc.vector.tensor_copy(topf[i][:], topi[i][:, :, 0:2]).then_inc(*f(f"idxf{i}"))

            def combine(b, f, i, w):
                for k in range(2):
                    for t in range(T):
                        ins = nc.vector.tensor_scalar(one[i][:, k, t], iota8, topf[i][:, t, k:k + 1], w(k, t),
                                                      ALU.is_equal, ALU.mult)
                ins.then_inc(*f(f"one{i}"))
                dve.wait_ge(*f.at(b, f"one{i}"))
                nc.vector.tensor_tensor(cw[i][:], one[i][:, 0], one[i][:, 1], ALU.add).then_inc(*f(f"cw{i}"))

            def front0(b, k):
                if k == 0:
                    dve.wait_ge(x_loaded, b * 16 + 32)
                    layer_norm_stats(b, dve_f0, 0, x_in)
                if k == 1:
                    dve.wait_ge(*pool_f0.at(b, "rstd0"))
                    normalise(xn, x_in, 0).then_inc(*dve_f0("xn0"))
                    dve.wait_ge(*dve_f0.at(b, "xn0"))
                    layer_norm_stats(b, dve_f0, 1, xn)
                    nc.vector.tensor_tensor(var[1][:, T:2 * T], mv[1][:, :, 0], mv[1][:, :, 0], ALU.mult)\
                        .then_inc(*dve_f0("msq"))
                    dve.wait_ge(*dve_f0.at(b, "msq"))
                    nc.vector.scalar_tensor_tensor(out=var[1][:, T:2 * T], in0=var[1][:, T:2 * T], scalar=RMS_EPS,
                                                   in1=mv[1][:, :, 1], op0=ALU.add, op1=ALU.add).then_inc(*dve_f0("ms"))
                if k == 3:
                    dve.wait_ge(*pool_f0.at(b, "rstd1"))
                    dve.wait_ge(*pe_f1.at(b - 2, "T1"))
                    normalise(tin, xn, 1)
                    for t in range(T):
                        ins = nc.vector.tensor_scalar(tin[:, T + t], xn[:, t], rstd[1][:, T + t:T + t + 1], None, ALU.mult)
                    ins.then_inc(*dve_f0("tin0"))
                    dve.wait_ge(*dve_moe[0].at(b - 1, "y0"))
                    nc.vector.scalar_tensor_tensor(out=start0[:], in0=xn[:], scalar=2.0, in1=x_in[:], op0=ALU.mult, op1=ALU.add)\
                        .then_inc(*dve_f0("start0"))
                if k == 5:
                    dve.wait_ge(*pe_f0.at(b, "qk0"))
                    nc.vector.tensor_reduce(nkmax[:], b_front[:, S:2 * S], AX.X, ALU.max, negate=True)\
                        .then_inc(*dve_f0("nkmax"))
                if k == 6:
                    dve.wait_ge(*act_f0.at(b, "kexp"))
                    nc.vector.reciprocal(ksum[:, 1:2], ksum[:, 0:1]).then_inc(*dve_f0("rksum"))
                    dve.wait_ge(*dve_f0.at(b, "rksum"))
                    nc.vector.tensor_scalar(qsT[:], b_front[:, 0:S], ksum[:, 1:2], float(DH0) ** -0.5, ALU.mult, ALU.mult)\
                        .then_inc(*dve_f0("qsT"))
                if k == 7:
                    dve.wait_ge(const_in, 16)
                    dve.wait_ge(*pe_f0.at(b, "ctx"))
                    nc.vector.tensor_tensor(ctxT[:], b_front[:, 0:P], head_mask, ALU.mult).then_inc(*dve_f0("ctxT"))
                if k == 10:
                    dve.wait_ge(*dve_f0.at(b, "start0"))
                    dve.wait_ge(*pe_f0.at(b, "out0"))
                    nc.vector.tensor_tensor(start0[:].rearrange("p t d -> p (t d)"), b_front[:, 0:S],
                                            start0[:].rearrange("p t d -> p (t d)"), ALU.add).then_inc(*dve_f0("out0"))
                    nc.vector.tensor_copy(rt[0][:].rearrange("p t e -> p (t e)"), b_front[:, S:S + T * E])\
                        .then_inc(*dve_f0("rt0"))
                    dve.wait_ge(*dve_f0.at(b, "rt0"))
                    dve.sem_inc(dve_met, 1)
                    top2_max(b, dve_f0, 0, rt[0])
                    top2_float(b, dve_f0, 0)
                    nc.vector.tensor_tensor(tw[0][:, 0], top[0][:, :, 1], top[0][:, :, 0], ALU.subtract)\
                        .then_inc(*dve_f0("gap"))
                if k == 11:
                    dve.wait_ge(*act_f0.at(b, "topexp"))
                    nc.vector.tensor_scalar(tw[0][:, 2], tw[0][:, 1], 1.0, None, ALU.add).then_inc(*dve_f0("den0"))
                    dve.wait_ge(*dve_f0.at(b, "den0"))
                    nc.vector.reciprocal(tw[0][:, 3], tw[0][:, 2]).then_inc(*dve_f0("w1_0"))
                    dve.wait_ge(*dve_f0.at(b, "w1_0"))
                    nc.vector.tensor_tensor(tw[0][:, 4], tw[0][:, 3], tw[0][:, 1], ALU.mult).then_inc(*dve_f0("w2_0"))
                    nc.vector.tensor_scalar(tw[0][:, 5], tw[0][:, 3], 0.5, None, ALU.mult).then_inc(*dve_f0("w1h"))
                    dve.wait_ge(*dve_f0.at(b, "w2_0"))
                    nc.vector.tensor_scalar(tw[0][:, 6], tw[0][:, 4], 0.5, None, ALU.mult).then_inc(*dve_f0("w2h"))
                if k == 17:
                    dve.wait_ge(*dve_f0.at(b, "w2h"))
                    dve.wait_ge(*dve_moe[0].at(b - 1, f"y{E - 1}"))
                    combine(b, dve_f0, 0, lambda k, t: tw[0][:, 5 + k, t:t + 1])

            def front1(b, k):
                if k == 17:
                    dve.wait_ge(*dve_moe[0].at(b, f"y{E - 1}"))
                    layer_norm_stats(b, dve_f1, 2, acc0)
                if k == 18:
                    dve.wait_ge(*pool_f1.at(b, "rstd2"))
                    dve.wait_ge(*pe_f0.at(b + 1, "T0"))
                    normalise(tin[:, T:2 * T], acc0, 2).then_inc(*dve_f1("xn1"))
                    dve.wait_ge(*dve_f1.at(b, "xn1"))
                    layer_norm_stats(b, dve_f1, 3, tin[:, T:2 * T])
                if k == 19:
                    dve.wait_ge(*pool_f1.at(b, "rstd3"))
                    normalise(tin, tin[:, T:2 * T], 3).then_inc(*dve_f1("tin1"))
                if k == 21:
                    dve.wait_ge(*pe_f1.at(b, "logit1"))
                    nc.vector.tensor_copy(rt[1][:].rearrange("p t e -> p (t e)"), b_front[:, 0:T * E]).then_inc(*dve_f1("rt1"))
                    dve.wait_ge(*dve_f1.at(b, "rt1"))
                    nc.vector.tensor_reduce(tw[1][:, 0], rt[1][:], AX.X, ALU.max, negate=True).then_inc(*dve_f1("nrmax"))
                if k == 22:
                    dve.wait_ge(*act_f1.at(b, "rexp1"))
                    nc.vector.reciprocal(tw[1][:, 2], tw[1][:, 1]).then_inc(*dve_f1("rsum"))
                    dve.wait_ge(*dve_f1.at(b, "rsum"))
                    for t in range(T):
                        ins = nc.vector.tensor_scalar(prob[:, t], prob[:, t], tw[1][:, 2, t:t + 1], None, ALU.mult)
                    ins.then_inc(*dve_f1("prob"))
                    dve.wait_ge(*dve_f1.at(b, "prob"))
                    dve.wait_ge(pad_set, 1)
                    nc.vector.tensor_reduce(gpad[:, :, 0:GROUPS], prob[:].rearrange("p t (g e) -> p t g e", g=GROUPS), AX.X, ALU.max)\
                        .then_inc(*dve_f1("group"))
                if k == 23:
                    dve.wait_ge(*dve_f1.at(b, "group"))
                    dve.sem_inc(dve_met, 1)
                    for t in range(T):
                        ins = nc.vector.max(gtop[:, t], gpad[:, t])
                    ins.then_inc(*dve_f1("gmax"))
                    dve.wait_ge(*dve_f1.at(b, "gmax"))
                    dve.sem_inc(dve_met, 1)
                    for t in range(T):
                        ins = nc.vector.max_index(gidx[:, t], gtop[:, t], gpad[:, t])
                    ins.then_inc(*dve_f1("gidx"))
                    dve.wait_ge(*dve_f1.at(b, "gidx"))
                    nc.vector.tensor_copy(gidxf[:], gidx[:, :, 0:2]).then_inc(*dve_f1("gidxf"))
                if k == 24:
                    dve.wait_ge(*dve_f1.at(b, "gidxf"))
                    for c in range(2):
                        for t in range(T):
                            ins = nc.vector.tensor_scalar(gmask[:, t, c], iota8[:, 0:GROUPS], gidxf[:, t, c:c + 1], None, ALU.is_equal)
                    ins.then_inc(*dve_f1("gone"))
                    dve.wait_ge(*dve_f1.at(b, "gone"))
                    nc.vector.tensor_tensor(gmask[:, :, 0], gmask[:, :, 0], gmask[:, :, 1], ALU.add).then_inc(*dve_f1("gmask"))
                    dve.wait_ge(*dve_f1.at(b, "gmask"))
                    for t in range(T):
                        ins = nc.vector.tensor_tensor(masked[:, t].rearrange("p (g e) -> p g e", g=GROUPS),
                                                      prob[:, t].rearrange("p (g e) -> p g e", g=GROUPS),
                                                      gmask[:, t, 0].unsqueeze(2).to_broadcast([P, GROUPS, E // GROUPS]), ALU.mult)
                    ins.then_inc(*dve_f1("masked"))
                if k == 25:
                    dve.wait_ge(*dve_f1.at(b, "masked"))
                    dve.sem_inc(dve_met, 1)
                    top2_max(b, dve_f1, 1, masked)
                if k == 26:
                    top2_float(b, dve_f1, 1)
                    nc.vector.tensor_tensor(tw[1][:, 3], top[1][:, :, 0], top[1][:, :, 1], ALU.add).then_inc(*dve_f1("den1"))
                    dve.wait_ge(*dve_f1.at(b, "den1"))
                    nc.vector.reciprocal(tw[1][:, 4], tw[1][:, 3]).then_inc(*dve_f1("rden"))
                    dve.wait_ge(*dve_f1.at(b, "rden"))
                    nc.vector.tensor_scalar(tw[1][:, 5], tw[1][:, 4], 0.5, None, ALU.mult).then_inc(*dve_f1("rdenh"))
                    dve.wait_ge(*dve_f1.at(b, "rdenh"))
                    for c in range(2):
                        ins = nc.vector.tensor_tensor(tw[1][:, 6 + c], top[1][:, :, c], tw[1][:, 5], ALU.mult)
                    ins.then_inc(*dve_f1("tw1"))
                if 24 <= k < 32:
                    n = k - 24
                    dve.wait_ge(*pool_f1.at(b, f"sq{n}"))
                    nc.vector.tensor_reduce(ss[:, n // 4, n // 2 % 2, n % 2 * 8:n % 2 * 8 + 8],
                                            sq[:].rearrange("p (h d) -> p h d", h=8), AX.X, ALU.add).then_inc(*dve_f1(f"ss{n}"))
                if k == 31:
                    dve.wait_ge(*dve_f1.at(b, "ss7"))
                    nc.vector.tensor_scalar(ss[:], ss[:], 1e-24, None, ALU.max).then_inc(*dve_f1("floor"))
                if k == PIECES - 1:
                    dve.wait_ge(*dve_f1.at(b, "tw1"))
                    dve.wait_ge(*dve_moe[1].at(b - 1, f"y{E - 1}"))
                    combine(b, dve_f1, 1, lambda k, t: tw[1][:, 6 + k, t:t + 1])

            def expert(b, layer, e):
                f = dve_moe[layer]
                dve.wait_ge(*act_moe[layer].at(b, f"th{e}"))
                nc.vector.scalar_tensor_tensor(out=th[e % 2][:], in0=th[e % 2][:], scalar=1.0, in1=b_gate[:],
                                               op0=ALU.add, op1=ALU.mult).then_inc(*f(f"ga{e}"))
                dve.wait_ge(*f.at(b, f"ga{e}"))
                nc.vector.tensor_tensor(hid[e % 2][:].rearrange("p a s -> p (a s)"), b_up[:], th[e % 2][:], ALU.mult)\
                    .then_inc(*f(f"hid{e}"))

            def expert_out(b, layer, e, m0):
                f, acc, start = dve_moe[layer], (acc0, acc1)[layer], (start0, start1)[layer]
                dve.wait_ge(*pe_moe[layer].at(b, f"dn{e}"))
                if e == 0 and layer == 0:
                    dve.wait_ge(*dve_f0.at(b, "cw0"))
                    dve.wait_ge(*pool_f1.at(b - 1, "start1"))
                if e == 0 and layer == 1:
                    dve.wait_ge(*dve_f1.at(b, "cw1"))
                    dve.wait_ge(*pool_f1.at(b, "start1"))
                    dve.wait_ge(out_stored, b * 16 + 16)
                for t in range(T):
                    begin = e == 0 and not (layer and m0 and t == 0)
                    ins = nc.vector.scalar_tensor_tensor(out=acc[:, t], in0=b_y[:, t * D:(t + 1) * D],
                                                         scalar=cw[layer][:, t, e:e + 1], in1=(start if begin else acc)[:, t],
                                                         op0=ALU.mult, op1=ALU.add)
                ins.then_inc(*f(f"y{e}"))
                dve.wait_ge(*f.at(b, f"y{e}"))

            def experts(b, p, m0, m1):
                for layer, e in experts_at(p, m0, m1):
                    expert(b + 1 - layer, layer, e)
                for layer, e in experts_at(p - 1, m0, m1):
                    expert_out(b + 1 - layer, layer, e, m0)

            def heads(b, p):
                qt = p // HP
                n = P * (qt + 1)
                for half in halves_at(p, 9):
                    dve.wait_ge(*pe_heads.at(b, f"op{half}"))
                    begin = half == 0 and not (isinstance(b, int) and b == B - 1)
                    if begin:
                        dve.wait_ge(*pool_f1.at(b, "start1"))
                        dve.wait_ge(out_stored, b * 16 + 16)
                    nc.vector.tensor_tensor(acc1[:, half // 2], b_prT[:, 0:D], (start1 if begin else acc1)[:, half // 2], ALU.add)\
                        .then_inc(*dve_heads(f"add{half}"))
                    dve.wait_ge(*dve_heads.at(b, f"add{half}"))
                if p < STEPS:
                    if p % HP == 0:
                        dve.wait_ge(*pe_heads.at(b, f"null{qt}"))
                        nc.vector.tensor_tensor(sn[:, qt].rearrange("p h j -> p (h j)"), b_sim[0][:, 0:NULL * H1], null_bias[:, qt],
                                                ALU.add).then_inc(*dve_heads(f"sn{qt}"))
                        dve.wait_ge(*dve_heads.at(b, f"sn{qt}"))
                        nc.vector.tensor_tensor(nmin[:, qt], sn[:, qt, :, 0], sn[:, qt, :, 1], ALU.min)\
                            .then_inc(*dve_heads(f"nmin{qt}"))
                        dve.wait_ge(*dve_heads.at(b, f"nmin{qt}"))
                    for i, ab in enumerate("AB"):
                        h = 2 * (p % HP) + i
                        if p >= 2:
                            dve.wait_ge(*pe_heads.at(b, f"prT{p - 2}"))
                        dve.wait_ge(*pe_heads.at(b, f"sim{ab}{p}"))
                        dve.sem_inc(dve_met, 1)
                        nc.vector.tensor_tensor_reduce(prb[p % 2][:, i, 0:n], b_sim[i][:, 0:n],
                                                       bias[:, h, S - n:S], 1.0, nmin[:, qt, h:h + 1],
                                                       ALU.add, ALU.min, mneg[:, qt, h:h + 1])\
                            .then_inc(*dve_heads(f"sim{ab}{p}"))
                for half in halves_at(p, 4):
                    q, h0 = half // 2, half % 2 * HALF
                    dve.wait_ge(*dve_heads.at(b, f"simB{4 * half + 3}"))
                    nc.vector.tensor_tensor(pnd[:], mneg[:, q, h0:h0 + HALF].unsqueeze(2).to_broadcast([P, HALF, NULL]),
                                            sn[:, q, h0:h0 + HALF], ALU.subtract).then_inc(*dve_heads(f"pnd{half}"))
                    dve.wait_ge(*act_heads.at(b, f"pn{half}"))
                    nc.vector.tensor_tensor(rl[:, q, h0:h0 + HALF], pn[:, :, 0], pn[:, :, 1], ALU.add)\
                        .then_inc(*dve_heads(f"l1_{half}"))
                    dve.wait_ge(*dve_heads.at(b, f"l1_{half}"))
                    nc.vector.tensor_tensor(rl[:, q, h0:h0 + HALF], rl[:, q, h0:h0 + HALF], lsum[:, q, h0:h0 + HALF], ALU.add)\
                        .then_inc(*dve_heads(f"l2_{half}"))
                    dve.wait_ge(*dve_heads.at(b, f"l2_{half}"))
                    nc.vector.reciprocal(rl[:, q, h0:h0 + HALF], rl[:, q, h0:h0 + HALF]).then_inc(*dve_heads(f"rl{half}"))
                for half in halves_at(p, 5):
                    dve.wait_ge(*pe_heads.at(b, f"pnT{half}"))
                    nc.vector.tensor_copy(pnT[:], b_prT[0:NULL * HALF, 0:P]).then_inc(*dve_heads(f"pnT{half}"))
                for half in halves_at(p, 6):
                    q, h0 = half // 2, half % 2 * HALF
                    dve.wait_ge(*dve_heads.at(b, f"rl{half}"))
                    dve.wait_ge(*pe_heads.at(b, f"pvn{half}"))
                    nc.vector.tensor_tensor(o[:].rearrange("p (h d) -> p h d", h=HALF),
                                            b_pv[:].rearrange("p (h d) -> p h d", h=HALF),
                                            rl[:, q, h0:h0 + HALF].unsqueeze(2).to_broadcast([P, HALF, DH1]), ALU.mult)\
                        .then_inc(*dve_heads(f"o{half}"))

            for k in range(PIECES):
                front0(0, k)
            dve.wait_ge(up_hi[0], 1)
            nc.vector.tensor_tensor(up_l[0][:].rearrange("p e n -> p (e n)"), raw_up[0],
                                    up_h[0][:].rearrange("p e n -> p (e n)").bitcast(F32), ALU.subtract).then_inc(up_lo[0], 1)
            dve.wait_ge(small_in, 16)
            nc.vector.tensor_tensor(qscale[:], qs2, ks2, ALU.mult).then_inc(qscale_set, 1)
            dve.wait_ge(qscale_set, 1)
            nc.vector.tensor_scalar(qscale[:], qscale[:], -SIM_SCALE, None, ALU.mult).then_inc(qscale_set, 1)
            dve.wait_ge(null_in, 32)
            nc.vector.tensor_tensor(nk_sq[:], nkw[:], nkw[:], ALU.mult).then_inc(null_dve, 1)
            dve.wait_ge(null_dve, 1)
            nc.vector.tensor_reduce(nk_ss[:, 0:2], nk_sq[:], AX.X, ALU.add).then_inc(null_dve, 1)
            dve.wait_ge(null_dve, 2)
            nc.vector.tensor_scalar(nk_ss[:, 0:2], nk_ss[:, 0:2], 1e-24, None, ALU.max).then_inc(null_dve, 1)
            dve.wait_ge(null_pool, 1)
            nc.vector.tensor_scalar(nkw[:], nkw[:], nk_ss[:, 2:3], None, ALU.mult).then_inc(null_dve, 1)
            nc.vector.memset(nkbd[:], 0.0).then_inc(null_dve, 1)
            dve.wait_ge(null_dve, 5)
            dve.wait_ge(null_pe, 1)
            turned = b_pv[:, 0:NULL * H1].rearrange("p (h i j) -> p h i j", i=2, j=NULL)
            nc.vector.tensor_copy(nkbd[0:DH1, :, 0:NULL], turned[0:DH1, :, 0]).then_inc(null_dve, 1)
            nc.vector.tensor_copy(nkbd[DH1:P, :, NULL:2 * NULL], turned[DH1:P, :, 1]).then_inc(null_dve, 1)
            dve.wait_ge(bias_set, H1)

            all_rounds(dve, (heads, experts, front0, front1))

        @block.tensor
        def _(pe):
            for prog in (pe_f0, pe_f1, *pe_moe, pe_heads):
                pe.sem_inc(prog.sem, 2 * prog.per)

            def matmul3(ps, w_h, w_l, x_h, x_l, start=True):
                nc.tensor.matmul(ps, w_h, x_h, start=start, stop=False, skip_group_check=True)
                nc.tensor.matmul(ps, w_h, x_l, start=False, stop=False, skip_group_check=True)
                return nc.tensor.matmul(ps, w_l, x_h, start=False, stop=True, skip_group_check=True)

            def turn_inputs(b, f, r):
                pe.wait_ge(const_in, 16)
                pe.wait_ge(*f.at(b, f"tin{r}"))
                for i in range(2 * T):
                    ins = nc.tensor.transpose(b_front[:, i * P:(i + 1) * P], tin[:, i], ident)
                return ins

            def front0(b, k):
                if k == 4:
                    pe.wait_ge(*act_f1.at(b - 2, "v3"))
                    turn_inputs(b, dve_f0, 0).then_inc(*pe_f0("T0"))
                if k == 5:
                    pe.wait_ge(small_in, 16)
                    pe.wait_ge(*act_f0.at(b, "xfT"))
                    nc.tensor.matmul(b_front[:, 0:S], wq0, xaT[:], start=True, stop=True)
                    nc.tensor.matmul(b_front[:, S:2 * S], wk0, xaT[:], start=True, stop=True).then_inc(*pe_f0("qk0"))
                if k == 6:
                    pe.wait_ge(*dve_f0.at(b, "qsT"))
                    for t in range(T):
                        nc.tensor.matmul(b_front[:, t * P:(t + 1) * P], xaT[:, t * P:(t + 1) * P], wv0, start=True, stop=True)
                    for t in range(T):
                        ins = nc.tensor.transpose(b_front[:, S + t * P:S + (t + 1) * P], keT[:, t * P:(t + 1) * P], ident)
                    ins.then_inc(*pe_f0("vk0"))
                if k == 7:
                    pe.wait_ge(*act_f0.at(b, "vk"))
                    for t in range(T):
                        ins = nc.tensor.matmul(b_front[:, 0:P], vk[:, 0, t], vk[:, 1, t], start=(t == 0), stop=(t == T - 1))
                    ins.then_inc(*pe_f0("ctx"))
                if k == 8:
                    pe.wait_ge(*dve_f0.at(b, "ctxT"))
                    nc.tensor.matmul(b_front[:, 0:D], ctxT[:], wout0, start=True, stop=True).then_inc(*pe_f0("mix"))
                if k == 9:
                    pe.wait_ge(*act_f0.at(b, "mix"))
                    for t in range(T):
                        nc.tensor.matmul(b_front[:, t * D:(t + 1) * D], qsT[:, t * P:(t + 1) * P], mix[:], start=True, stop=False)
                        nc.tensor.matmul(b_front[:, t * D:(t + 1) * D], ones_row, b_out, start=False, stop=True)
                    for t in range(T):
                        ins = nc.tensor.matmul(b_front[:, S + t * E:S + (t + 1) * E], xfT[:, t * P:(t + 1) * P], router0,
                                               start=True, stop=True)
                    ins.then_inc(*pe_f0("out0"))

            def project(ps, t, c):
                tok = slice(t * P, (t + 1) * P)
                return nc.tensor.matmul(ps[:], xaT[:, tok], qkv1[:, c:c + 512], start=True, stop=True)

            def turn_bank_free(b, m):
                if m >= 3:
                    pe.wait_ge(*act_f1.at(b, f"qkT{m - 3}" if m < 11 else "v0"))
                else:
                    pe.wait_ge(*(dve_heads.at(b - 1, f"sim{'AB'[m - 1]}{STEPS - 1}") if m else act_f1.at(b, "proj7")))

            def front1(b, k):
                if k == 20:
                    pe.wait_ge(*dve_f0.at(b + 1, "rt0"))
                    turn_inputs(b, dve_f1, 1).then_inc(*pe_f1("T1"))
                if k == 21:
                    pe.wait_ge(*act_f1.at(b, "xfT1"))
                    for t in range(T):
                        ins = nc.tensor.matmul(b_front[:, t * E:(t + 1) * E], xfT[:, t * P:(t + 1) * P], router1, start=True, stop=True)
                    ins.then_inc(*pe_f1("logit1"))
                if 22 <= k < 30:
                    n = k - 22
                    pe.wait_ge(*(act_f1.at(b, f"proj{n - 1}") if n else dve_f1.at(b, "rt1")))
                    if n == 0:
                        pe.wait_ge(qkv_in, 16)
                    project(b_front, n // 2 % 2, n // 4 * HD1 + n % 2 * 512).then_inc(*pe_f1(f"proj{n}"))
                if 32 <= k < 40:
                    n = k - 32
                    w, t, g = n // 4, n // 2 % 2, n % 2
                    turn_bank_free(b, n)
                    pe.wait_ge(*pool_f1.at(b, f"nrm{n // 2}"))
                    for i in range(4):
                        hp = 4 * g + i
                        ins = nc.tensor.transpose(turn_banks[n % 3][:, i * P:(i + 1) * P], qk[:, w, t, hp * P:(hp + 1) * P], ident)
                    ins.then_inc(*pe_f1(f"qkT{n}"))
                if 40 <= k < 44:
                    n = k - 40
                    turn_bank_free(b, 8 + n)
                    project(turn_banks[(8 + n) % 3], n // 2, 2 * HD1 + n % 2 * 512).then_inc(*pe_f1(f"v{n}"))

            def expert_up(b, layer, e):
                l1, b1, e1 = expert_before(b, layer, e)
                pe.wait_ge(*dve_moe[l1].at(b1, f"hid{e1}"))
                if e == 0:
                    pe.wait_ge(up_lo[layer], 1)
                    pe.wait_ge(*(pool_f1.at(b, "xfl1") if layer else pool_f0.at(b, "xfl")))
                for ps, c in ((b_gate, 0 if layer else HID), (b_up, HID if layer else 0)):
                    for a in range(HB):
                        cs = slice(c + a * P, c + (a + 1) * P)
                        ins = matmul3(ps[:, a * S:(a + 1) * S], up_h[layer][:, e, cs], up_l[layer][:, e, cs],
                                      xf_h[layer][:], xf_l[layer][:])
                ins.then_inc(*pe_moe[layer](f"gu{e}"))

            def expert_down(b, layer, e):
                if e == 0:
                    pe.wait_ge((dn0_in, dn1_in)[layer], 16)
                l1, b1, e1 = expert_before(b, layer, e)
                pe.wait_ge(*dve_moe[l1].at(b1, f"y{e1}"))
                pe.wait_ge(*dve_moe[layer].at(b, f"hid{e}"))
                for t in range(T):
                    for a in range(HB):
                        ins = nc.tensor.matmul(b_y[:, t * D:(t + 1) * D], hid[e % 2][:, a, t * P:(t + 1) * P], down[layer][:, e, a],
                                               start=(a == 0), stop=(a == HB - 1), skip_group_check=True)
                ins.then_inc(*pe_moe[layer](f"dn{e}"))

            def experts(b, p, m0, m1):
                for layer, e in experts_at(p, m0, m1):
                    expert_up(b + 1 - layer, layer, e)
                for layer, e in experts_at(p - 1, m0, m1):
                    expert_down(b + 1 - layer, layer, e)

            def heads(b, p):
                qt = p // HP
                toks = slice(qt * P, (qt + 1) * P)
                for half in halves_at(p, 9):
                    pe.wait_ge(wout_in, 16)
                    pe.wait_ge(*act_heads.at(b, f"oT{half}"))
                    for i in range(4):
                        ins = nc.tensor.matmul(b_prT[:, 0:D], oT[:, i], wout1[:, half % 2 * 4 + i], start=(i == 0), stop=(i == 3))
                    ins.then_inc(*pe_heads(f"op{half}"))
                if p < STEPS:
                    hp = p % HP
                    if p % HP == 0:
                        if qt:
                            pe.wait_ge(*dve_heads.at(b, f"simA{p - 1}"))
                        else:
                            pe.wait_ge(*dve_heads.at(b - 1, f"simA{STEPS - 1}"))
                            pe.wait_ge(*act_f1.at(b, "v3"))
                        for i in range(HP):
                            ins = nc.tensor.matmul(b_sim[0][:, 4 * i:4 * i + 4], qkT[:, 0, i, toks], nkbd[:, i], start=True, stop=True,
                                                   skip_group_check=True)
                        ins.then_inc(*pe_heads(f"null{qt}"))
                    for i, ab in enumerate("AB"):
                        ch = slice(i * DH1, (i + 1) * DH1)
                        if p % HP == 0 and i == 0:
                            pe.wait_ge(*dve_heads.at(b, f"sn{qt}"))
                        elif p:
                            pe.wait_ge(*dve_heads.at(b, f"sim{ab}{p - 1}"))
                        else:
                            pe.wait_ge(*dve_heads.at(b - 1, f"sim{ab}{STEPS - 1}"))
                        nc.tensor.matmul(b_sim[i][:, 0:P * (qt + 1)], qkT[ch, 0, hp, toks], qkT[ch, 1, hp, 0:P * (qt + 1)],
                                         start=True, stop=True).then_inc(*pe_heads(f"sim{ab}{p}"))
                if 1 <= p <= STEPS:
                    p1 = p - 1
                    nc1 = p1 // HP + 1
                    if p1:
                        pe.wait_ge(*act_heads.at(b, f"prT{p1 - 1}"))
                    for half in halves_at(p1, 5):
                        pe.wait_ge(*dve_heads.at(b, f"pnT{half}"))
                    for half in halves_at(p1, 8):
                        pe.wait_ge(*act_heads.at(b, f"oT{half}"))
                    for half in halves_at(p, 9):
                        pe.wait_ge(*dve_heads.at(b, f"add{half}"))
                    if p1 == 0:
                        pe.wait_ge(*dve_heads.at(b - 1, f"add{STEPS // 4 - 1}"))
                    pe.wait_ge(*act_heads.at(b, f"expB{p1}"))
                    for i in range(2):
                        for c in range(nc1):
                            ins = nc.tensor.transpose(b_prT[:, (i * nc1 + c) * P:(i * nc1 + c + 1) * P],
                                                      prb[p1 % 2][:, i, c * P:(c + 1) * P], ident)
                    ins.then_inc(*pe_heads(f"prT{p1}"))
                for half in halves_at(p, 5):
                    pe.wait_ge(*act_heads.at(b, f"pn{half}"))
                    pe.wait_ge(*act_heads.at(b, f"prT{min(p - 1, STEPS - 1)}"))
                    for before in halves_at(p, 9):
                        pe.wait_ge(*dve_heads.at(b, f"add{before}"))
                    nc.tensor.transpose(b_prT[0:NULL * HALF, 0:P], pn[:].rearrange("p h j -> p (h j)"), ident).then_inc(*pe_heads(f"pnT{half}"))
                if 3 <= p < STEPS + 3:
                    p3 = p - 3
                    q3 = p3 // HP
                    if p3 % 4 == 0:
                        pe.wait_ge(*(dve_heads.at(b, f"o{p3 // 4 - 1}") if p3 else dve_heads.at(b - 1, f"o{STEPS // 4 - 1}")))
                    if p3 == 0:
                        pe.wait_ge(*act_f1.at(b, "v3"))
                    pe.wait_ge(*act_heads.at(b, f"prT{p3}"))
                    for i in range(2):
                        h = 2 * (p3 % HP) + i
                        for c in range(q3 + 1):
                            ins = nc.tensor.matmul(b_pv[:, h % HALF * DH1:(h % HALF + 1) * DH1], prT[p3 % 3][:, i, c * P:(c + 1) * P],
                                                   v[:, c, h * DH1:(h + 1) * DH1], start=(p3 % 4 == 0 and i == 0 and c == 0),
                                                   stop=False, skip_group_check=True)
                    ins.then_inc(*pe_heads(f"pv{p3}"))
                for half in halves_at(p, 6):
                    pe.wait_ge(*dve_heads.at(b, f"pnT{half}"))
                    nc.tensor.matmul(b_pv[:], pnT[:], nvbd[:, half % 2], start=False, stop=True, skip_group_check=True)\
                        .then_inc(*pe_heads(f"pvn{half}"))
                for half in halves_at(p, 8):
                    pe.wait_ge(*dve_heads.at(b, f"o{half}"))
                    if p - 1 < STEPS:
                        pe.wait_ge(*act_heads.at(b, f"prT{p - 1}"))
                    for i in range(4):
                        ins = nc.tensor.transpose(b_prT[:, i * P:(i + 1) * P], o[:, i * P:(i + 1) * P], ident)
                    ins.then_inc(*pe_heads(f"oT{half}"))

            for k in range(PIECES):
                front0(0, k)
            pe.wait_ge(null_dve, 4)
            nc.tensor.transpose(b_pv[:, 0:NULL * H1], nkw[:].rearrange("p a d -> p (a d)"), ident[0:NULL * H1, 0:NULL * H1])\
                .then_inc(null_pe, 1)
            pe.wait_ge(null_dve, 7)
            all_rounds(pe, (heads, experts, front0, front1))


def table(widths):
    out, at = {}, 0
    for name, n in widths:
        out[name] = (at, n)
        at += n
    return out, at


SMALL, SMALL_COLS = table([("wq0", P), ("wk0", P), ("wv0", P), ("wout0", D), ("router0", E), ("router1", E), ("b_out", D),
                           ("gamma0", 1), ("beta0", 1), ("rms", 1), ("gamma1", 1), ("qs2", 1), ("ks2", 1)])
CONST, CONST_COLS = table([("ident", P), ("ones", P), ("null_bias", T * NULL * H1), ("head_mask", P), ("iota8", E)])


def constants():
    c = np.zeros((P, CONST_COLS), np.float32)

    def put(name, a):
        at, n = CONST[name]
        c[:, at:at + n] = a

    row = np.arange(P)[:, None]
    put("ident", np.eye(P))
    put("ones", 1.0)
    slope = np.array(slopes(), np.float32)
    gone = np.arange(T)[None, :, None, None] * P + row[:, :, None, None] + NULL - np.arange(NULL)[None, None, None, :]
    put("null_bias", (gone * slope[None, None, :, None]).astype(np.float32).reshape(P, -1))
    put("head_mask", (row // DH0) == (np.arange(P)[None, :] // DH0))
    put("iota8", np.arange(E)[None, :])
    return c


def distances():
    d = P + np.arange(P)[:, None] - np.arange(S)[None, :]
    return np.where(d < 0, np.float32(FAR), d.astype(np.float32))


def kernel(**inputs):
    import numpy as _np
    import concourse.bacc as _bacc
    from concourse import mybir as _mybir
    from concourse.bass_utils import run_bass_kernel_spmd as _run

    a = {k: _np.asarray(v) for k, v in inputs.items()}
    qkv0 = a["L0_attn_w_qkv"]
    parts = {
        "wq0": qkv0[:, 0:P], "wk0": qkv0[:, P:2 * P], "wv0": qkv0[:, 2 * P:3 * P], "wout0": a["L0_attn_w_out"],
        "router0": a["L0_ffn_w_router"].T, "router1": a["L1_ffn_gate_w"].T,
        "b_out": _np.broadcast_to(a["L0_attn_b_out"][None, :], (P, D)),
        "gamma0": a["L0_attn_gamma"].reshape(D, 1), "beta0": a["L0_attn_beta"].reshape(D, 1),
        "rms": a["L0_ffn_norm_scale"].reshape(D, 1), "gamma1": a["L1_attn_gamma"].reshape(D, 1),
        "qs2": _np.concatenate([a["L1_attn_q_scale"]] * 2).reshape(P, 1),
        "ks2": _np.concatenate([a["L1_attn_k_scale"]] * 2).reshape(P, 1),
    }
    null = a["L1_attn_null_kv"].reshape(H1, NULL, 2, DH1)
    null_k = null[:, :, 0].reshape(H1 * NULL, DH1)
    null_v = _np.zeros((HALF, NULL, T, HALF, DH1), null.dtype)
    for h in range(H1):
        null_v[h % HALF, :, h // HALF, h % HALF] = null[h, :, 1]
    arrays = {
        "x": a["L0_attn_x"],
        "w_small": _np.concatenate([parts[n] for n in SMALL], axis=1),
        "w_up0": a["L0_ffn_w_up"].transpose(2, 0, 1).reshape(D, -1),
        "w_dn0": a["L0_ffn_w_down"].reshape(E, D, HB, P).transpose(3, 0, 2, 1).reshape(P, -1),
        "w_qkv1": _np.concatenate([a["L1_attn_w_q"], a["L1_attn_w_kv"]], axis=1),
        "w_out1": a["L1_attn_w_out"].reshape(HP, P, D).transpose(1, 0, 2).reshape(P, -1),
        "w_up1": a["L1_ffn_w13_weight"].transpose(2, 0, 1).reshape(D, -1),
        "w_dn1": a["L1_ffn_w2_weight"].reshape(E, D, HB, P).transpose(3, 0, 2, 1).reshape(P, -1),
        "null_k": _np.concatenate([null_k, null_k], axis=1),
        "null_v": null_v.reshape(HALF * NULL, -1),
        "consts": constants(),
        "distance": distances(),
    }
    arrays = {n: _np.ascontiguousarray(v) for n, v in arrays.items()}
    nc = _bacc.Bacc("TRN2", target_bir_lowering=False, num_devices=1)
    args = [nc.dram_tensor(n, v.shape, _mybir.dt.from_np(v.dtype), kind="ExternalInput").ap() for n, v in arrays.items()]
    args.append(nc.dram_tensor("result", (B, S, D), _mybir.dt.float32, kind="ExternalOutput").ap())
    build(nc, *args)
    r = _run(nc, [arrays], core_ids=[0])
    return r.results[0]["result"]
```

```python
from contextlib import ExitStack

import numpy as np

import concourse.bass as bass
from concourse import mybir

F32 = mybir.dt.float32
F32R = mybir.dt.float32r
U32 = mybir.dt.uint32
ALU = mybir.AluOpType
ACT = mybir.ActivationFunctionType
AX = mybir.AxisListType

P = 128
B, S, D = 8, 256, 128
T = S // P
E = 8
HID = 256
HB = HID // P
H0, DH0 = 4, 32
H1, DH1 = 16, 64
HD1 = H1 * DH1
HP = H1 // 2
NULL = 2
SIM_SCALE = 8.0
GROUPS = 4
LN_EPS, RMS_EPS = 1e-5, 1e-6
HALF = 8
STEPS = T * HP
ROUND = STEPS + 6
PIECES = 2 * ROUND
FAR = 1e38


def slopes():
    start = 2.0 ** (-2.0 ** (-(np.log2(H1) - 3.0)))
    return [float(np.float32(start * start ** i)) for i in range(H1)]


class Progress:

    def __init__(self, sem, names):
        self.sem, self.names, self.per = sem, list(names), len(names)
        self.index = {n: i + 1 for i, n in enumerate(self.names)}
        self.next = 0

    def __call__(self, name):
        assert self.names[self.next % self.per] == name, (name, self.names[self.next % self.per])
        self.next += 1
        return self.sem, 1

    def at(self, b, name):
        if isinstance(b, int):
            b = min(b, B - 1)
        return self.sem, b * self.per + (2 * self.per + self.index[name])


def experts_at(p, m0, m1):
    first = range(E) if m0 else []
    second = [8, 9, 10, 11, 14, 16, 17, 18] if m0 else [1, 2, 3, 4, 8, 11, 12, 13]
    out = [(0, p)] if p in first else []
    return out + [(1, second.index(p))] if m1 and p in second else out


def moe_order(layer, at, after):
    out = []
    for p in range(ROUND):
        out += [f"{n}{e}" for l, e in experts_at(p, True, True) if l == layer for n in at]
        out += [f"{n}{e}" for l, e in experts_at(p - 1, True, True) if l == layer for n in after]
    return out


def build(nc, x, w_small, w_up0, w_dn0, w_qkv1, w_out1, w_up1, w_dn1, null_k, null_v, consts, distance, out):
    ctx = ExitStack()
    with ctx:
        def sb(name, shape, dt=F32):
            return ctx.enter_context(nc.sbuf_tensor(name, shape, dt))

        def bank(name):
            return ctx.enter_context(nc.psum_tensor(name, [P, 512], F32))

        def sem(name):
            return ctx.enter_context(nc.semaphore(name))

        def progress(name, names):
            return Progress(sem(name), names)

        small = sb("small", [P, SMALL_COLS])
        cst = sb("cst", [P, CONST_COLS])
        up_h = [sb(f"up_h{i}", [P, E, 2 * HID], F32R) for i in range(2)]
        up_l = [sb(f"up_l{i}", [P, E, 2 * HID], F32R) for i in range(2)]
        down = [sb(f"down{i}", [P, E, HB, D]) for i in range(2)]
        qkv1 = sb("qkv1", [P, 3 * HD1])
        wout1 = sb("wout1", [P, HP, D])
        bias = sb("bias", [P, H1, S])
        nkw = sb("nkw", [NULL * H1, 2, DH1])
        nk_ss = sb("nk_ss", [NULL * H1, 4])
        nkbd = sb("nkbd", [P, HP, 2 * NULL])
        nvbd = sb("nvbd", [NULL * HALF, T, HALF * DH1])
        qscale = sb("qscale", [P, 1])
        halves = sb("halves", [P, 64])

        def cols(tile, table, name):
            at, n = table[name]
            return tile[:, at:at + n]

        ident = cols(cst, CONST, "ident")
        null_bias = cols(cst, CONST, "null_bias").rearrange("p (t n) -> p t n", t=T)
        head_mask = cols(cst, CONST, "head_mask")
        iota8 = cols(cst, CONST, "iota8")
        wq0, wk0, wv0 = (cols(small, SMALL, n) for n in ("wq0", "wk0", "wv0"))
        wout0, router0, router1 = (cols(small, SMALL, n) for n in ("wout0", "router0", "router1"))
        gamma0, beta0, rms_scale, gamma1 = (cols(small, SMALL, n) for n in ("gamma0", "beta0", "rms", "gamma1"))
        qs2, ks2 = (cols(small, SMALL, n) for n in ("qs2", "ks2"))
        b_out = cols(small, SMALL, "b_out")[0:1]
        ones_row = cols(cst, CONST, "ones")[0:1]

        x_in = sb("x_in", [P, T, D])
        xn = sb("xn", [P, T, D])
        tin = sb("tin", [P, 2 * T, D])
        stats = [sb(f"stats{i}", [P, T, 6]) for i in range(4)]
        mv = [sb(f"mv{i}", [P, T, 2]) for i in range(4)]
        var = [sb(f"var{i}", [P, 2 * T]) for i in range(4)]
        rstd = [sb(f"rstd{i}", [P, 2 * T]) for i in range(4)]
        start0 = sb("start0", [P, T, D])
        acc0 = sb("acc0", [P, T, D])
        start1 = sb("start1", [P, T, D])
        acc1 = sb("acc1", [P, T, D])
        xaT = sb("xaT", [P, S])
        xfT = sb("xfT", [P, S])
        xf_h = [sb(f"xf_h{i}", [P, S], F32R) for i in range(2)]
        xf_l = [sb(f"xf_l{i}", [P, S], F32R) for i in range(2)]
        nkmax = sb("nkmax", [P, 1])
        ksum = sb("ksum", [P, 2])
        keT = xn[:].rearrange("p t d -> p (t d)")
        qsT = sb("qsT", [P, S])
        vk = sb("vk", [P, 2, T, P])
        ctxT = sb("ctxT", [P, P])
        mix = sb("mix", [P, D])
        rt = [sb(f"rt{i}", [P, T, E]) for i in range(2)]
        prob = sb("prob", [P, T, E])
        gpad = sb("gpad", [P, T, E])
        gtop = sb("gtop", [P, T, E])
        gidx = sb("gidx", [P, T, E], U32)
        gidxf = sb("gidxf", [P, T, 2])
        gmask = sb("gmask", [P, T, 2, GROUPS])
        masked = sb("masked", [P, T, E])
        top = [sb(f"top{i}", [P, T, E]) for i in range(2)]
        topi = [sb(f"topi{i}", [P, T, E], U32) for i in range(2)]
        topf = [sb(f"topf{i}", [P, T, 2]) for i in range(2)]
        tw = [sb(f"tw{i}", [P, 8, T]) for i in range(2)]
        one = [sb(f"one{i}", [P, 2, T, E]) for i in range(2)]
        cw = [sb(f"cw{i}", [P, T, E]) for i in range(2)]
        qk = sb("qk", [P, 2, T, HD1])
        sq = sb("sq", [P, HD1 // 2])
        ss = sb("ss", [P, 2, T, H1])
        rn = sb("rn", [P, 2, T, H1])
        qkT = sb("qkT", [P, 2, HP, S])
        v = sb("v", [P, T, HD1])
        th = [sb(f"th{i}", [P, HB * S]) for i in range(2)]
        hid = [sb(f"hid{i}", [P, HB, S]) for i in range(2)]
        sn = sb("sn", [P, T, H1, NULL])
        nmin = sb("nmin", [P, T, H1])
        mneg = sb("mneg", [P, T, H1])
        lsum = sb("lsum", [P, T, H1])
        rl = sb("rl", [P, T, H1])
        prb = [sb(f"prb{i}", [P, 2, S]) for i in range(2)]
        prT = [sb(f"prT{i}", [P, 2, S]) for i in range(3)]
        pnd = sb("pnd", [P, HALF, NULL])
        pn = sb("pn", [P, HALF, NULL])
        pnT = sb("pnT", [NULL * HALF, P])
        o = sb("o", [P, HALF * DH1])
        oT = sb("oT", [P, 4, P])

        raw_up = [qkT[:].rearrange("p a b c -> p (a b c)"), qk[:].rearrange("p a b c -> p (a b c)")]
        dist = prb[0][:, 0]

        def quarter(t, c):
            flat = t if len(t.shape) == 2 else t[:].rearrange("p e n -> p (e n)")
            n = E * 2 * HID // 4
            return flat[:, c * n:(c + 1) * n]

        nk_sq = prT[0][0:NULL * H1, 0, 0:2 * DH1].rearrange("p (a d) -> p a d", a=2)

        b_gate, b_up, b_y = bank("b_gate"), bank("b_up"), bank("b_y")
        b_sim = [bank("b_simA"), bank("b_simB")]
        b_prT, b_pv, b_front = bank("b_prT"), bank("b_pv"), bank("b_front")

        def proj_bank(b, n):
            return turn_banks[n % 3] if isinstance(b, int) and b == 0 else b_front

        turn_banks = [b_front, *b_sim]

        small_in, const_in, up0_in, dn0_in = (sem(n) for n in ("small_in", "const_in", "up0_in", "dn0_in"))
        qkv_in, wout_in, up1_in, dn1_in, null_in, dist_in = (sem(n) for n in ("qkv_in", "wout_in", "up1_in", "dn1_in", "null_in", "dist_in"))
        half_set = sem("half_set")
        pad_set = sem("pad_set")
        bias_set = sem("bias_set")
        qscale_set = sem("qscale_set")
        up_hi, up_lo = [sem(f"up_hi{i}") for i in range(2)], [sem(f"up_lo{i}") for i in range(2)]
        null_dve, null_pool, null_pe = sem("null_dve"), sem("null_pool"), sem("null_pe")

        x_loaded, out_stored = sem("x_loaded"), sem("out_stored")
        dve_met, pool_met = sem("dve_met"), sem("pool_met")
        QKT = [f"qkT{n}" for n in range(8)]
        PROJ = [f"proj{n}" for n in range(8)]
        VS = [f"v{n}" for n in range(4)]
        SS = lambda n: [f"ss{n}", f"floor{n}"]
        LN = lambda r: [f"stats{r}", f"aggr{r}", f"var{r}"]
        TOP = lambda r: [f"{n}{r}" for n in ("max", "idx", "idxf")]
        pe_f0 = progress("pe_f0", ["T0", "qk0", "vk0", "ctx", "mix", "out0"])
        act_f0 = progress("act_f0", ["xaT", "xfT", "kexp", "vk", "mix", "xfh", "topexp"])
        pool_f0 = progress("pool_f0", ["rstd0", "rstd1", "xfl"])
        dve_f0 = progress("dve_f0", LN(0) + ["xn0"] + LN(1) + ["msq", "ms", "tin0", "start0", "nkmax", "rksum", "qsT", "ctxT",
                                                               "out0", "rt0"] + TOP(0)
                          + ["gap", "den0", "w1_0", "w2_0", "w1h", "w2h", "one0", "cw0"])
        pe_f1 = progress("pe_f1", ["T1", "logit1"] + PROJ + QKT + VS)
        act_f1 = progress("act_f1", ["xaT1", "xfT1", "rexp0", "rexp1"] + [x for n in range(8) for x in (f"proj{n}", f"sq{n}")] + QKT + VS + ["xfh1"])
        pool_f1 = progress("pool_f1", ["rstd2", "rstd3", "start1"] + [x for n in range(8) for x in (f"rn{n}", f"nrm{n}")] + ["xfl1"])
        dve_f1 = progress("dve_f1", LN(2) + ["xn1"] + LN(3) + ["tin1", "rt1", "nrmax"]
                          + [x for n in range(8) for x in SS(n)]
                          + ["rsum", "prob", "group", "gmax", "gidx", "gidxf", "gone", "gmask", "masked"] + TOP(1)
                          + ["den1", "rden", "rdenh", "tw1", "one1", "cw1"])
        pe_moe = [progress(f"pe_moe{i}", moe_order(i, ["g", "u"], ["dn"])) for i in range(2)]
        act_moe = [progress(f"act_moe{i}", moe_order(i, ["th"], [])) for i in range(2)]
        dve_moe = [progress(f"dve_moe{i}", moe_order(i, ["ga", "hid"], ["y"])) for i in range(2)]

        def expert_before(b, layer, e):
            if e:
                return layer, b, e - 1
            return (0, b + 1, E - 1) if layer else (1, b - 2, E - 1)

        def head_order(per_step):
            return [n for p in range(ROUND) for n in per_step(p)]

        def halves_at(p, late):
            return [(p - late) // 4] if p >= late and (p - late) % 4 == 0 and (p - late) // 4 < STEPS // 4 else []

        def pair_order(p):
            return ((1, "B"), (0, "A")) if p % HP == 0 else ((0, "A"), (1, "B"))

        def pe_head_steps(p):
            out = []
            if p < STEPS:
                out += [f"null{p // HP}"] * (p % HP == 0) + [f"sim{ab}{p}" for _, ab in pair_order(p)]
            out += [f"pnT{h}" for h in halves_at(p, 5)] + [f"oT{h}" for h in halves_at(p, 8)] + [f"op{h}" for h in halves_at(p, 9)]
            out += [f"prT{p - 1}"] * (1 <= p <= STEPS)
            out += [f"pv{p - 3}"] * (3 <= p < STEPS + 3)
            return out + [f"pvn{h}" for h in halves_at(p, 6)]

        def dve_head_steps(p):
            out = [f"pnd{h}" for h in halves_at(p, 4)]
            if p < STEPS:
                out += [f"sn{p // HP}", f"nmin{p // HP}"] * (p % HP == 0) + [f"sim{ab}{p}" for _, ab in pair_order(p)]
            out += [f"add{h}" for h in halves_at(p, 9)]
            out += [n for h in halves_at(p, 5) for n in (f"pnT{h}", f"l1_{h}", f"l2_{h}", f"rl{h}")]
            return out + [f"o{h}" for h in halves_at(p, 6)]

        def act_head_steps(p):
            out = [f"pn{h}" for h in halves_at(p, 4)]
            out += [f"exp{ab}{p}" for _, ab in pair_order(p)] if p < STEPS else []
            out += [f"oT{h}" for h in halves_at(p, 8)]
            return out + [f"prT{p - 1}"] * (1 <= p <= STEPS)

        pe_heads = progress("pe_heads", head_order(pe_head_steps))
        dve_heads = progress("dve_heads", head_order(dve_head_steps))
        act_heads = progress("act_heads", head_order(act_head_steps))

        def in_round(b, scores, values, outputs, hidden, front0, front1, m0=True, m1=True, f0=True, f1=True, h=True):
            for p in range(ROUND):
                for piece in (2 * p, 2 * p + 1):
                    if h and piece % 2 == 0:
                        scores(b, p, m0, m1)
                    if h and piece % 2:
                        values(b, p, m0, m1)
                    if piece % 2 == 0:
                        hidden(b, p, m0, m1)
                        outputs(b, p, m0, m1)
                    if f0:
                        front0(b + 2, piece)
                    if f1:
                        front1(b + 1, piece)

        def nothing(*_):
            pass

        def all_rounds(engine, parts):
            in_round(-1, *parts, m1=False, h=False)
            with engine.Fori(0, B - 2) as b:
                in_round(b, *parts)
            in_round(B - 2, *parts, f0=False)
            in_round(B - 1, *parts, m0=False, f0=False, f1=False)

        block = ctx.enter_context(nc.Block())

        @block.sync
        def _(sp):
            sp.sem_inc(x_loaded, 16)
            sp.sem_inc(out_stored, 16)

            def load_x(b):
                sp.wait_ge(*dve_f0.at(b - 1, "start0"))
                sp.dma_start(x_in[:], x[b].rearrange("(t p) d -> p t d", p=P)).then_inc(x_loaded, 16)

            def store(b):
                sp.wait_ge(*dve_heads.at(b, f"add{STEPS // 4 - 1}"))
                sp.wait_ge(*dve_moe[1].at(b, f"y{E - 1}"))
                sp.dma_start(out[b].rearrange("(t p) d -> p t d", p=P), acc1[:]).then_inc(out_stored, 16)

            load_x(0)
            sp.dma_start(cst[:], consts).then_inc(const_in, 16)
            sp.dma_start(small[:], w_small).then_inc(small_in, 16)
            sp.dma_start(raw_up[0], w_up0).then_inc(up0_in, 16)
            sp.dma_start(down[0][:].rearrange("p e a c -> p (e a c)"), w_dn0).then_inc(dn0_in, 16)
            sp.dma_start(dist, distance).then_inc(dist_in, 16)
            sp.dma_start(nkw[:].rearrange("p a d -> p (a d)"), null_k).then_inc(null_in, 16)
            sp.dma_start(nvbd[:].rearrange("p a d -> p (a d)"), null_v).then_inc(null_in, 16)
            sp.dma_start(raw_up[1], w_up1).then_inc(up1_in, 16)
            sp.dma_start(qkv1[:], w_qkv1).then_inc(qkv_in, 16)
            sp.dma_start(wout1[:].rearrange("p h c -> p (h c)"), w_out1).then_inc(wout_in, 16)
            sp.dma_start(down[1][:].rearrange("p e a c -> p (e a c)"), w_dn1).then_inc(dn1_in, 16)
            load_x(1)
            with sp.Fori(0, B - 2) as b:
                load_x(b + 2)
                store(b)
            store(B - 2)
            store(B - 1)
            sp.wait_ge(out_stored, 16 * (B + 1))

        @block.gpsimd
        def _(pool):
            for prog in (pool_f0, pool_f1):
                pool.sem_inc(prog.sem, 2 * prog.per)
            nc.gpsimd.memset(halves[:], -0.5).then_inc(half_set, 1)

            def front0(b, k):
                if k == 0:
                    pool.wait_ge(half_set, 1)
                    pool.wait_ge(*dve_f0.at(b, "var0"))
                    nc.gpsimd.tensor_tensor(rstd[0][:, 0:T], var[0][:, 0:T], halves[:, 0:T], ALU.pow)\
                        .then_inc(*pool_f0("rstd0"))
                if k == 1:
                    pool.wait_ge(*dve_f0.at(b, "ms"))
                    nc.gpsimd.tensor_tensor(rstd[1][:], var[1][:], halves[:, 0:2 * T], ALU.pow)\
                        .then_inc(*pool_f0("rstd1"))
                if k == 18:
                    pool.wait_ge(*act_f0.at(b, "xfh"))
                    pool.wait_ge(*pe_moe[0].at(b - 1, f"u{E - 1}"))
                    nc.gpsimd.tensor_tensor(xf_l[0][:], xfT[:], xf_h[0][:].bitcast(F32), ALU.subtract)\
                        .then_inc(*pool_f0("xfl"))

            def front1(b, k):
                if k in (17, 18):
                    r = k - 15
                    pool.wait_ge(*dve_f1.at(b, f"var{r}"))
                    nc.gpsimd.tensor_tensor(rstd[r][:, 0:T], var[r][:, 0:T], halves[:, 0:T], ALU.pow)\
                        .then_inc(*pool_f1(f"rstd{r}"))
                if k == 24:
                    pool.wait_ge(*dve_moe[0].at(b, f"y{E - 1}"))
                    pool.wait_ge(*dve_moe[1].at(b - 1, "y0"))
                    pool.wait_ge(*dve_heads.at(b - 1, "add0"))
                    pool.sem_inc(pool_met, 1)
                    nc.gpsimd.tensor_copy(start1[:], acc0[:]).then_inc(*pool_f1("start1"))
                def piece_of(n):
                    return n // 4, n // 2 % 2, n % 2

                if 26 <= k < 34:
                    n = k - 26
                    w, t, g = piece_of(n)
                    hs = slice(g * HALF, (g + 1) * HALF)
                    pool.wait_ge(*dve_f1.at(b, f"floor{n}"))
                    nc.gpsimd.tensor_tensor(rn[:, w, t, hs], ss[:, w, t, hs], halves[:, 0:HALF], ALU.pow).then_inc(*pool_f1(f"rn{n}"))
                    part = qk[:, w, t, g * 512:g * 512 + 512].rearrange("p (h d) -> p h d", h=HALF)
                    pool.wait_ge(*pool_f1.at(b, f"rn{n}"))
                    nc.gpsimd.tensor_tensor(part, part, rn[:, w, t, hs].unsqueeze(2).to_broadcast([P, HALF, DH1]), ALU.mult)\
                        .then_inc(*pool_f1(f"nrm{n}"))
                if k == PIECES - 1:
                    pool.wait_ge(*act_f1.at(b, "xfh1"))
                    pool.wait_ge(*pe_moe[1].at(b - 1, f"u{E - 1}"))
                    nc.gpsimd.tensor_tensor(xf_l[1][:], xfT[:], xf_h[1][:].bitcast(F32), ALU.subtract)\
                        .then_inc(*pool_f1("xfl1"))

            for k in range(2):
                front0(0, k)
            pool.wait_ge(null_dve, 3)
            nc.gpsimd.tensor_tensor(nk_ss[:, 2:4], nk_ss[:, 0:2], halves[0:NULL * H1, 0:2], ALU.pow).then_inc(null_pool, 1)
            for k in range(2, PIECES):
                front0(0, k)
            pool.wait_ge(up_hi[1], 1)
            nc.gpsimd.tensor_tensor(up_l[1][:].rearrange("p e n -> p (e n)"), raw_up[1],
                                    up_h[1][:].rearrange("p e n -> p (e n)").bitcast(F32), ALU.subtract)\
                .then_inc(up_lo[1], 1)
            all_rounds(pool, (nothing, nothing, nothing, nothing, front0, front1))

        @block.scalar
        def _(act):
            for prog in (act_f0, act_f1, *act_moe, act_heads):
                act.sem_inc(prog.sem, 2 * prog.per)

            def front0(b, k):
                if k == 5:
                    act.wait_ge(small_in, 16)
                    act.wait_ge(*pe_f1.at(b - 2, "v3"))
                    act.wait_ge(*pe_f0.at(b, "T0"))
                    nc.scalar.activation(xaT[:], b_front[:, 0:S], ACT.Identity, bias=beta0, scale=gamma0)\
                        .then_inc(*act_f0("xaT"))
                    act.wait_ge(*pool_f1.at(b - 2, "xfl1"))
                    nc.scalar.activation(xfT[:], b_front[:, S:2 * S], ACT.Copy, scale=rms_scale).then_inc(*act_f0("xfT"))
                if k == 8:
                    act.wait_ge(*dve_f0.at(b, "nkmax"))
                    nc.scalar.activation(keT, b_front[:, S:2 * S], ACT.Exp, bias=nkmax[:], accum_out=ksum[:, 0:1])\
                        .then_inc(*act_f0("kexp"))
                if k == 10:
                    act.wait_ge(*pe_f0.at(b, "vk0"))
                    nc.scalar.activation(vk[:].rearrange("p a t d -> p (a t d)"), b_front[:], ACT.Copy).then_inc(*act_f0("vk"))
                if k == 13:
                    act.wait_ge(*pe_f0.at(b, "mix"))
                    nc.scalar.activation(mix[:], b_front[:, 0:D], ACT.Copy).then_inc(*act_f0("mix"))
                if k == 36:
                    act.wait_ge(*dve_f0.at(b, "gap"))
                    nc.scalar.activation(tw[0][:, 1], tw[0][:, 0], ACT.Exp).then_inc(*act_f0("topexp"))
                if k == 17:
                    act.wait_ge(*pe_moe[0].at(b - 1, f"u{E - 1}"))
                    act.wait_ge(*act_f0.at(b, "xfT"))
                    nc.scalar.activation(xf_h[0][:], xfT[:], ACT.Copy).then_inc(*act_f0("xfh"))

            def front1(b, k):
                if k == 21:
                    act.wait_ge(*pe_f0.at(b + 1, "out0"))
                    act.wait_ge(*pool_f0.at(b + 1, "xfl"))
                    act.wait_ge(*pe_f1.at(b, "T1"))
                    nc.scalar.activation(xaT[:], b_front[:, 0:S], ACT.Copy, scale=gamma1).then_inc(*act_f1("xaT1"))
                    nc.scalar.activation(xfT[:], b_front[:, S:2 * S], ACT.Copy).then_inc(*act_f1("xfT1"))
                if k == 23:
                    act.wait_ge(*dve_f1.at(b, "nrmax"))
                    for t in range(T):
                        nc.scalar.activation(prob[:, t], rt[1][:, t], ACT.Exp, bias=tw[1][:, 0, t:t + 1],
                                             accum_out=tw[1][:, 1, t:t + 1]).then_inc(*act_f1(f"rexp{t}"))
                if 24 <= k < 32:
                    n = k - 24
                    act.wait_ge(*pe_f1.at(b, f"proj{n}"))
                    if n == 0:
                        act.wait_ge(up_lo[1], 1)
                        act.wait_ge(*pe_f1.at(b - 1, "qkT7"))
                    part = qk[:, n // 4, n // 2 % 2, n % 2 * 512:n % 2 * 512 + 512]
                    nc.scalar.activation(part, proj_bank(b, n)[:], ACT.Copy).then_inc(*act_f1(f"proj{n}"))
                    act.wait_ge(*act_f1.at(b, f"proj{n}"))
                    act.wait_ge(*(dve_f1.at(b, f"ss{n - 1}") if n else dve_f1.at(b - 1, "ss7")))
                    nc.scalar.activation(sq[:], part, ACT.Square).then_inc(*act_f1(f"sq{n}"))
                if 31 <= k < 39:
                    n = k - 31
                    w, t, g = n // 4, n // 2 % 2, n % 2
                    act.wait_ge(*pe_f1.at(b, f"qkT{n}"))
                    if n == 0:
                        act.wait_ge(qscale_set, 2)
                        act.wait_ge(up_lo[0], 4)
                        act.wait_ge(*pe_heads.at(b - 1, f"simB{STEPS - 1}"))
                    nc.scalar.activation(qkT[:, w, 4 * g:4 * g + 4, t * P:(t + 1) * P],
                                         turn_banks[n % 3][:].rearrange("p (h q) -> p h q", h=4), ACT.Copy,
                                         **({} if w else {"scale": qscale[:]})).then_inc(*act_f1(f"qkT{n}"))
                if 38 <= k < 42:
                    n = k - 38
                    act.wait_ge(*pe_f1.at(b, f"v{n}"))
                    if n == 0:
                        act.wait_ge(*pe_heads.at(b - 1, f"pv{STEPS - 1}"))
                    nc.scalar.activation(v[:, n // 2, n % 2 * 512:n % 2 * 512 + 512], turn_banks[(8 + n) % 3][:], ACT.Copy)\
                        .then_inc(*act_f1(f"v{n}"))
                if k == PIECES - 1:
                    act.wait_ge(*act_f1.at(b, "xfT1"))
                    act.wait_ge(*pe_moe[1].at(b - 1, f"u{E - 1}"))
                    nc.scalar.activation(xf_h[1][:], xfT[:], ACT.Copy).then_inc(*act_f1("xfh1"))

            def hidden(b, p, m0, m1):
                for layer, e in experts_at(p, m0, m1):
                    act.wait_ge(*pe_moe[layer].at(b + 1 - layer, f"g{e}"))
                    if e < 2:
                        l1, b1, e1 = expert_before(b + 1 - layer, layer, 0)
                        act.wait_ge(*dve_moe[l1].at(b1, f"hid{E - 2 + e}"))
                    else:
                        act.wait_ge(*dve_moe[layer].at(b + 1 - layer, f"hid{e - 2}"))
                    nc.scalar.activation(th[e % 2][:], b_gate[:], ACT.Tanh, scale=0.5).then_inc(*act_moe[layer](f"th{e}"))

            def scores(b, p, m0, m1):
                qt = p // HP
                n = P * (qt + 1)
                for half in halves_at(p, 4):
                    act.wait_ge(*dve_heads.at(b, f"pnd{half}"))
                    nc.scalar.activation(pn[:], pnd[:], ACT.Exp).then_inc(*act_heads(f"pn{half}"))
                if p < STEPS:
                    for i, ab in pair_order(p):
                        h = 2 * (p % HP) + i
                        act.wait_ge(*dve_heads.at(b, f"sim{ab}{p}"))
                        nc.scalar.activation(prb[p % 2][:, i, 0:n], prb[p % 2][:, i, 0:n], ACT.Exp, scale=-1.0,
                                             bias=mneg[:, qt, h:h + 1], accum_out=lsum[:, qt, h:h + 1])\
                            .then_inc(*act_heads(f"exp{ab}{p}"))
                for half in halves_at(p, 8):
                    act.wait_ge(*pe_heads.at(b, f"oT{half}"))
                    nc.scalar.activation(oT[:].rearrange("p a q -> p (a q)"), b_y[:], ACT.Copy)\
                        .then_inc(*act_heads(f"oT{half}"))

            def values(b, p, m0, m1):
                if 1 <= p <= STEPS:
                    p1 = p - 1
                    n1 = P * (p1 // HP + 1)
                    act.wait_ge(*pe_heads.at(b, f"prT{p1}"))
                    if p1 >= 3:
                        act.wait_ge(*pe_heads.at(b, f"pv{p1 - 3}"))
                    nc.scalar.activation(prT[p1 % 3][:, :, 0:n1], b_prT[:, 0:2 * n1].rearrange("p (a n) -> p a n", a=2),
                                         ACT.Copy).then_inc(*act_heads(f"prT{p1}"))

            def split_up0(parts):
                act.wait_ge(up0_in, 16)
                for c in parts:
                    nc.scalar.activation(quarter(up_h[0], c), quarter(raw_up[0], c), ACT.Copy).then_inc(up_hi[0], 1)

            def biases(heads):
                act.wait_ge(dist_in, 16)
                for h in heads:
                    nc.scalar.activation(bias[:, h], dist, ACT.Copy, scale=slopes()[h]).then_inc(bias_set, 1)

            for k in range(8):
                front0(0, k)
            split_up0((0, 1))
            front0(0, 8)
            split_up0((2, 3))
            for k in range(9, 13):
                front0(0, k)
            biases(range(0, 6))
            for k in range(13, 18):
                front0(0, k)
            act.wait_ge(up1_in, 16)
            nc.scalar.activation(up_h[1][:].rearrange("p e n -> p (e n)"), raw_up[1], ACT.Copy).then_inc(up_hi[1], 1)
            for k in range(18, PIECES):
                front0(0, k)
            biases(range(6, H1))
            all_rounds(act, (scores, values, nothing, hidden, front0, front1))

        @block.vector
        def _(dve):
            for prog in (dve_f0, dve_f1, *dve_moe, dve_heads):
                dve.sem_inc(prog.sem, 2 * prog.per)
            nc.vector.memset(gpad[:], -1.0).then_inc(pad_set, 1)

            def layer_norm_stats(b, f, r, src, eps=LN_EPS):
                for t in range(T):
                    ins = nc.vector.bn_stats(stats[r][:, t], src[:, t])
                ins.then_inc(*f(f"stats{r}"))
                dve.wait_ge(*f.at(b, f"stats{r}"))
                dve.sem_inc(dve_met, 1)
                for t in range(T):
                    ins = nc.vector.bn_aggr(mv[r][:, t], stats[r][:, t])
                ins.then_inc(*f(f"aggr{r}"))
                dve.wait_ge(*f.at(b, f"aggr{r}"))
                nc.vector.tensor_scalar(var[r][:, 0:T], mv[r][:, :, 1], eps, None, ALU.add).then_inc(*f(f"var{r}"))

            def normalise(dst, src, r):
                for t in range(T):
                    ins = nc.vector.tensor_scalar(dst[:, t], src[:, t], mv[r][:, t, 0:1], rstd[r][:, t:t + 1],
                                                  ALU.subtract, ALU.mult)
                return ins

            def top2_max(b, f, i, src):
                for t in range(T):
                    ins = nc.vector.max(top[i][:, t], src[:, t])
                ins.then_inc(*f(f"max{i}"))
                dve.wait_ge(*f.at(b, f"max{i}"))
                dve.sem_inc(dve_met, 1)
                for t in range(T):
                    ins = nc.vector.max_index(topi[i][:, t], top[i][:, t], src[:, t])
                ins.then_inc(*f(f"idx{i}"))

            def top2_float(b, f, i):
                dve.wait_ge(*f.at(b, f"idx{i}"))
                nc.vector.tensor_copy(topf[i][:], topi[i][:, :, 0:2]).then_inc(*f(f"idxf{i}"))

            def combine(b, f, i, w):
                for k in range(2):
                    for t in range(T):
                        ins = nc.vector.tensor_scalar(one[i][:, k, t], iota8, topf[i][:, t, k:k + 1], w(k, t),
                                                      ALU.is_equal, ALU.mult)
                ins.then_inc(*f(f"one{i}"))
                dve.wait_ge(*f.at(b, f"one{i}"))
                nc.vector.tensor_tensor(cw[i][:], one[i][:, 0], one[i][:, 1], ALU.add).then_inc(*f(f"cw{i}"))

            def front0(b, k):
                if k == 0:
                    dve.wait_ge(x_loaded, b * 16 + 32)
                    layer_norm_stats(b, dve_f0, 0, x_in)
                if k == 1:
                    dve.wait_ge(*pool_f0.at(b, "rstd0"))
                    normalise(xn, x_in, 0).then_inc(*dve_f0("xn0"))
                    dve.wait_ge(*dve_f0.at(b, "xn0"))
                    layer_norm_stats(b, dve_f0, 1, xn)
                    nc.vector.tensor_tensor(var[1][:, T:2 * T], mv[1][:, :, 0], mv[1][:, :, 0], ALU.mult)\
                        .then_inc(*dve_f0("msq"))
                    dve.wait_ge(*dve_f0.at(b, "msq"))
                    nc.vector.scalar_tensor_tensor(out=var[1][:, T:2 * T], in0=var[1][:, T:2 * T], scalar=RMS_EPS,
                                                   in1=mv[1][:, :, 1], op0=ALU.add, op1=ALU.add).then_inc(*dve_f0("ms"))
                if k == 3:
                    dve.wait_ge(*pool_f0.at(b, "rstd1"))
                    dve.wait_ge(*pe_f1.at(b - 2, "T1"))
                    normalise(tin, xn, 1)
                    for t in range(T):
                        ins = nc.vector.tensor_scalar(tin[:, T + t], xn[:, t], rstd[1][:, T + t:T + t + 1], None, ALU.mult)
                    ins.then_inc(*dve_f0("tin0"))
                    dve.wait_ge(*dve_moe[0].at(b - 1, "y0"))
                    nc.vector.scalar_tensor_tensor(out=start0[:], in0=xn[:], scalar=2.0, in1=x_in[:], op0=ALU.mult, op1=ALU.add)\
                        .then_inc(*dve_f0("start0"))
                if k == 7:
                    dve.wait_ge(*pe_f0.at(b, "qk0"))
                    nc.vector.tensor_reduce(nkmax[:], b_front[:, S:2 * S], AX.X, ALU.max, negate=True)\
                        .then_inc(*dve_f0("nkmax"))
                if k == 9:
                    dve.wait_ge(*act_f0.at(b, "kexp"))
                    nc.vector.reciprocal(ksum[:, 1:2], ksum[:, 0:1]).then_inc(*dve_f0("rksum"))
                    dve.wait_ge(*dve_f0.at(b, "rksum"))
                    nc.vector.tensor_scalar(qsT[:], b_front[:, 0:S], ksum[:, 1:2], float(DH0) ** -0.5, ALU.mult, ALU.mult)\
                        .then_inc(*dve_f0("qsT"))
                if k == 12:
                    dve.wait_ge(const_in, 16)
                    dve.wait_ge(*pe_f0.at(b, "ctx"))
                    nc.vector.tensor_tensor(ctxT[:], b_front[:, 0:P], head_mask, ALU.mult).then_inc(*dve_f0("ctxT"))
                if k == 16:
                    dve.wait_ge(*dve_f0.at(b, "start0"))
                    dve.wait_ge(*pe_f0.at(b, "out0"))
                    nc.vector.tensor_tensor(start0[:].rearrange("p t d -> p (t d)"), b_front[:, 0:S],
                                            start0[:].rearrange("p t d -> p (t d)"), ALU.add).then_inc(*dve_f0("out0"))
                    nc.vector.tensor_copy(rt[0][:].rearrange("p t e -> p (t e)"), b_front[:, S:S + T * E])\
                        .then_inc(*dve_f0("rt0"))
                if k == 34:
                    dve.wait_ge(*dve_f0.at(b, "rt0"))
                    dve.sem_inc(dve_met, 1)
                    top2_max(b, dve_f0, 0, rt[0])
                    top2_float(b, dve_f0, 0)
                    nc.vector.tensor_tensor(tw[0][:, 0], top[0][:, :, 1], top[0][:, :, 0], ALU.subtract)\
                        .then_inc(*dve_f0("gap"))
                if k == 37:
                    dve.wait_ge(*act_f0.at(b, "topexp"))
                    nc.vector.tensor_scalar(tw[0][:, 2], tw[0][:, 1], 1.0, None, ALU.add).then_inc(*dve_f0("den0"))
                    dve.wait_ge(*dve_f0.at(b, "den0"))
                    nc.vector.reciprocal(tw[0][:, 3], tw[0][:, 2]).then_inc(*dve_f0("w1_0"))
                    dve.wait_ge(*dve_f0.at(b, "w1_0"))
                    nc.vector.tensor_tensor(tw[0][:, 4], tw[0][:, 3], tw[0][:, 1], ALU.mult).then_inc(*dve_f0("w2_0"))
                    nc.vector.tensor_scalar(tw[0][:, 5], tw[0][:, 3], 0.5, None, ALU.mult).then_inc(*dve_f0("w1h"))
                    dve.wait_ge(*dve_f0.at(b, "w2_0"))
                    nc.vector.tensor_scalar(tw[0][:, 6], tw[0][:, 4], 0.5, None, ALU.mult).then_inc(*dve_f0("w2h"))
                if k == 38:
                    dve.wait_ge(*dve_f0.at(b, "w2h"))
                    dve.wait_ge(*dve_moe[0].at(b - 1, f"y{E - 1}"))
                    combine(b, dve_f0, 0, lambda k, t: tw[0][:, 5 + k, t:t + 1])

            def front1(b, k):
                if k == 17:
                    dve.wait_ge(*dve_moe[0].at(b, f"y{E - 1}"))
                    layer_norm_stats(b, dve_f1, 2, acc0)
                if k == 18:
                    dve.wait_ge(*pool_f1.at(b, "rstd2"))
                    dve.wait_ge(*pe_f0.at(b + 1, "T0"))
                    normalise(tin[:, T:2 * T], acc0, 2).then_inc(*dve_f1("xn1"))
                    dve.wait_ge(*dve_f1.at(b, "xn1"))
                    layer_norm_stats(b, dve_f1, 3, tin[:, T:2 * T])
                if k == 19:
                    dve.wait_ge(*pool_f1.at(b, "rstd3"))
                    normalise(tin, tin[:, T:2 * T], 3).then_inc(*dve_f1("tin1"))
                if k == 23:
                    dve.wait_ge(*pe_f1.at(b, "logit1"))
                    nc.vector.tensor_copy(rt[1][:].rearrange("p t e -> p (t e)"), b_front[:, 0:T * E]).then_inc(*dve_f1("rt1"))
                    dve.wait_ge(*dve_f1.at(b, "rt1"))
                    nc.vector.tensor_reduce(tw[1][:, 0], rt[1][:], AX.X, ALU.max, negate=True).then_inc(*dve_f1("nrmax"))
                if 25 <= k < 33:
                    n = k - 25
                    dve.wait_ge(*act_f1.at(b, f"sq{n}"))
                    part = ss[:, n // 4, n // 2 % 2, n % 2 * 8:n % 2 * 8 + 8]
                    nc.vector.tensor_reduce(part, sq[:].rearrange("p (h d) -> p h d", h=8), AX.X, ALU.add).then_inc(*dve_f1(f"ss{n}"))
                    dve.wait_ge(*dve_f1.at(b, f"ss{n}"))
                    nc.vector.tensor_scalar(part, part, 1e-24, None, ALU.max).then_inc(*dve_f1(f"floor{n}"))
                if k == 33:
                    dve.wait_ge(*act_f1.at(b, "rexp1"))
                    nc.vector.reciprocal(tw[1][:, 2], tw[1][:, 1]).then_inc(*dve_f1("rsum"))
                    dve.wait_ge(*dve_f1.at(b, "rsum"))
                    for t in range(T):
                        ins = nc.vector.tensor_scalar(prob[:, t], prob[:, t], tw[1][:, 2, t:t + 1], None, ALU.mult)
                    ins.then_inc(*dve_f1("prob"))
                    dve.wait_ge(*dve_f1.at(b, "prob"))
                    dve.wait_ge(pad_set, 1)
                    nc.vector.tensor_reduce(gpad[:, :, 0:GROUPS], prob[:].rearrange("p t (g e) -> p t g e", g=GROUPS), AX.X, ALU.max)\
                        .then_inc(*dve_f1("group"))
                if k == 34:
                    dve.wait_ge(*dve_f1.at(b, "group"))
                    dve.sem_inc(dve_met, 1)
                    for t in range(T):
                        ins = nc.vector.max(gtop[:, t], gpad[:, t])
                    ins.then_inc(*dve_f1("gmax"))
                    dve.wait_ge(*dve_f1.at(b, "gmax"))
                    dve.sem_inc(dve_met, 1)
                    for t in range(T):
                        ins = nc.vector.max_index(gidx[:, t], gtop[:, t], gpad[:, t])
                    ins.then_inc(*dve_f1("gidx"))
                    dve.wait_ge(*dve_f1.at(b, "gidx"))
                    nc.vector.tensor_copy(gidxf[:], gidx[:, :, 0:2]).then_inc(*dve_f1("gidxf"))
                if k == 35:
                    dve.wait_ge(*dve_f1.at(b, "gidxf"))
                    for c in range(2):
                        for t in range(T):
                            ins = nc.vector.tensor_scalar(gmask[:, t, c], iota8[:, 0:GROUPS], gidxf[:, t, c:c + 1], None, ALU.is_equal)
                    ins.then_inc(*dve_f1("gone"))
                    dve.wait_ge(*dve_f1.at(b, "gone"))
                    nc.vector.tensor_tensor(gmask[:, :, 0], gmask[:, :, 0], gmask[:, :, 1], ALU.add).then_inc(*dve_f1("gmask"))
                    dve.wait_ge(*dve_f1.at(b, "gmask"))
                    for t in range(T):
                        ins = nc.vector.tensor_tensor(masked[:, t].rearrange("p (g e) -> p g e", g=GROUPS),
                                                      prob[:, t].rearrange("p (g e) -> p g e", g=GROUPS),
                                                      gmask[:, t, 0].unsqueeze(2).to_broadcast([P, GROUPS, E // GROUPS]), ALU.mult)
                    ins.then_inc(*dve_f1("masked"))
                if k == 36:
                    dve.wait_ge(*dve_f1.at(b, "masked"))
                    dve.sem_inc(dve_met, 1)
                    top2_max(b, dve_f1, 1, masked)
                if k == 37:
                    top2_float(b, dve_f1, 1)
                    nc.vector.tensor_tensor(tw[1][:, 3], top[1][:, :, 0], top[1][:, :, 1], ALU.add).then_inc(*dve_f1("den1"))
                    dve.wait_ge(*dve_f1.at(b, "den1"))
                    nc.vector.reciprocal(tw[1][:, 4], tw[1][:, 3]).then_inc(*dve_f1("rden"))
                    dve.wait_ge(*dve_f1.at(b, "rden"))
                    nc.vector.tensor_scalar(tw[1][:, 5], tw[1][:, 4], 0.5, None, ALU.mult).then_inc(*dve_f1("rdenh"))
                    dve.wait_ge(*dve_f1.at(b, "rdenh"))
                    for c in range(2):
                        ins = nc.vector.tensor_tensor(tw[1][:, 6 + c], top[1][:, :, c], tw[1][:, 5], ALU.mult)
                    ins.then_inc(*dve_f1("tw1"))
                if k == PIECES - 1:
                    dve.wait_ge(*dve_f1.at(b, "tw1"))
                    dve.wait_ge(*dve_moe[1].at(b - 1, f"y{E - 1}"))
                    combine(b, dve_f1, 1, lambda k, t: tw[1][:, 6 + k, t:t + 1])

            def expert(b, layer, e):
                f = dve_moe[layer]
                dve.wait_ge(*act_moe[layer].at(b, f"th{e}"))
                nc.vector.scalar_tensor_tensor(out=th[e % 2][:], in0=th[e % 2][:], scalar=1.0, in1=b_gate[:],
                                               op0=ALU.add, op1=ALU.mult).then_inc(*f(f"ga{e}"))
                dve.wait_ge(*f.at(b, f"ga{e}"))
                dve.wait_ge(*pe_moe[layer].at(b, f"u{e}"))
                nc.vector.tensor_tensor(hid[e % 2][:].rearrange("p a s -> p (a s)"), b_up[:], th[e % 2][:], ALU.mult)\
                    .then_inc(*f(f"hid{e}"))

            def expert_out(b, layer, e, m0):
                f, acc, start = dve_moe[layer], (acc0, acc1)[layer], (start0, start1)[layer]
                dve.wait_ge(*pe_moe[layer].at(b, f"dn{e}"))
                if e == 0 and layer == 0:
                    dve.wait_ge(*dve_f0.at(b, "cw0"))
                    dve.wait_ge(*pool_f1.at(b - 1, "start1"))
                if e == 0 and layer == 1:
                    dve.wait_ge(*dve_f1.at(b, "cw1"))
                    dve.wait_ge(*pool_f1.at(b, "start1"))
                    dve.wait_ge(out_stored, b * 16 + 16)
                for t in range(T):
                    begin = e == 0 and not (layer and m0 and t == 0)
                    ins = nc.vector.scalar_tensor_tensor(out=acc[:, t], in0=b_y[:, t * D:(t + 1) * D],
                                                         scalar=cw[layer][:, t, e:e + 1], in1=(start if begin else acc)[:, t],
                                                         op0=ALU.mult, op1=ALU.add)
                ins.then_inc(*f(f"y{e}"))
                dve.wait_ge(*f.at(b, f"y{e}"))

            def outputs(b, p, m0, m1):
                for layer, e in experts_at(p - 1, m0, m1):
                    expert_out(b + 1 - layer, layer, e, m0)

            def hidden(b, p, m0, m1):
                for layer, e in experts_at(p, m0, m1):
                    expert(b + 1 - layer, layer, e)

            def scores(b, p, m0, m1):
                qt = p // HP
                n = P * (qt + 1)
                for half in halves_at(p, 4):
                    q, h0 = half // 2, half % 2 * HALF
                    dve.wait_ge(*dve_heads.at(b, f"simB{4 * half + 3}"))
                    nc.vector.tensor_tensor(pnd[:], mneg[:, q, h0:h0 + HALF].unsqueeze(2).to_broadcast([P, HALF, NULL]),
                                            sn[:, q, h0:h0 + HALF], ALU.subtract).then_inc(*dve_heads(f"pnd{half}"))
                if p < STEPS:
                    if p % HP == 0:
                        dve.wait_ge(bias_set, H1)
                        dve.wait_ge(*pe_heads.at(b, f"null{qt}"))
                        nc.vector.tensor_tensor(sn[:, qt].rearrange("p h j -> p (h j)"), b_sim[0][:, 0:NULL * H1], null_bias[:, qt],
                                                ALU.add).then_inc(*dve_heads(f"sn{qt}"))
                        dve.wait_ge(*dve_heads.at(b, f"sn{qt}"))
                        nc.vector.tensor_tensor(nmin[:, qt], sn[:, qt, :, 0], sn[:, qt, :, 1], ALU.min)\
                            .then_inc(*dve_heads(f"nmin{qt}"))
                        dve.wait_ge(*dve_heads.at(b, f"nmin{qt}"))
                    for i, ab in pair_order(p):
                        h = 2 * (p % HP) + i
                        if p >= 2:
                            dve.wait_ge(*pe_heads.at(b, f"prT{p - 2}"))
                        dve.wait_ge(*pe_heads.at(b, f"sim{ab}{p}"))
                        dve.sem_inc(dve_met, 1)
                        nc.vector.tensor_tensor_reduce(prb[p % 2][:, i, 0:n], b_sim[i][:, 0:n],
                                                       bias[:, h, S - n:S], 1.0, nmin[:, qt, h:h + 1],
                                                       ALU.add, ALU.min, mneg[:, qt, h:h + 1])\
                            .then_inc(*dve_heads(f"sim{ab}{p}"))
                for half in halves_at(p, 9):
                    dve.wait_ge(*pe_heads.at(b, f"op{half}"))
                    begin = half == 0 and not (isinstance(b, int) and b == B - 1)
                    if begin:
                        dve.wait_ge(*pool_f1.at(b, "start1"))
                        dve.wait_ge(out_stored, b * 16 + 16)
                    nc.vector.tensor_tensor(acc1[:, half // 2], b_y[:, 0:D], (start1 if begin else acc1)[:, half // 2], ALU.add)\
                        .then_inc(*dve_heads(f"add{half}"))
                    dve.wait_ge(*dve_heads.at(b, f"add{half}"))
                for half in halves_at(p, 5):
                    for before in halves_at(p, 9):
                        dve.wait_ge(*pe_heads.at(b, f"op{before}"))
                    dve.wait_ge(*pe_heads.at(b, f"pnT{half}"))
                    nc.vector.tensor_copy(pnT[:], b_y[0:NULL * HALF, D:D + P]).then_inc(*dve_heads(f"pnT{half}"))
                    q, h0 = half // 2, half % 2 * HALF
                    dve.wait_ge(*act_heads.at(b, f"pn{half}"))
                    nc.vector.tensor_tensor(rl[:, q, h0:h0 + HALF], pn[:, :, 0], pn[:, :, 1], ALU.add)\
                        .then_inc(*dve_heads(f"l1_{half}"))
                    dve.wait_ge(*dve_heads.at(b, f"l1_{half}"))
                    nc.vector.tensor_tensor(rl[:, q, h0:h0 + HALF], rl[:, q, h0:h0 + HALF], lsum[:, q, h0:h0 + HALF], ALU.add)\
                        .then_inc(*dve_heads(f"l2_{half}"))
                    dve.wait_ge(*dve_heads.at(b, f"l2_{half}"))
                    nc.vector.reciprocal(rl[:, q, h0:h0 + HALF], rl[:, q, h0:h0 + HALF]).then_inc(*dve_heads(f"rl{half}"))

            def values(b, p, m0, m1):
                for half in halves_at(p, 6):
                    q, h0 = half // 2, half % 2 * HALF
                    dve.wait_ge(*dve_heads.at(b, f"rl{half}"))
                    dve.wait_ge(*pe_heads.at(b, f"pvn{half}"))
                    nc.vector.tensor_tensor(o[:].rearrange("p (h d) -> p h d", h=HALF),
                                            b_pv[:].rearrange("p (h d) -> p h d", h=HALF),
                                            rl[:, q, h0:h0 + HALF].unsqueeze(2).to_broadcast([P, HALF, DH1]), ALU.mult)\
                        .then_inc(*dve_heads(f"o{half}"))

            def split_up0(parts):
                for c in parts:
                    dve.wait_ge(up_hi[0], c + 1)
                    nc.vector.tensor_tensor(quarter(up_l[0], c), quarter(raw_up[0], c), quarter(up_h[0], c).bitcast(F32), ALU.subtract)\
                        .then_inc(up_lo[0], 1)

            for k in range(8):
                front0(0, k)
            split_up0((0,))
            for k in range(8, 10):
                front0(0, k)
            dve.wait_ge(null_in, 32)
            nc.vector.tensor_tensor(nk_sq[:], nkw[:], nkw[:], ALU.mult).then_inc(null_dve, 1)
            dve.wait_ge(null_dve, 1)
            nc.vector.tensor_reduce(nk_ss[:, 0:2], nk_sq[:], AX.X, ALU.add).then_inc(null_dve, 1)
            dve.wait_ge(null_dve, 2)
            nc.vector.tensor_scalar(nk_ss[:, 0:2], nk_ss[:, 0:2], 1e-24, None, ALU.max).then_inc(null_dve, 1)
            split_up0((1, 2))
            for k in range(10, 13):
                front0(0, k)
            dve.wait_ge(null_pool, 1)
            nc.vector.tensor_scalar(nkw[:], nkw[:], nk_ss[:, 2:3], None, ALU.mult).then_inc(null_dve, 1)
            nc.vector.memset(nkbd[:], 0.0).then_inc(null_dve, 1)
            dve.wait_ge(small_in, 16)
            nc.vector.tensor_tensor(qscale[:], qs2, ks2, ALU.mult).then_inc(qscale_set, 1)
            dve.wait_ge(qscale_set, 1)
            nc.vector.tensor_scalar(qscale[:], qscale[:], -SIM_SCALE, None, ALU.mult).then_inc(qscale_set, 1)
            split_up0((3,))
            for k in range(13, PIECES):
                front0(0, k)
            dve.wait_ge(null_dve, 5)
            dve.wait_ge(null_pe, 1)
            turned = b_pv[:, 0:NULL * H1].rearrange("p (h i j) -> p h i j", i=2, j=NULL)
            nc.vector.tensor_copy(nkbd[0:DH1, :, 0:NULL], turned[0:DH1, :, 0]).then_inc(null_dve, 1)
            nc.vector.tensor_copy(nkbd[DH1:P, :, NULL:2 * NULL], turned[DH1:P, :, 1]).then_inc(null_dve, 1)
            all_rounds(dve, (scores, values, outputs, hidden, front0, front1))

        @block.tensor
        def _(pe):
            for prog in (pe_f0, pe_f1, *pe_moe, pe_heads):
                pe.sem_inc(prog.sem, 2 * prog.per)

            def matmul3(ps, w_h, w_l, x_h, x_l, start=True):
                nc.tensor.matmul(ps, w_h, x_h, start=start, stop=False, skip_group_check=True)
                nc.tensor.matmul(ps, w_h, x_l, start=False, stop=False, skip_group_check=True)
                return nc.tensor.matmul(ps, w_l, x_h, start=False, stop=True, skip_group_check=True)

            def turn_inputs(b, f, r):
                pe.wait_ge(const_in, 16)
                pe.wait_ge(*f.at(b, f"tin{r}"))
                for i in range(2 * T):
                    ins = nc.tensor.transpose(b_front[:, i * P:(i + 1) * P], tin[:, i], ident)
                return ins

            def front0(b, k):
                if k == 5:
                    pe.wait_ge(*act_f1.at(b - 2, "v3"))
                    turn_inputs(b, dve_f0, 0).then_inc(*pe_f0("T0"))
                if k == 7:
                    pe.wait_ge(small_in, 16)
                    pe.wait_ge(*act_f0.at(b, "xfT"))
                    nc.tensor.matmul(b_front[:, 0:S], wq0, xaT[:], start=True, stop=True)
                    nc.tensor.matmul(b_front[:, S:2 * S], wk0, xaT[:], start=True, stop=True).then_inc(*pe_f0("qk0"))
                if k == 10:
                    pe.wait_ge(*dve_f0.at(b, "qsT"))
                    for t in range(T):
                        nc.tensor.matmul(b_front[:, t * P:(t + 1) * P], xaT[:, t * P:(t + 1) * P], wv0, start=True, stop=True)
                    for t in range(T):
                        ins = nc.tensor.transpose(b_front[:, S + t * P:S + (t + 1) * P], keT[:, t * P:(t + 1) * P], ident)
                    ins.then_inc(*pe_f0("vk0"))
                if k == 12:
                    pe.wait_ge(*act_f0.at(b, "vk"))
                    for t in range(T):
                        ins = nc.tensor.matmul(b_front[:, 0:P], vk[:, 0, t], vk[:, 1, t], start=(t == 0), stop=(t == T - 1))
                    ins.then_inc(*pe_f0("ctx"))
                if k == 13:
                    pe.wait_ge(*dve_f0.at(b, "ctxT"))
                    nc.tensor.matmul(b_front[:, 0:D], ctxT[:], wout0, start=True, stop=True).then_inc(*pe_f0("mix"))
                if k == 15:
                    pe.wait_ge(*act_f0.at(b, "mix"))
                    for t in range(T):
                        nc.tensor.matmul(b_front[:, t * D:(t + 1) * D], qsT[:, t * P:(t + 1) * P], mix[:], start=True, stop=False)
                        nc.tensor.matmul(b_front[:, t * D:(t + 1) * D], ones_row, b_out, start=False, stop=True)
                    for t in range(T):
                        ins = nc.tensor.matmul(b_front[:, S + t * E:S + (t + 1) * E], xfT[:, t * P:(t + 1) * P], router0,
                                               start=True, stop=True)
                    ins.then_inc(*pe_f0("out0"))

            def project(ps, t, c):
                tok = slice(t * P, (t + 1) * P)
                return nc.tensor.matmul(ps[:], xaT[:, tok], qkv1[:, c:c + 512], start=True, stop=True)

            def turn_bank_free(b, m):
                if m >= 3:
                    pe.wait_ge(*act_f1.at(b, f"qkT{m - 3}" if m < 11 else "v0"))
                else:
                    pe.wait_ge(*(dve_heads.at(b - 1, f"sim{'AB'[m - 1]}{STEPS - 1}") if m else act_f1.at(b, "proj7")))

            def front1(b, k):
                if k == 21:
                    pe.wait_ge(*dve_f0.at(b + 1, "rt0"))
                    turn_inputs(b, dve_f1, 1).then_inc(*pe_f1("T1"))
                if k == 23:
                    pe.wait_ge(*act_f1.at(b, "xfT1"))
                    for t in range(T):
                        ins = nc.tensor.matmul(b_front[:, t * E:(t + 1) * E], xfT[:, t * P:(t + 1) * P], router1, start=True, stop=True)
                    ins.then_inc(*pe_f1("logit1"))
                if 24 <= k < 32:
                    n = k - 24
                    back = n - (3 if proj_bank(b, 1) is b_sim[0] else 1)
                    pe.wait_ge(*(act_f1.at(b, f"proj{back}") if back >= 0 else dve_f1.at(b, "rt1")))
                    if n == 0:
                        pe.wait_ge(qkv_in, 16)
                    project(proj_bank(b, n), n // 2 % 2, n // 4 * HD1 + n % 2 * 512).then_inc(*pe_f1(f"proj{n}"))
                if 31 <= k < 39:
                    n = k - 31
                    w, t, g = n // 4, n // 2 % 2, n % 2
                    turn_bank_free(b, n)
                    pe.wait_ge(*pool_f1.at(b, f"nrm{n}"))
                    for i in range(4):
                        hp = 4 * g + i
                        ins = nc.tensor.transpose(turn_banks[n % 3][:, i * P:(i + 1) * P], qk[:, w, t, hp * P:(hp + 1) * P], ident)
                    ins.then_inc(*pe_f1(f"qkT{n}"))
                if 38 <= k < 42:
                    n = k - 38
                    turn_bank_free(b, 8 + n)
                    project(turn_banks[(8 + n) % 3], n // 2, 2 * HD1 + n % 2 * 512).then_inc(*pe_f1(f"v{n}"))

            def expert_up(b, layer, e):
                l1, b1, e1 = expert_before(b, layer, e)
                if e == 0:
                    pe.wait_ge(up_lo[layer], 1 if layer else 4)
                    pe.wait_ge(*(pool_f1.at(b, "xfl1") if layer else pool_f0.at(b, "xfl")))
                for name, ps, c, free in (("g", b_gate, 0 if layer else HID, "ga"), ("u", b_up, HID if layer else 0, "hid")):
                    pe.wait_ge(*dve_moe[l1].at(b1, f"{free}{e1}"))
                    for a in range(HB):
                        cs = slice(c + a * P, c + (a + 1) * P)
                        ins = matmul3(ps[:, a * S:(a + 1) * S], up_h[layer][:, e, cs], up_l[layer][:, e, cs],
                                      xf_h[layer][:], xf_l[layer][:])
                    ins.then_inc(*pe_moe[layer](f"{name}{e}"))

            def shared_bank_free(b, steps):
                for p in steps:
                    for half in halves_at(p, 5):
                        pe.wait_ge(*dve_heads.at(b, f"pnT{half}"))
                    for half in halves_at(p, 8):
                        pe.wait_ge(*act_heads.at(b, f"oT{half}"))
                    for half in halves_at(p, 9):
                        pe.wait_ge(*dve_heads.at(b, f"add{half}"))

            def expert_down(b, layer, e, p, h):
                if e == 0:
                    pe.wait_ge((dn0_in, dn1_in)[layer], 16)
                l1, b1, e1 = expert_before(b, layer, e)
                pe.wait_ge(*dve_moe[l1].at(b1, f"y{e1}"))
                if h:
                    shared_bank_free(b - 1 + layer, [p - 1, p])
                pe.wait_ge(*dve_moe[layer].at(b, f"hid{e}"))
                for t in range(T):
                    for a in range(HB):
                        ins = nc.tensor.matmul(b_y[:, t * D:(t + 1) * D], hid[e % 2][:, a, t * P:(t + 1) * P], down[layer][:, e, a],
                                               start=(a == 0), stop=(a == HB - 1), skip_group_check=True)
                ins.then_inc(*pe_moe[layer](f"dn{e}"))

            def outputs(b, p, m0, m1):
                for layer, e in experts_at(p - 1, m0, m1):
                    expert_down(b + 1 - layer, layer, e, p, m1)

            def hidden(b, p, m0, m1):
                for layer, e in experts_at(p, m0, m1):
                    expert_up(b + 1 - layer, layer, e)

            def scores(b, p, m0, m1):
                qt = p // HP
                toks = slice(qt * P, (qt + 1) * P)
                if p < STEPS:
                    hp = p % HP
                    if p % HP == 0:
                        pe.wait_ge(null_dve, 7)
                        if qt:
                            pe.wait_ge(*dve_heads.at(b, f"simA{p - 1}"))
                        else:
                            pe.wait_ge(*dve_heads.at(b - 1, f"simA{STEPS - 1}"))
                            pe.wait_ge(*act_f1.at(b, "v3"))
                        for i in range(HP):
                            ins = nc.tensor.matmul(b_sim[0][:, 4 * i:4 * i + 4], qkT[:, 0, i, toks], nkbd[:, i], start=True, stop=True,
                                                   skip_group_check=True)
                        ins.then_inc(*pe_heads(f"null{qt}"))
                    for i, ab in pair_order(p):
                        ch = slice(i * DH1, (i + 1) * DH1)
                        if p % HP == 0 and i == 0:
                            pe.wait_ge(*dve_heads.at(b, f"sn{qt}"))
                        elif p:
                            pe.wait_ge(*dve_heads.at(b, f"sim{ab}{p - 1}"))
                        else:
                            pe.wait_ge(*dve_heads.at(b - 1, f"sim{ab}{STEPS - 1}"))
                        nc.tensor.matmul(b_sim[i][:, 0:P * (qt + 1)], qkT[ch, 0, hp, toks], qkT[ch, 1, hp, 0:P * (qt + 1)],
                                         start=True, stop=True).then_inc(*pe_heads(f"sim{ab}{p}"))
                if halves_at(p, 5) + halves_at(p, 8) + halves_at(p, 9):
                    shared_bank_free(b, range(p - 3, p))
                    layer, e = [x for q in range(p - 1) for x in experts_at(q, m0, m1)][-1]
                    pe.wait_ge(*dve_moe[layer].at(b + 1 - layer, f"y{e}"))
                for half in halves_at(p, 5):
                    pe.wait_ge(*act_heads.at(b, f"pn{half}"))
                    nc.tensor.transpose(b_y[0:NULL * HALF, D:D + P], pn[:].rearrange("p h j -> p (h j)"), ident)\
                        .then_inc(*pe_heads(f"pnT{half}"))
                for half in halves_at(p, 8):
                    pe.wait_ge(*dve_heads.at(b, f"o{half}"))
                    for i in range(4):
                        ins = nc.tensor.transpose(b_y[:, i * P:(i + 1) * P], o[:, i * P:(i + 1) * P], ident)
                    ins.then_inc(*pe_heads(f"oT{half}"))
                for half in halves_at(p, 9):
                    pe.wait_ge(wout_in, 16)
                    pe.wait_ge(*act_heads.at(b, f"oT{half}"))
                    for i in range(4):
                        ins = nc.tensor.matmul(b_y[:, 0:D], oT[:, i], wout1[:, half % 2 * 4 + i], start=(i == 0), stop=(i == 3))
                    ins.then_inc(*pe_heads(f"op{half}"))

            def values(b, p, m0, m1):
                if 1 <= p <= STEPS:
                    p1 = p - 1
                    nc1 = p1 // HP + 1
                    pe.wait_ge(*(act_heads.at(b, f"prT{p1 - 1}") if p1 else act_heads.at(b - 1, f"prT{STEPS - 1}")))
                    pe.wait_ge(*act_heads.at(b, f"exp{pair_order(p1)[1][1]}{p1}"))
                    for i in range(2):
                        for c in range(nc1):
                            ins = nc.tensor.transpose(b_prT[:, (i * nc1 + c) * P:(i * nc1 + c + 1) * P],
                                                      prb[p1 % 2][:, i, c * P:(c + 1) * P], ident)
                    ins.then_inc(*pe_heads(f"prT{p1}"))
                if 3 <= p < STEPS + 3:
                    p3 = p - 3
                    q3 = p3 // HP
                    if p3 % 4 == 0:
                        pe.wait_ge(*(dve_heads.at(b, f"o{p3 // 4 - 1}") if p3 else dve_heads.at(b - 1, f"o{STEPS // 4 - 1}")))
                    if p3 == 0:
                        pe.wait_ge(*act_f1.at(b, "v3"))
                    pe.wait_ge(*act_heads.at(b, f"prT{p3}"))
                    for i in range(2):
                        h = 2 * (p3 % HP) + i
                        for c in range(q3 + 1):
                            ins = nc.tensor.matmul(b_pv[:, h % HALF * DH1:(h % HALF + 1) * DH1], prT[p3 % 3][:, i, c * P:(c + 1) * P],
                                                   v[:, c, h * DH1:(h + 1) * DH1], start=(p3 % 4 == 0 and i == 0 and c == 0),
                                                   stop=False, skip_group_check=True)
                    ins.then_inc(*pe_heads(f"pv{p3}"))
                for half in halves_at(p, 6):
                    pe.wait_ge(*dve_heads.at(b, f"pnT{half}"))
                    nc.tensor.matmul(b_pv[:], pnT[:], nvbd[:, half % 2], start=False, stop=True, skip_group_check=True)\
                        .then_inc(*pe_heads(f"pvn{half}"))

            for k in range(PIECES):
                front0(0, k)
            pe.wait_ge(null_dve, 4)
            nc.tensor.transpose(b_pv[:, 0:NULL * H1], nkw[:].rearrange("p a d -> p (a d)"), ident[0:NULL * H1, 0:NULL * H1])\
                .then_inc(null_pe, 1)
            all_rounds(pe, (scores, values, outputs, hidden, front0, front1))


def table(widths):
    out, at = {}, 0
    for name, n in widths:
        out[name] = (at, n)
        at += n
    return out, at


SMALL, SMALL_COLS = table([("wq0", P), ("wk0", P), ("wv0", P), ("wout0", D), ("router0", E), ("router1", E), ("b_out", D),
                           ("gamma0", 1), ("beta0", 1), ("rms", 1), ("gamma1", 1), ("qs2", 1), ("ks2", 1)])
CONST, CONST_COLS = table([("ident", P), ("ones", P), ("null_bias", T * NULL * H1), ("head_mask", P), ("iota8", E)])


def constants():
    c = np.zeros((P, CONST_COLS), np.float32)

    def put(name, a):
        at, n = CONST[name]
        c[:, at:at + n] = a

    row = np.arange(P)[:, None]
    put("ident", np.eye(P))
    put("ones", 1.0)
    slope = np.array(slopes(), np.float32)
    gone = np.arange(T)[None, :, None, None] * P + row[:, :, None, None] + NULL - np.arange(NULL)[None, None, None, :]
    put("null_bias", (gone * slope[None, None, :, None]).astype(np.float32).reshape(P, -1))
    put("head_mask", (row // DH0) == (np.arange(P)[None, :] // DH0))
    put("iota8", np.arange(E)[None, :])
    return c


def distances():
    d = P + np.arange(P)[:, None] - np.arange(S)[None, :]
    return np.where(d < 0, np.float32(FAR), d.astype(np.float32))


def kernel(**inputs):
    import numpy as _np
    import concourse.bacc as _bacc
    from concourse import mybir as _mybir
    from concourse.bass_utils import run_bass_kernel_spmd as _run

    a = {k: _np.asarray(v) for k, v in inputs.items()}
    qkv0 = a["L0_attn_w_qkv"]
    parts = {
        "wq0": qkv0[:, 0:P], "wk0": qkv0[:, P:2 * P], "wv0": qkv0[:, 2 * P:3 * P], "wout0": a["L0_attn_w_out"],
        "router0": a["L0_ffn_w_router"].T, "router1": a["L1_ffn_gate_w"].T,
        "b_out": _np.broadcast_to(a["L0_attn_b_out"][None, :], (P, D)),
        "gamma0": a["L0_attn_gamma"].reshape(D, 1), "beta0": a["L0_attn_beta"].reshape(D, 1),
        "rms": a["L0_ffn_norm_scale"].reshape(D, 1), "gamma1": a["L1_attn_gamma"].reshape(D, 1),
        "qs2": _np.concatenate([a["L1_attn_q_scale"]] * 2).reshape(P, 1),
        "ks2": _np.concatenate([a["L1_attn_k_scale"]] * 2).reshape(P, 1),
    }
    null = a["L1_attn_null_kv"].reshape(H1, NULL, 2, DH1)
    null_k = null[:, :, 0].reshape(H1 * NULL, DH1)
    null_v = _np.zeros((HALF, NULL, T, HALF, DH1), null.dtype)
    for h in range(H1):
        null_v[h % HALF, :, h // HALF, h % HALF] = null[h, :, 1]
    arrays = {
        "x": a["L0_attn_x"],
        "w_small": _np.concatenate([parts[n] for n in SMALL], axis=1),
        "w_up0": a["L0_ffn_w_up"].transpose(2, 0, 1).reshape(D, -1),
        "w_dn0": a["L0_ffn_w_down"].reshape(E, D, HB, P).transpose(3, 0, 2, 1).reshape(P, -1),
        "w_qkv1": _np.concatenate([a["L1_attn_w_q"], a["L1_attn_w_kv"]], axis=1),
        "w_out1": a["L1_attn_w_out"].reshape(HP, P, D).transpose(1, 0, 2).reshape(P, -1),
        "w_up1": a["L1_ffn_w13_weight"].transpose(2, 0, 1).reshape(D, -1),
        "w_dn1": a["L1_ffn_w2_weight"].reshape(E, D, HB, P).transpose(3, 0, 2, 1).reshape(P, -1),
        "null_k": _np.concatenate([null_k, null_k], axis=1),
        "null_v": null_v.reshape(HALF * NULL, -1),
        "consts": constants(),
        "distance": distances(),
    }
    arrays = {n: _np.ascontiguousarray(v) for n, v in arrays.items()}
    nc = _bacc.Bacc("TRN2", target_bir_lowering=False, num_devices=1)
    args = [nc.dram_tensor(n, v.shape, _mybir.dt.from_np(v.dtype), kind="ExternalInput").ap() for n, v in arrays.items()]
    args.append(nc.dram_tensor("result", (B, S, D), _mybir.dt.float32, kind="ExternalOutput").ap())
    build(nc, *args)
    r = _run(nc, [arrays], core_ids=[0])
    return r.results[0]["result"]
```

```python
from contextlib import ExitStack

import numpy as np

import concourse.bass as bass
from concourse import mybir

F32 = mybir.dt.float32
F32R = mybir.dt.float32r
U32 = mybir.dt.uint32
ALU = mybir.AluOpType
ACT = mybir.ActivationFunctionType
AX = mybir.AxisListType

P = 128
B, S, D = 8, 256, 128
T = S // P
E = 8
HID = 256
HB = HID // P
H0, DH0 = 4, 32
H1, DH1 = 16, 64
HD1 = H1 * DH1
HP = H1 // 2
NULL = 2
KEYS = NULL + S
SIM_SCALE = 8.0
GROUPS = 4
LN_EPS, RMS_EPS = 1e-5, 1e-6
POOLED = 6
HALF = 8
STEPS = T * HP
ROUND = STEPS + 6
PIECES = 2 * ROUND
ROUTER0 = 34
NULL_PARTS = (0, 32, 64)
NULL_ROWS = 96
FAR = 1e38


def slopes():
    start = 2.0 ** (-2.0 ** (-(np.log2(H1) - 3.0)))
    return [float(np.float32(start * start ** i)) for i in range(H1)]


class Progress:

    def __init__(self, sem, names):
        self.sem, self.names, self.per = sem, list(names), len(names)
        self.index = {n: i + 1 for i, n in enumerate(self.names)}
        self.next = 0

    def __call__(self, name):
        assert self.names[self.next % self.per] == name, (name, self.names[self.next % self.per])
        self.next += 1
        return self.sem, 1

    def at(self, b, name):
        if isinstance(b, int):
            b = min(b, B - 1)
        return self.sem, b * self.per + (2 * self.per + self.index[name])


def experts_at(p, m0, m1):
    first = range(E) if m0 else []
    second = [9, 10, 11, 13, 14, 16, 18, 20] if m0 else [1, 2, 3, 5, 6, 8, 10, 12]
    out = [(0, p)] if p in first else []
    return out + [(1, second.index(p))] if m1 and p in second else out


def pooled(layer, e):
    return layer == 0 and e < POOLED


def moe_order(layer, at, after, last=(), skip=lambda name, e: False):
    out = []
    for p in range(ROUND):
        for q, names in ((p, at), (p - 1, after), (p, last)):
            out += [f"{n}{e}" for l, e in experts_at(q, True, True) if l == layer for n in names if not skip(n, e)]
    return out


def build(nc, x, w_small, w_up0, w_dn0, w_qk1, w_v1, w_out1, w_up1, w_dn1, null_k, null_v, consts, distance, out):
    ctx = ExitStack()
    with ctx:
        def sb(name, shape, dt=F32):
            return ctx.enter_context(nc.sbuf_tensor(name, shape, dt))

        def bank(name):
            return ctx.enter_context(nc.psum_tensor(name, [P, 512], F32))

        def sem(name):
            return ctx.enter_context(nc.semaphore(name))

        def progress(name, names):
            return Progress(sem(name), names)

        small = sb("small", [P, SMALL_COLS])
        cst = sb("cst", [P, CONST_COLS])
        up_h = [sb(f"up_h{i}", [P, E, 2 * HID], F32R) for i in range(2)]
        up_l = [sb(f"up_l{i}", [P, E, 2 * HID], F32R) for i in range(2)]
        down = [sb(f"down{i}", [P, E, HB, D]) for i in range(2)]
        wqk_h, wqk_l = (sb(f"wqk_{n}", [P, 2 * HD1], F32R) for n in "hl")
        wv1 = sb("wv1", [P, HD1])
        wout1 = sb("wout1", [P, HP, D])
        bias = sb("bias", [P, H1, KEYS])
        nkw = sb("nkw", [NULL * H1, 2, DH1])
        nk_ss = sb("nk_ss", [NULL * H1, 4])
        nvbd = sb("nvbd", [NULL_ROWS, T, HALF * DH1], F32R)
        warm = sb("warm", [P, 1])
        qscale = sb("qscale", [P, 1])
        halves = sb("halves", [P, HALF])

        def cols(tile, table, name):
            at, n = table[name]
            return tile[:, at:at + n]

        ident = cols(cst, CONST, "ident")
        head_mask = cols(cst, CONST, "head_mask")
        iota8 = cols(cst, CONST, "iota8")
        wq0, wk0, wv0 = (cols(small, SMALL, n) for n in ("wq0", "wk0", "wv0"))
        wout0, router0, router1 = (cols(small, SMALL, n) for n in ("wout0", "router0", "router1"))
        gamma0, beta0, rms_scale, gamma1 = (cols(small, SMALL, n) for n in ("gamma0", "beta0", "rms", "gamma1"))
        qs2, ks2 = (cols(small, SMALL, n) for n in ("qs2", "ks2"))
        b_out = cols(small, SMALL, "b_out")[0:1]
        ones_row = cols(cst, CONST, "ones")[0:1]

        x_in = sb("x_in", [P, T, D])
        xn = sb("xn", [P, T, D])
        tin = sb("tin", [P, 2 * T, D])
        stats = [sb(f"stats{i}", [P, T, 6]) for i in range(4)]
        mv = [sb(f"mv{i}", [P, T, 2]) for i in range(4)]
        var = [sb(f"var{i}", [P, 2 * T]) for i in range(4)]
        rstd = [sb(f"rstd{i}", [P, 2 * T]) for i in range(4)]
        start0 = sb("start0", [P, T, D])
        acc0 = sb("acc0", [P, T, D])
        start1 = sb("start1", [P, T, D])
        acc1 = sb("acc1", [P, T, D])
        xaT = sb("xaT", [P, S])
        xfT = sb("xfT", [P, S])
        xf_h = [sb(f"xf_h{i}", [P, S], F32R) for i in range(2)]
        xf_l = [sb(f"xf_l{i}", [P, S], F32R) for i in range(2)]
        nkmax = sb("nkmax", [P, 1])
        ksum = sb("ksum", [P, 2])
        keT = xn[:].rearrange("p t d -> p (t d)")
        qsT = sb("qsT", [P, S])
        xa_h, xa_l = (sb(f"xa_{n}", [P, S], F32R) for n in "hl")
        vk = tin[:].rearrange("p (a t) c -> p a t c", t=T)
        ctxT = sb("ctxT", [P, P])
        mix = sb("mix", [P, D])
        rt = [sb(f"rt{i}", [P, T, E]) for i in range(2)]
        prob = sb("prob", [P, T, E])
        gpad = sb("gpad", [P, T, E])
        gtop = sb("gtop", [P, T, E])
        gidx = sb("gidx", [P, T, E], U32)
        gidxf = sb("gidxf", [P, T, 2])
        gmask = sb("gmask", [P, T, 2, GROUPS])
        masked = sb("masked", [P, T, E])
        top = [sb(f"top{i}", [P, T, E]) for i in range(2)]
        topi = [sb(f"topi{i}", [P, T, E], U32) for i in range(2)]
        topf = [sb(f"topf{i}", [P, T, 2]) for i in range(2)]
        tw = [sb(f"tw{i}", [P, 8, T]) for i in range(2)]
        one = [sb(f"one{i}", [P, 2, T, E]) for i in range(2)]
        cw = [sb(f"cw{i}", [P, T, E]) for i in range(2)]
        qk = sb("qk", [P, 2, T, HD1])
        sq = tin[:].rearrange("p t d -> p (t d)")
        ss = sb("ss", [P, 2, T, H1])
        rn = sb("rn", [P, 2, T, H1])
        qkT = sb("qkT", [P, HP * (S + KEYS)])
        qT = qkT[:, 0:HP * S].rearrange("p (h n) -> p h n", h=HP)
        kT = qkT[:, HP * S:].rearrange("p (h n) -> p h n", h=HP)
        v = sb("v", [P, T, HD1])
        th = [sb(f"th{i}", [P, HB * S]) for i in range(2)]
        yw = sb("yw", [P, T, D])
        mneg = sb("mneg", [P, T, H1])
        lsum = sb("lsum", [P, T, H1])
        rl = sb("rl", [P, T, H1])
        prb = [sb(f"prb{i}", [P, 2, KEYS]) for i in range(2)]
        prT = [sb(f"prT{i}", [P, 2, S]) for i in range(3)]
        pn3 = sb("pn3", [P, NULL_ROWS], F32R)
        pnT = sb("pnT", [NULL_ROWS, P], F32R)
        oT = sb("oT", [P, 4, P])

        raw_up = [qkT[:, 0:E * 2 * HID], qk[:].rearrange("p a b c -> p (a b c)")]
        dist = prb[0][:, 0]

        raw_qk = qkT[:, 0:2 * HD1]

        def quarter(t, c):
            flat = t if len(t.shape) == 2 else t[:].rearrange("p e n -> p (e n)")
            n = E * 2 * HID // 4
            return flat[:, c * n:(c + 1) * n]

        raw_nv = v[0:NULL_ROWS].rearrange("p t (a n) -> p (t a) n", a=2)[:, 0:T]
        nk_sq = prT[0][0:NULL * H1, 0, 0:2 * DH1].rearrange("p (a d) -> p a d", a=2)

        b_gate, b_up, b_y = bank("b_gate"), bank("b_up"), bank("b_y")
        b_sim = [bank("b_simA"), bank("b_simB")]
        b_prT, b_pv, b_front = bank("b_prT"), bank("b_pv"), bank("b_front")

        def proj_bank(b, n):
            return turn_banks[n % 3] if isinstance(b, int) and b == 0 else b_front

        turn_banks = [b_front, *b_sim]

        def turn_bank(name):
            return turn_banks[TURNS.index(name) % 3]


        small_in, const_in, up0_in, dn0_in = (sem(n) for n in ("small_in", "const_in", "up0_in", "dn0_in"))
        wqk_in, wv_in, wout_in, up1_in, dn1_in, null_in, dist_in = (sem(n) for n in ("wqk_in", "wv_in", "wout_in", "up1_in", "dn1_in", "null_in", "dist_in"))
        half_set, warm_set = sem("half_set"), sem("warm_set")
        pad_set = sem("pad_set")
        bias_set = sem("bias_set")
        qscale_set = sem("qscale_set")
        up_hi, up_lo = [sem(f"up_hi{i}") for i in range(2)], [sem(f"up_lo{i}") for i in range(2)]
        wqk_hi, wqk_lo = sem("wqk_hi"), sem("wqk_lo")
        null_dve, null_pool, null_pe = sem("null_dve"), sem("null_pool"), sem("null_pe")
        nv_in, nv_zero, nv_high, nv_set = (sem(n) for n in ("nv_in", "nv_zero", "nv_high", "nv_set"))

        x_loaded, out_stored = sem("x_loaded"), sem("out_stored")
        dve_met, pool_met = sem("dve_met"), sem("pool_met")
        QKT = [f"qkT{n}" for n in range(8)]
        PROJ = [f"proj{n}" for n in range(8)]
        TURNS = QKT[:4] + [x for n in range(4) for x in (f"qkT{n + 4}", f"v{n}")]
        SS = lambda n: [f"ss{n}", f"floor{n}"]
        LN = lambda r: [f"stats{r}", f"aggr{r}"]
        TOP = lambda r: [f"{n}{r}" for n in ("max", "idx", "idxf")]
        pe_f0 = progress("pe_f0", ["T0", "qk0", "vk0", "ctx", "mix", "out0"])
        act_f0 = progress("act_f0", ["xaT", "xfT", "kexp", "vk", "mix", "xfh", "topexp"])
        pool_f0 = progress("pool_f0", ["var0", "rstd0", "var1", "rstd1", "msq", "ms", "mse", "rstds", "x_xn", "start0", "xfl"])
        dve_f0 = progress("dve_f0", LN(0) + ["xn0"] + LN(1) + ["tin0", "nkmax", "rksum", "qsT", "ctxT",
                                                               "out0", "rt0"] + TOP(0)
                          + ["gap", "den0", "w1_0", "w2_0", "w1h", "w2h", "one0", "cw0"])
        pe_f1 = progress("pe_f1", ["T1", "logit1"] + PROJ + TURNS)
        act_f1 = progress("act_f1", ["xaT1", "xfT1", "xa_h", "rexp0", "rexp1"] + [x for n in range(8) for x in (f"proj{n}", f"sq{n}")] + TURNS + ["xfh1"])
        pool_f1 = progress("pool_f1", ["var2", "rstd2", "var3", "rstd3", "start1"] + [f"rn{n}" for n in range(8)] + ["xfl1"])
        unit = progress("unit", [f"nrm{n}" for n in range(8)])
        dve_f1 = progress("dve_f1", LN(2) + ["xn1"] + LN(3) + ["tin1", "xa_l", "rt1", "nrmax"]
                          + [x for n in range(8) for x in SS(n)]
                          + ["rsum", "prob", "group", "gmax", "gidx", "gidxf", "gone", "gmask", "masked"] + TOP(1)
                          + ["den1", "rden", "rdenh", "tw1", "one1", "cw1"])
        pe_moe = [progress(f"pe_moe{i}", moe_order(i, ["g"], ["dn"], ["u"])) for i in range(2)]
        act_moe = [progress(f"act_moe{i}", moe_order(i, ["th"], ["yw"], skip=lambda n, e: n == "yw" and not pooled(i, e)))
                   for i in range(2)]
        pool_moe = progress("pool_moe", [f"y{e}" for e in range(E) if pooled(0, e)])
        dve_moe = [progress(f"dve_moe{i}", moe_order(i, ["ga"], ["y"], ["hid"], lambda n, e: n == "y" and pooled(i, e)))
                   for i in range(2)]

        def taken(b, layer, e):
            return act_moe[0].at(b, f"yw{e}") if pooled(layer, e) else dve_moe[layer].at(b, f"y{e}")

        def added(b, layer, e):
            return pool_moe.at(b, f"y{e}") if pooled(layer, e) else dve_moe[layer].at(b, f"y{e}")

        def piece_of(n):
            return n // 4, n // 2 % 2, n % 2

        def unit_vectors(engine, n):
            w, t, g = piece_of(n)
            part = qk[:, w, t, g * 512:g * 512 + 512].rearrange("p (h d) -> p h d", h=HALF)
            norms = rn[:, w, t, g * HALF:(g + 1) * HALF]
            engine.tensor_tensor(part, part, norms.unsqueeze(2).to_broadcast([P, HALF, DH1]), ALU.mult)\
                .then_inc(*unit(f"nrm{n}"))

        def expert_before(b, layer, e):
            if e:
                return layer, b, e - 1
            return (0, b + 1, E - 1) if layer else (1, b - 2, E - 1)

        def head_order(per_step):
            return [n for p in range(ROUND) for n in per_step(p)]

        def halves_at(p, late):
            return [(p - late) // 4] if p >= late and (p - late) % 4 == 0 and (p - late) // 4 < STEPS // 4 else []

        def pe_head_steps(p):
            out = [f"pnT{h}" for h in halves_at(p, 6)] + [f"op{h}" for h in halves_at(p, 8)]
            if p < STEPS:
                out += [f"simA{p}", f"simB{p}"]
            out += [f"prT{p - 1}"] * (1 <= p <= STEPS)
            out += [f"pv{p - 3}"] * (3 <= p < STEPS + 3)
            return out + [f"pvn{h}" for h in halves_at(p, 6)]

        def dve_head_steps(p):
            out = [f"add{h}" for h in halves_at(p, 8)] + [f"pnT{h}" for h in halves_at(p, 6)]
            if 1 <= p <= STEPS:
                out += [f"norm{p - 1}"]
            if p < STEPS:
                out += [f"simA{p}", f"simB{p}", f"rl{p}"]
            return out

        def act_head_steps(p):
            out = [f"oT{h}" for h in halves_at(p, 7)]
            out += [f"exp{ab}{p}" for ab in "AB"] if p < STEPS else []
            return out + [f"prT{p - 1}"] * (1 <= p <= STEPS)

        pe_heads = progress("pe_heads", head_order(pe_head_steps))
        dve_heads = progress("dve_heads", head_order(dve_head_steps))
        act_heads = progress("act_heads", head_order(act_head_steps))
        pool_heads = progress("pool_heads", [f"{n}{p}" for p in range(STEPS) for n in ("pnh", "pnl")])

        def in_round(b, steps, m0=True, m1=True, f0=True, f1=True, h=True):
            for p in range(ROUND):
                for step in steps:
                    step(b, p, m0, m1, f0, f1, h)

        def heads(step):
            return lambda b, p, m0, m1, f0, f1, h: step(b, p, m0, m1) if h else None

        def experts(step):
            return lambda b, p, m0, m1, f0, f1, h: step(b, p, m0, m1)

        def fronts(front0, front1):
            def piece(i):
                def run(b, p, m0, m1, f0, f1, h):
                    if f0:
                        front0(b + 2, 2 * p + i)
                    if f1:
                        front1(b + 1, 2 * p + i)
                return run
            return piece(0), piece(1)

        def all_rounds(engine, *steps):
            in_round(-1, steps, m1=False, h=False)
            with engine.Fori(0, B - 2) as b:
                in_round(b, steps)
            in_round(B - 2, steps, f0=False)
            in_round(B - 1, steps, m0=False, f0=False, f1=False)

        block = ctx.enter_context(nc.Block())

        @block.sync
        def _(sp):
            sp.sem_inc(x_loaded, 16)
            sp.sem_inc(out_stored, 16)

            def load_x(b):
                sp.wait_ge(*pool_f0.at(b - 1, "start0"))
                sp.dma_start(x_in[:], x[b].rearrange("(t p) d -> p t d", p=P)).then_inc(x_loaded, 16)

            def store(b):
                sp.wait_ge(*dve_heads.at(b, f"add{STEPS // 4 - 1}"))
                sp.wait_ge(*dve_moe[1].at(b, f"y{E - 1}"))
                sp.dma_start(out[b].rearrange("(t p) d -> p t d", p=P), acc1[:]).then_inc(out_stored, 16)

            load_x(0)
            sp.dma_start(cst[:], consts).then_inc(const_in, 16)
            sp.dma_start(small[:], w_small).then_inc(small_in, 16)
            sp.dma_start(raw_up[0], w_up0).then_inc(up0_in, 16)
            sp.dma_start(down[0][:].rearrange("p e a c -> p (e a c)"), w_dn0).then_inc(dn0_in, 16)
            sp.dma_start(dist, distance).then_inc(dist_in, 16)
            sp.dma_start(nkw[:].rearrange("p a d -> p (a d)"), null_k).then_inc(null_in, 16)
            for row in NULL_PARTS:
                sp.dma_start(raw_nv[row:row + NULL * HALF].rearrange("p a d -> p (a d)"), null_v).then_inc(nv_in, 16)
            sp.dma_start(raw_up[1], w_up1).then_inc(up1_in, 16)
            sp.dma_start(wv1[:], w_v1).then_inc(wv_in, 16)
            sp.dma_start(wout1[:].rearrange("p h c -> p (h c)"), w_out1).then_inc(wout_in, 16)
            sp.dma_start(down[1][:].rearrange("p e a c -> p (e a c)"), w_dn1).then_inc(dn1_in, 16)
            load_x(1)
            sp.wait_ge(up_hi[0], 4)
            sp.wait_ge(up_lo[0], 4)
            sp.dma_start(raw_qk, w_qk1).then_inc(wqk_in, 16)
            with sp.Fori(0, B - 2) as b:
                load_x(b + 2)
                store(b)
            store(B - 2)
            store(B - 1)
            sp.wait_ge(out_stored, 16 * (B + 1))

        @block.gpsimd
        def _(pool):
            for prog in (pool_f0, pool_f1, unit, pool_moe, pool_heads):
                pool.sem_inc(prog.sem, 2 * prog.per)
            nc.gpsimd.memset(halves[:], -0.5).then_inc(half_set, 1)
            nc.gpsimd.memset(nvbd[:].bitcast(F32), 0.0).then_inc(nv_zero, 1)
            nc.gpsimd.memset(pn3[:].bitcast(F32), 0.0).then_inc(nv_zero, 1)

            def inverse_std(b, stats, f, r, eps=LN_EPS):
                pool.wait_ge(*stats.at(b, f"aggr{r}"))
                pool.sem_inc(pool_met, 1)
                nc.gpsimd.tensor_scalar(var[r][:, 0:T], mv[r][:, :, 1], eps, None, ALU.add).then_inc(*f(f"var{r}"))
                pool.wait_ge(*f.at(b, f"var{r}"))
                nc.gpsimd.tensor_tensor(rstd[r][:, 0:T], var[r][:, 0:T], halves[:, 0:T], ALU.pow).then_inc(*f(f"rstd{r}"))

            def front0(b, k):
                if k == 0:
                    pool.wait_ge(half_set, 1)
                    inverse_std(b, dve_f0, pool_f0, 0)
                if k == 5:
                    inverse_std(b, dve_f0, pool_f0, 1)
                    squares = var[1][:, T:2 * T]
                    nc.gpsimd.tensor_tensor(squares, mv[1][:, :, 0], mv[1][:, :, 0], ALU.mult).then_inc(*pool_f0("msq"))
                    pool.wait_ge(*pool_f0.at(b, "msq"))
                    nc.gpsimd.tensor_tensor(squares, squares, mv[1][:, :, 1], ALU.add).then_inc(*pool_f0("ms"))
                    pool.wait_ge(*pool_f0.at(b, "ms"))
                    pool.sem_inc(pool_met, 1)
                    nc.gpsimd.tensor_scalar(squares, squares, RMS_EPS, None, ALU.add).then_inc(*pool_f0("mse"))
                    pool.wait_ge(*pool_f0.at(b, "mse"))
                    nc.gpsimd.tensor_tensor(rstd[1][:, T:2 * T], squares, halves[:, 0:T], ALU.pow).then_inc(*pool_f0("rstds"))
                if k == 7:
                    pool.wait_ge(*added(b - 1, 0, 0))
                    pool.sem_inc(pool_met, 1)
                    nc.gpsimd.tensor_tensor(start0[:], x_in[:], xn[:], ALU.add).then_inc(*pool_f0("x_xn"))
                    pool.wait_ge(*pool_f0.at(b, "x_xn"))
                    nc.gpsimd.tensor_tensor(start0[:], start0[:], xn[:], ALU.add).then_inc(*pool_f0("start0"))
                if k == 18:
                    pool.wait_ge(*act_f0.at(b, "xfh"))
                    pool.wait_ge(*pe_moe[0].at(b - 1, f"u{E - 1}"))
                    nc.gpsimd.tensor_tensor(xf_l[0][:], xfT[:], xf_h[0][:].bitcast(F32), ALU.subtract)\
                        .then_inc(*pool_f0("xfl"))

            def front1(b, k):
                if k in (17, 20):
                    r = 2 if k == 17 else 3
                    inverse_std(b, dve_f1, pool_f1, r)
                if k == 24:
                    pool.wait_ge(*dve_moe[0].at(b, f"y{E - 1}"))
                    pool.wait_ge(*dve_moe[1].at(b - 1, "y0"))
                    pool.wait_ge(*dve_heads.at(b - 1, "add0"))
                    pool.sem_inc(pool_met, 1)
                    nc.gpsimd.tensor_copy(start1[:], acc0[:]).then_inc(*pool_f1("start1"))
                if 28 <= k < 36:
                    n = k - 28
                    w, t, g = piece_of(n)
                    hs = slice(g * HALF, (g + 1) * HALF)
                    pool.wait_ge(*dve_f1.at(b, f"floor{n}"))
                    nc.gpsimd.tensor_tensor(rn[:, w, t, hs], ss[:, w, t, hs], halves[:, 0:HALF], ALU.pow).then_inc(*pool_f1(f"rn{n}"))
                    if not (isinstance(b, int) and b == 0):
                        pool.wait_ge(*pool_f1.at(b, f"rn{n}"))
                        unit_vectors(nc.gpsimd, n)
                if k in (10, 12) and isinstance(b, int) and b == 0:
                    n = k // 2 - 5
                    c = slice(n * HD1, (n + 1) * HD1)
                    pool.wait_ge(wqk_hi, n + 1)
                    nc.gpsimd.tensor_tensor(wqk_l[:, c], raw_qk[:, c], wqk_h[:, c].bitcast(F32), ALU.subtract).then_inc(wqk_lo, 1)
                if k == 22 and isinstance(b, int) and b == 0:
                    pool.wait_ge(nv_high, 3)
                    pool.wait_ge(*pool_f1.at(b, "rstd3"))
                    low = slice(NULL_PARTS[2], NULL_PARTS[2] + NULL * HALF)
                    nc.gpsimd.tensor_tensor(nvbd[low], raw_nv[low], nvbd[low].bitcast(F32), ALU.subtract).then_inc(nv_set, 1)
                    pool.wait_ge(nv_set, 1)
                if k == PIECES - 1:
                    pool.wait_ge(*act_f1.at(b, "xfh1"))
                    pool.wait_ge(*pe_moe[1].at(b - 1, f"u{E - 1}"))
                    nc.gpsimd.tensor_tensor(xf_l[1][:], xfT[:], xf_h[1][:].bitcast(F32), ALU.subtract)\
                        .then_inc(*pool_f1("xfl1"))

            def outputs(b, p, m0, m1):
                for _, e in [x for x in experts_at(p - 1, m0, m1) if pooled(*x)]:
                    pool.wait_ge(*act_moe[0].at(b + 1, f"yw{e}"))
                    if e == 0:
                        pool.wait_ge(*dve_f0.at(b + 1, "out0"))
                        pool.wait_ge(*dve_f1.at(b, "xn1"))
                        pool.wait_ge(*pool_f1.at(b, "start1"))
                    else:
                        pool.wait_ge(*pool_moe.at(b + 1, f"y{e - 1}"))
                    pool.sem_inc(pool_met, 1)
                    nc.gpsimd.tensor_tensor(acc0[:], yw[:], (acc0 if e else start0)[:], ALU.add).then_inc(*pool_moe(f"y{e}"))

            def scores(b, p, m0, m1):
                if 1 <= p <= STEPS:
                    p1 = p - 1
                    if p1 >= 4 and p1 % 4 == 0:
                        pool.wait_ge(*pe_heads.at(b, f"pnT{p1 // 4 - 1}"))
                    if p1 == 0:
                        pool.wait_ge(nv_zero, 2)
                        pool.wait_ge(*pe_heads.at(b - 1, f"pnT{STEPS // 4 - 1}"))
                    pool.wait_ge(*dve_heads.at(b, f"norm{p1}"))
                    pool.sem_inc(pool_met, 1)
                    at = p1 % 4 * 2 * NULL
                    null = prb[p1 % 2][:, :, 0:NULL]
                    part = pn3[:].rearrange("p (g c) -> p g c", c=32)[:, :, at:at + 2 * NULL].rearrange("p g (i j) -> p g i j", i=2)
                    for g in (0, 2):
                        ins = nc.gpsimd.tensor_copy(part[:, g], null)
                    ins.then_inc(*pool_heads(f"pnh{p1}"))
                    pool.wait_ge(*pool_heads.at(b, f"pnh{p1}"))
                    nc.gpsimd.tensor_tensor(part[:, 1], null, part[:, 0].bitcast(F32), ALU.subtract).then_inc(*pool_heads(f"pnl{p1}"))

            for k in range(8):
                front0(0, k)
            pool.wait_ge(null_dve, 3)
            nc.gpsimd.tensor_tensor(nk_ss[:, 2:4], nk_ss[:, 0:2], halves[0:NULL * H1, 0:2], ALU.pow).then_inc(null_pool, 1)
            for k in range(8, PIECES):
                front0(0, k)
            front = fronts(front0, front1)
            all_rounds(pool, heads(scores), front[0], experts(outputs), front[1])

        @block.scalar
        def _(act):
            for prog in (act_f0, act_f1, *act_moe, act_heads):
                act.sem_inc(prog.sem, 2 * prog.per)

            act.wait_ge(half_set, 1)
            nc.scalar.activation(warm[:], halves[:, 0:1], ACT.Exp).then_inc(warm_set, 1)

            def front0(b, k):
                if k == 9:
                    act.wait_ge(small_in, 16)
                    act.wait_ge(*pe_f1.at(b - 2, "v3"))
                    act.wait_ge(*pe_f0.at(b, "T0"))
                    nc.scalar.activation(xaT[:], b_front[:, 0:S], ACT.Identity, bias=beta0, scale=gamma0)\
                        .then_inc(*act_f0("xaT"))
                    act.wait_ge(*pool_f1.at(b - 2, "xfl1"))
                    nc.scalar.activation(xfT[:], b_front[:, S:2 * S], ACT.Copy, scale=rms_scale).then_inc(*act_f0("xfT"))
                if k == 12:
                    act.wait_ge(*dve_f0.at(b, "nkmax"))
                    act.wait_ge(*pool_f0.at(b, "start0"))
                    nc.scalar.activation(keT, b_front[:, S:2 * S], ACT.Exp, bias=nkmax[:], accum_out=ksum[:, 0:1])\
                        .then_inc(*act_f0("kexp"))
                if k == 14:
                    act.wait_ge(*pe_f0.at(b, "vk0"))
                    nc.scalar.activation(tin[:].rearrange("p t d -> p (t d)"), b_front[:], ACT.Copy).then_inc(*act_f0("vk"))
                if k == 16:
                    act.wait_ge(*pe_f0.at(b, "mix"))
                    nc.scalar.activation(mix[:], b_front[:, 0:D], ACT.Copy).then_inc(*act_f0("mix"))
                if k == 36:
                    act.wait_ge(*dve_f0.at(b, "gap"))
                    nc.scalar.activation(tw[0][:, 1], tw[0][:, 0], ACT.Exp).then_inc(*act_f0("topexp"))
                if k == 17:
                    act.wait_ge(*pe_moe[0].at(b - 1, f"u{E - 1}"))
                    act.wait_ge(*act_f0.at(b, "xfT"))
                    nc.scalar.activation(xf_h[0][:], xfT[:], ACT.Copy).then_inc(*act_f0("xfh"))

            def front1(b, k):
                if k == 24:
                    act.wait_ge(*pe_f0.at(b + 1, "out0"))
                    act.wait_ge(*pool_f0.at(b + 1, "xfl"))
                    act.wait_ge(*pe_f1.at(b, "T1"))
                    nc.scalar.activation(xaT[:], b_front[:, 0:S], ACT.Copy, scale=gamma1).then_inc(*act_f1("xaT1"))
                    nc.scalar.activation(xfT[:], b_front[:, S:2 * S], ACT.Copy).then_inc(*act_f1("xfT1"))
                    act.wait_ge(*act_f1.at(b, "xaT1"))
                    nc.scalar.activation(xa_h[:], xaT[:], ACT.Copy).then_inc(*act_f1("xa_h"))
                if k == 25:
                    act.wait_ge(*dve_f1.at(b, "nrmax"))
                    for t in range(T):
                        nc.scalar.activation(prob[:, t], rt[1][:, t], ACT.Exp, bias=tw[1][:, 0, t:t + 1],
                                             accum_out=tw[1][:, 1, t:t + 1]).then_inc(*act_f1(f"rexp{t}"))
                if k in (2, 4) and isinstance(b, int) and b == 0:
                    act.wait_ge(wqk_in, 16)
                    c = slice((k // 2 - 1) * HD1, k // 2 * HD1)
                    nc.scalar.activation(wqk_h[:, c], raw_qk[:, c], ACT.Copy).then_inc(wqk_hi, 1)
                if k == 19 and isinstance(b, int) and b == 0:
                    biases(range(6, H1))
                    act.wait_ge(nv_in, 48)
                    act.wait_ge(nv_zero, 1)
                    for row in NULL_PARTS:
                        rows = slice(row, row + NULL * HALF)
                        nc.scalar.activation(nvbd[rows], raw_nv[rows], ACT.Copy).then_inc(nv_high, 1)
                if 26 <= k < 34:
                    n = k - 26
                    act.wait_ge(*pe_f1.at(b, f"proj{n}"))
                    if n == 0:
                        act.wait_ge(up_lo[1], 4)
                        act.wait_ge(*pe_f1.at(b - 1, "qkT7"))
                    part = qk[:, n // 4, n // 2 % 2, n % 2 * 512:n % 2 * 512 + 512]
                    nc.scalar.activation(part, proj_bank(b, n)[:], ACT.Copy).then_inc(*act_f1(f"proj{n}"))
                    act.wait_ge(*act_f1.at(b, f"proj{n}"))
                    act.wait_ge(*(dve_f1.at(b, f"ss{n - 1}") if n else dve_f1.at(b - 1, "ss7")))
                    nc.scalar.activation(sq, part, ACT.Square).then_inc(*act_f1(f"sq{n}"))
                if 34 <= k < 42:
                    n = k - 34
                    w, t, g = n // 4, n // 2 % 2, n % 2
                    act.wait_ge(*pe_f1.at(b, f"qkT{n}"))
                    if n == 0:
                        act.wait_ge(qscale_set, 2)
                        act.wait_ge(wqk_lo, 2)
                        act.wait_ge(*pe_heads.at(b - 1, f"simB{STEPS - 1}"))
                    dst = kT[:, 4 * g:4 * g + 4, NULL + t * P:NULL + (t + 1) * P] if w else qT[:, 4 * g:4 * g + 4, t * P:(t + 1) * P]
                    nc.scalar.activation(dst,
                                         turn_bank(f"qkT{n}")[:].rearrange("p (h q) -> p h q", h=4), ACT.Copy,
                                         **({} if w else {"scale": qscale[:]})).then_inc(*act_f1(f"qkT{n}"))
                if 38 <= k < 42:
                    n = k - 38
                    act.wait_ge(*pe_f1.at(b, f"v{n}"))
                    if n == 0:
                        act.wait_ge(nv_set, 1)
                        act.wait_ge(*pe_heads.at(b - 1, f"pv{STEPS - 1}"))
                    nc.scalar.activation(v[:, n // 2, n % 2 * 512:n % 2 * 512 + 512], turn_bank(f"v{n}")[:], ACT.Copy)\
                        .then_inc(*act_f1(f"v{n}"))
                if k == PIECES - 1:
                    act.wait_ge(*act_f1.at(b, "xfT1"))
                    act.wait_ge(*pe_moe[1].at(b - 1, f"u{E - 1}"))
                    nc.scalar.activation(xf_h[1][:], xfT[:], ACT.Copy).then_inc(*act_f1("xfh1"))

            def tanh(b, p, m0, m1):
                for half in halves_at(p, 7) if m1 else []:
                    act.wait_ge(*(pe_heads.at(b, f"op{half - 1}") if half else pe_heads.at(b - 1, f"op{STEPS // 4 - 1}")))
                    act.wait_ge(*pe_heads.at(b, f"pvn{half}"))
                    nc.scalar.activation(oT[:].rearrange("p a q -> p (a q)"), b_pv[:], ACT.Copy)\
                        .then_inc(*act_heads(f"oT{half}"))
                for layer, e in experts_at(p, m0, m1):
                    act.wait_ge(*pe_moe[layer].at(b + 1 - layer, f"g{e}"))
                    if e < 2:
                        l1, b1, e1 = expert_before(b + 1 - layer, layer, 0)
                        act.wait_ge(*pe_moe[l1].at(b1, f"dn{E - 2 + e}"))
                    else:
                        act.wait_ge(*pe_moe[layer].at(b + 1 - layer, f"dn{e - 2}"))
                    nc.scalar.activation(th[e % 2][:], b_gate[:], ACT.Tanh, scale=0.5).then_inc(*act_moe[layer](f"th{e}"))
                if p == 0 and isinstance(b, int) and b == -1:
                    for k in range(ROUTER0, PIECES):
                        front0(0, k)

            def outputs(b, p, m0, m1):
                for _, e in [x for x in experts_at(p - 1, m0, m1) if pooled(*x)]:
                    act.wait_ge(*pe_moe[0].at(b + 1, f"dn{e}"))
                    if e == 0:
                        act.wait_ge(*dve_f0.at(b + 1, "cw0"))
                    act.wait_ge(*(pool_moe.at(b + 1, f"y{e - 1}") if e else pool_moe.at(b, f"y{POOLED - 1}")))
                    for t in range(T):
                        ins = nc.scalar.activation(yw[:, t], b_y[:, t * D:(t + 1) * D], ACT.Copy, scale=cw[0][:, t, e:e + 1])
                    ins.then_inc(*act_moe[0](f"yw{e}"))

            def scores(b, p, m0, m1):
                qt = p // HP
                n = NULL + P * (qt + 1)
                if p < STEPS:
                    for i, ab in enumerate("AB"):
                        h = 2 * (p % HP) + i
                        act.wait_ge(*dve_heads.at(b, f"sim{ab}{p}"))
                        nc.scalar.activation(prb[p % 2][:, i, 0:n], prb[p % 2][:, i, 0:n], ACT.Exp, scale=-1.0,
                                             bias=mneg[:, qt, h:h + 1], accum_out=lsum[:, qt, h:h + 1])\
                            .then_inc(*act_heads(f"exp{ab}{p}"))

            def values(b, p, m0, m1):
                if 1 <= p <= STEPS:
                    p1 = p - 1
                    n1 = P * (p1 // HP + 1)
                    act.wait_ge(*pe_heads.at(b, f"prT{p1}"))
                    if p1 >= 3:
                        act.wait_ge(*pe_heads.at(b, f"pv{p1 - 3}"))
                    nc.scalar.activation(prT[p1 % 3][:, :, 0:n1], b_prT[:, 0:2 * n1].rearrange("p (a n) -> p a n", a=2),
                                         ACT.Copy).then_inc(*act_heads(f"prT{p1}"))

            def split_up0(parts):
                act.wait_ge(up0_in, 16)
                for c in parts:
                    nc.scalar.activation(quarter(up_h[0], c), quarter(raw_up[0], c), ACT.Copy).then_inc(up_hi[0], 1)

            def biases(heads):
                act.wait_ge(dist_in, 16)
                for h in heads:
                    nc.scalar.activation(bias[:, h], dist, ACT.Copy, scale=slopes()[h]).then_inc(bias_set, 1)

            for k in range(12):
                front0(0, k)
            split_up0((0, 1))
            front0(0, 12)
            split_up0((2, 3))
            for k in range(13, 15):
                front0(0, k)
            biases(range(0, 6))
            for k in range(15, 18):
                front0(0, k)
            act.wait_ge(up1_in, 16)
            nc.scalar.activation(up_h[1][:].rearrange("p e n -> p (e n)"), raw_up[1], ACT.Copy).then_inc(up_hi[1], 1)
            for k in range(18, ROUTER0):
                front0(0, k)
            front = fronts(front0, front1)
            all_rounds(act, experts(tanh), experts(outputs), heads(scores), front[0], heads(values), front[1])

        @block.vector
        def _(dve):
            for prog in (dve_f0, dve_f1, *dve_moe, dve_heads):
                dve.sem_inc(prog.sem, 2 * prog.per)
            nc.vector.memset(gpad[:], -1.0).then_inc(pad_set, 1)

            def layer_norm_stats(b, f, r, src):
                for t in range(T):
                    ins = nc.vector.bn_stats(stats[r][:, t], src[:, t])
                ins.then_inc(*f(f"stats{r}"))
                dve.wait_ge(*f.at(b, f"stats{r}"))
                dve.sem_inc(dve_met, 1)
                for t in range(T):
                    ins = nc.vector.bn_aggr(mv[r][:, t], stats[r][:, t])
                ins.then_inc(*f(f"aggr{r}"))

            def normalise(dst, src, r):
                for t in range(T):
                    ins = nc.vector.tensor_scalar(dst[:, t], src[:, t], mv[r][:, t, 0:1], rstd[r][:, t:t + 1],
                                                  ALU.subtract, ALU.mult)
                return ins

            def top2_max(b, f, i, src):
                for t in range(T):
                    ins = nc.vector.max(top[i][:, t], src[:, t])
                ins.then_inc(*f(f"max{i}"))
                dve.wait_ge(*f.at(b, f"max{i}"))
                dve.sem_inc(dve_met, 1)
                for t in range(T):
                    ins = nc.vector.max_index(topi[i][:, t], top[i][:, t], src[:, t])
                ins.then_inc(*f(f"idx{i}"))

            def top2_float(b, f, i):
                dve.wait_ge(*f.at(b, f"idx{i}"))
                nc.vector.tensor_copy(topf[i][:], topi[i][:, :, 0:2]).then_inc(*f(f"idxf{i}"))

            def weigh(b, f, i, w):
                for k in range(2):
                    for t in range(T):
                        ins = nc.vector.tensor_scalar(one[i][:, k, t], iota8, topf[i][:, t, k:k + 1], w(k, t),
                                                      ALU.is_equal, ALU.mult)
                ins.then_inc(*f(f"one{i}"))

            def combine(b, f, i):
                dve.wait_ge(*dve_moe[i].at(b - 1, f"y{E - 1}"))
                dve.wait_ge(*f.at(b, f"one{i}"))
                nc.vector.tensor_tensor(cw[i][:], one[i][:, 0], one[i][:, 1], ALU.add).then_inc(*f(f"cw{i}"))

            def front0(b, k):
                if k == 0:
                    dve.wait_ge(x_loaded, b * 16 + 32)
                    layer_norm_stats(b, dve_f0, 0, x_in)
                if k == 2:
                    dve.wait_ge(*pool_f0.at(b, "rstd0"))
                    normalise(xn, x_in, 0).then_inc(*dve_f0("xn0"))
                if k == 4:
                    dve.wait_ge(*dve_f0.at(b, "xn0"))
                    layer_norm_stats(b, dve_f0, 1, xn)
                if k == 6:
                    dve.wait_ge(*pool_f0.at(b, "rstds"))
                    dve.wait_ge(*pe_f1.at(b - 2, "T1"))
                    normalise(tin, xn, 1)
                if k == 7:
                    for t in range(T):
                        ins = nc.vector.tensor_scalar(tin[:, T + t], xn[:, t], rstd[1][:, T + t:T + t + 1], None, ALU.mult)
                    ins.then_inc(*dve_f0("tin0"))
                if k == 11:
                    dve.wait_ge(*pe_f0.at(b, "qk0"))
                    nc.vector.tensor_reduce(nkmax[:], b_front[:, S:2 * S], AX.X, ALU.max, negate=True)\
                        .then_inc(*dve_f0("nkmax"))
                if k == 13:
                    dve.wait_ge(*act_f0.at(b, "kexp"))
                    nc.vector.reciprocal(ksum[:, 1:2], ksum[:, 0:1]).then_inc(*dve_f0("rksum"))
                    dve.wait_ge(*dve_f0.at(b, "rksum"))
                    nc.vector.tensor_scalar(qsT[:], b_front[:, 0:S], ksum[:, 1:2], float(DH0) ** -0.5, ALU.mult, ALU.mult)\
                        .then_inc(*dve_f0("qsT"))
                if k == 15:
                    dve.wait_ge(const_in, 16)
                    dve.wait_ge(*pe_f0.at(b, "ctx"))
                    nc.vector.tensor_tensor(ctxT[:], b_front[:, 0:P], head_mask, ALU.mult).then_inc(*dve_f0("ctxT"))
                if k == 18:
                    dve.wait_ge(*pool_f0.at(b, "start0"))
                    dve.wait_ge(*pe_f0.at(b, "out0"))
                    nc.vector.tensor_tensor(start0[:].rearrange("p t d -> p (t d)"), b_front[:, 0:S],
                                            start0[:].rearrange("p t d -> p (t d)"), ALU.add).then_inc(*dve_f0("out0"))
                    nc.vector.tensor_copy(rt[0][:].rearrange("p t e -> p (t e)"), b_front[:, S:S + T * E])\
                        .then_inc(*dve_f0("rt0"))
                if k == ROUTER0:
                    dve.wait_ge(*dve_f0.at(b, "rt0"))
                    dve.sem_inc(dve_met, 1)
                    top2_max(b, dve_f0, 0, rt[0])
                    top2_float(b, dve_f0, 0)
                    nc.vector.tensor_tensor(tw[0][:, 0], top[0][:, :, 1], top[0][:, :, 0], ALU.subtract)\
                        .then_inc(*dve_f0("gap"))
                if k == 37:
                    dve.wait_ge(*act_f0.at(b, "topexp"))
                    nc.vector.tensor_scalar(tw[0][:, 2], tw[0][:, 1], 1.0, None, ALU.add).then_inc(*dve_f0("den0"))
                    dve.wait_ge(*dve_f0.at(b, "den0"))
                    nc.vector.reciprocal(tw[0][:, 3], tw[0][:, 2]).then_inc(*dve_f0("w1_0"))
                    dve.wait_ge(*dve_f0.at(b, "w1_0"))
                    nc.vector.tensor_tensor(tw[0][:, 4], tw[0][:, 3], tw[0][:, 1], ALU.mult).then_inc(*dve_f0("w2_0"))
                    nc.vector.tensor_scalar(tw[0][:, 5], tw[0][:, 3], 0.5, None, ALU.mult).then_inc(*dve_f0("w1h"))
                    dve.wait_ge(*dve_f0.at(b, "w2_0"))
                    nc.vector.tensor_scalar(tw[0][:, 6], tw[0][:, 4], 0.5, None, ALU.mult).then_inc(*dve_f0("w2h"))
                if k == 38:
                    dve.wait_ge(*dve_f0.at(b, "w2h"))
                    weigh(b, dve_f0, 0, lambda k, t: tw[0][:, 5 + k, t:t + 1])
                    combine(b, dve_f0, 0)

            def front1(b, k):
                if k in (8, 10, 12, 14) and isinstance(b, int) and b == 0:
                    c = (k - 8) // 2
                    dve.wait_ge(up_hi[1], 1)
                    nc.vector.tensor_tensor(quarter(up_l[1], c), quarter(raw_up[1], c), quarter(up_h[1], c).bitcast(F32), ALU.subtract)\
                        .then_inc(up_lo[1], 1)
                if k == 17:
                    dve.wait_ge(*dve_moe[0].at(b, f"y{E - 1}"))
                    layer_norm_stats(b, dve_f1, 2, acc0)
                if k == 19:
                    dve.wait_ge(*pool_f1.at(b, "rstd2"))
                    dve.wait_ge(*pe_f0.at(b + 1, "T0"))
                    normalise(tin[:, T:2 * T], acc0, 2).then_inc(*dve_f1("xn1"))
                if k == 20:
                    dve.wait_ge(*dve_f1.at(b, "xn1"))
                    layer_norm_stats(b, dve_f1, 3, tin[:, T:2 * T])
                if k == 22:
                    dve.wait_ge(*pool_f1.at(b, "rstd3"))
                    normalise(tin, tin[:, T:2 * T], 3).then_inc(*dve_f1("tin1"))
                if k == 25:
                    dve.wait_ge(*act_f1.at(b, "xa_h"))
                    nc.vector.tensor_tensor(xa_l[:], xaT[:], xa_h[:].bitcast(F32), ALU.subtract).then_inc(*dve_f1("xa_l"))
                    dve.wait_ge(*pe_f1.at(b, "logit1"))
                    nc.vector.tensor_copy(rt[1][:].rearrange("p t e -> p (t e)"), b_front[:, 0:T * E]).then_inc(*dve_f1("rt1"))
                    dve.wait_ge(*dve_f1.at(b, "rt1"))
                    nc.vector.tensor_reduce(tw[1][:, 0], rt[1][:], AX.X, ALU.max, negate=True).then_inc(*dve_f1("nrmax"))
                if 27 <= k < 35:
                    n = k - 27
                    dve.wait_ge(*act_f1.at(b, f"sq{n}"))
                    part = ss[:, n // 4, n // 2 % 2, n % 2 * 8:n % 2 * 8 + 8]
                    nc.vector.tensor_reduce(part, sq.rearrange("p (h d) -> p h d", h=8), AX.X, ALU.add).then_inc(*dve_f1(f"ss{n}"))
                    dve.wait_ge(*dve_f1.at(b, f"ss{n}"))
                    nc.vector.tensor_scalar(part, part, 1e-24, None, ALU.max).then_inc(*dve_f1(f"floor{n}"))
                if k == 35:
                    dve.wait_ge(*act_f1.at(b, "rexp1"))
                    nc.vector.reciprocal(tw[1][:, 2], tw[1][:, 1]).then_inc(*dve_f1("rsum"))
                    dve.wait_ge(*dve_f1.at(b, "rsum"))
                    for t in range(T):
                        ins = nc.vector.tensor_scalar(prob[:, t], prob[:, t], tw[1][:, 2, t:t + 1], None, ALU.mult)
                    ins.then_inc(*dve_f1("prob"))
                    dve.wait_ge(*dve_f1.at(b, "prob"))
                    dve.wait_ge(pad_set, 1)
                    nc.vector.tensor_reduce(gpad[:, :, 0:GROUPS], prob[:].rearrange("p t (g e) -> p t g e", g=GROUPS), AX.X, ALU.max)\
                        .then_inc(*dve_f1("group"))
                if k == 36:
                    dve.wait_ge(*dve_f1.at(b, "group"))
                    dve.sem_inc(dve_met, 1)
                    for t in range(T):
                        ins = nc.vector.max(gtop[:, t], gpad[:, t])
                    ins.then_inc(*dve_f1("gmax"))
                    dve.wait_ge(*dve_f1.at(b, "gmax"))
                    dve.sem_inc(dve_met, 1)
                    for t in range(T):
                        ins = nc.vector.max_index(gidx[:, t], gtop[:, t], gpad[:, t])
                    ins.then_inc(*dve_f1("gidx"))
                    dve.wait_ge(*dve_f1.at(b, "gidx"))
                    nc.vector.tensor_copy(gidxf[:], gidx[:, :, 0:2]).then_inc(*dve_f1("gidxf"))
                if k == 37:
                    dve.wait_ge(*dve_f1.at(b, "gidxf"))
                    for c in range(2):
                        for t in range(T):
                            ins = nc.vector.tensor_scalar(gmask[:, t, c], iota8[:, 0:GROUPS], gidxf[:, t, c:c + 1], None, ALU.is_equal)
                    ins.then_inc(*dve_f1("gone"))
                    dve.wait_ge(*dve_f1.at(b, "gone"))
                    nc.vector.tensor_tensor(gmask[:, :, 0], gmask[:, :, 0], gmask[:, :, 1], ALU.add).then_inc(*dve_f1("gmask"))
                    dve.wait_ge(*dve_f1.at(b, "gmask"))
                    for t in range(T):
                        ins = nc.vector.tensor_tensor(masked[:, t].rearrange("p (g e) -> p g e", g=GROUPS),
                                                      prob[:, t].rearrange("p (g e) -> p g e", g=GROUPS),
                                                      gmask[:, t, 0].unsqueeze(2).to_broadcast([P, GROUPS, E // GROUPS]), ALU.mult)
                    ins.then_inc(*dve_f1("masked"))
                if k == 38:
                    dve.wait_ge(*dve_f1.at(b, "masked"))
                    dve.sem_inc(dve_met, 1)
                    top2_max(b, dve_f1, 1, masked)
                if k == 39:
                    top2_float(b, dve_f1, 1)
                    nc.vector.tensor_tensor(tw[1][:, 3], top[1][:, :, 0], top[1][:, :, 1], ALU.add).then_inc(*dve_f1("den1"))
                    dve.wait_ge(*dve_f1.at(b, "den1"))
                    nc.vector.reciprocal(tw[1][:, 4], tw[1][:, 3]).then_inc(*dve_f1("rden"))
                    dve.wait_ge(*dve_f1.at(b, "rden"))
                    nc.vector.tensor_scalar(tw[1][:, 5], tw[1][:, 4], 0.5, None, ALU.mult).then_inc(*dve_f1("rdenh"))
                    dve.wait_ge(*dve_f1.at(b, "rdenh"))
                    for c in range(2):
                        ins = nc.vector.tensor_tensor(tw[1][:, 6 + c], top[1][:, :, c], tw[1][:, 5], ALU.mult)
                    ins.then_inc(*dve_f1("tw1"))
                if k == 40:
                    dve.wait_ge(*dve_f1.at(b, "tw1"))
                    weigh(b, dve_f1, 1, lambda k, t: tw[1][:, 6 + k, t:t + 1])
                if 29 <= k < 37 and isinstance(b, int) and b == 0:
                    n = k - 29
                    dve.wait_ge(*pool_f1.at(b, f"rn{n}"))
                    dve.wait_ge(*act_f1.at(b, f"sq{n}"))
                    unit_vectors(nc.vector, n)
                if k == PIECES - 1:
                    combine(b, dve_f1, 1)

            def expert_gate(b, layer, e):
                f = dve_moe[layer]
                dve.wait_ge(*act_moe[layer].at(b, f"th{e}"))
                nc.vector.scalar_tensor_tensor(out=th[e % 2][:], in0=th[e % 2][:], scalar=1.0, in1=b_gate[:],
                                               op0=ALU.add, op1=ALU.mult).then_inc(*f(f"ga{e}"))

            def expert_hidden(b, layer, e):
                f = dve_moe[layer]
                dve.wait_ge(*f.at(b, f"ga{e}"))
                dve.wait_ge(*pe_moe[layer].at(b, f"u{e}"))
                nc.vector.tensor_tensor(th[e % 2][:], b_up[:], th[e % 2][:], ALU.mult)\
                    .then_inc(*f(f"hid{e}"))

            def expert_out(b, layer, e, m0, p):
                f, acc, start = dve_moe[layer], (acc0, acc1)[layer], start1
                dve.wait_ge(*pe_moe[layer].at(b, f"dn{e}"))
                if e == 0 and layer == 1:
                    dve.wait_ge(*dve_f1.at(b, "cw1"))
                    dve.wait_ge(*pool_f1.at(b, "start1"))
                    dve.wait_ge(out_stored, b * 16 + 16)
                if e:
                    dve.wait_ge(*added(b, layer, e - 1))
                for half in [h for q in range(p + 1) for h in halves_at(q, 8)][-1:] if layer else []:
                    dve.wait_ge(*dve_heads.at(b, f"add{half}"))
                for t in range(T):
                    begin = e == 0 and not (layer and m0 and t == 0)
                    ins = nc.vector.scalar_tensor_tensor(out=acc[:, t], in0=b_y[:, t * D:(t + 1) * D],
                                                         scalar=cw[layer][:, t, e:e + 1], in1=(start if begin else acc)[:, t],
                                                         op0=ALU.mult, op1=ALU.add)
                ins.then_inc(*f(f"y{e}"))

            def outputs(b, p, m0, m1):
                for layer, e in experts_at(p - 1, m0, m1):
                    if not pooled(layer, e):
                        expert_out(b + 1 - layer, layer, e, m0, p)

            def hidden(b, p, m0, m1):
                for layer, e in experts_at(p, m0, m1):
                    expert_hidden(b + 1 - layer, layer, e)
                if p == 0 and isinstance(b, int) and b == -1:
                    for k in range(ROUTER0, PIECES):
                        front0(0, k)

            def sums(b, p, m0, m1):
                if p < STEPS:
                    qt, h = p // HP, 2 * (p % HP)
                    dve.wait_ge(*act_heads.at(b, f"expB{p}"))
                    nc.vector.reciprocal(rl[:, qt, h:h + 2], lsum[:, qt, h:h + 2]).then_inc(*dve_heads(f"rl{p}"))

            def gates(b, p, m0, m1):
                for layer, e in experts_at(p, m0, m1):
                    expert_gate(b + 1 - layer, layer, e)

            def scores(b, p, m0, m1):
                qt = p // HP
                n = NULL + P * (qt + 1)
                for half in halves_at(p, 8):
                    dve.wait_ge(*pe_heads.at(b, f"op{half}"))
                    begin = half == 0 and not (isinstance(b, int) and b == B - 1)
                    if begin:
                        dve.wait_ge(*pool_f1.at(b, "start1"))
                        dve.wait_ge(out_stored, b * 16 + 16)
                    for _, e in [x for q in range(p - 1) for x in experts_at(q, m0, m1) if x[0] == 1][-1:]:
                        dve.wait_ge(*dve_moe[1].at(b, f"y{e}"))
                    if half:
                        dve.wait_ge(*dve_heads.at(b, f"add{half - 1}"))
                    nc.vector.tensor_tensor(acc1[:, half // 2], b_y[:, 0:D], (start1 if begin else acc1)[:, half // 2], ALU.add)\
                        .then_inc(*dve_heads(f"add{half}"))
                for half in halves_at(p, 6):
                    dve.wait_ge(*pe_heads.at(b, f"pnT{half}"))
                    nc.vector.tensor_copy(pnT[:], b_y[0:NULL_ROWS, D:D + P]).then_inc(*dve_heads(f"pnT{half}"))
                if 1 <= p <= STEPS:
                    p1 = p - 1
                    q1, h1, n1 = p1 // HP, 2 * (p1 % HP), NULL + P * (p1 // HP + 1)
                    dve.wait_ge(*dve_heads.at(b, f"rl{p1}"))
                    for i in range(2):
                        ins = nc.vector.tensor_scalar(prb[p1 % 2][:, i, 0:n1], prb[p1 % 2][:, i, 0:n1], rl[:, q1, h1 + i:h1 + i + 1],
                                                      None, ALU.mult)
                    ins.then_inc(*dve_heads(f"norm{p1}"))
                if p < STEPS:
                    if p == 0:
                        dve.wait_ge(bias_set, H1)
                    for i, ab in enumerate("AB"):
                        h = 2 * (p % HP) + i
                        if p >= 2:
                            dve.wait_ge(*pe_heads.at(b, f"prT{p - 2}"))
                            dve.wait_ge(*pool_heads.at(b, f"pnl{p - 2}"))
                        dve.wait_ge(*pe_heads.at(b, f"sim{ab}{p}"))
                        dve.sem_inc(dve_met, 1)
                        nc.vector.tensor_tensor_reduce(prb[p % 2][:, i, 0:n], b_sim[i][:, 0:n],
                                                       bias[:, h, KEYS - n:KEYS], 1.0, float(np.finfo(np.float32).max),
                                                       ALU.add, ALU.min, mneg[:, qt, h:h + 1])\
                            .then_inc(*dve_heads(f"sim{ab}{p}"))

            def split_up0(parts):
                for c in parts:
                    dve.wait_ge(up_hi[0], c + 1)
                    nc.vector.tensor_tensor(quarter(up_l[0], c), quarter(raw_up[0], c), quarter(up_h[0], c).bitcast(F32), ALU.subtract)\
                        .then_inc(up_lo[0], 1)

            for k in range(12):
                front0(0, k)
            split_up0((0,))
            for k in range(12, 14):
                front0(0, k)
            dve.wait_ge(null_in, 16)
            nc.vector.tensor_tensor(nk_sq, nkw[:], nkw[:], ALU.mult).then_inc(null_dve, 1)
            dve.wait_ge(null_dve, 1)
            nc.vector.tensor_reduce(nk_ss[:, 0:2], nk_sq, AX.X, ALU.add).then_inc(null_dve, 1)
            dve.wait_ge(null_dve, 2)
            nc.vector.tensor_scalar(nk_ss[:, 0:2], nk_ss[:, 0:2], 1e-24, None, ALU.max).then_inc(null_dve, 1)
            split_up0((1, 2))
            for k in range(14, 16):
                front0(0, k)
            dve.wait_ge(null_pool, 1)
            nc.vector.tensor_scalar(nkw[:], nkw[:], nk_ss[:, 2:3], None, ALU.mult).then_inc(null_dve, 1)
            dve.wait_ge(small_in, 16)
            nc.vector.tensor_tensor(qscale[:], qs2, ks2, ALU.mult).then_inc(qscale_set, 1)
            dve.wait_ge(qscale_set, 1)
            nc.vector.tensor_scalar(qscale[:], qscale[:], -SIM_SCALE, None, ALU.mult).then_inc(qscale_set, 1)
            split_up0((3,))
            for k in range(16, ROUTER0):
                front0(0, k)
            dve.wait_ge(up_lo[0], 4)
            dve.wait_ge(null_pe, 1)
            turned = b_pv[:, 0:NULL * H1].rearrange("p (h i j) -> p h i j", i=2, j=NULL)
            for i in range(2):
                ch = slice(i * DH1, (i + 1) * DH1)
                nc.vector.tensor_copy(kT[ch, :, 0:NULL], turned[ch, :, i]).then_inc(null_dve, 1)
            front = fronts(front0, front1)
            all_rounds(dve, heads(scores), experts(gates), experts(outputs), experts(hidden), heads(sums), front[0], front[1])

        @block.tensor
        def _(pe):
            for prog in (pe_f0, pe_f1, *pe_moe, pe_heads):
                pe.sem_inc(prog.sem, 2 * prog.per)

            def matmul3(ps, w_h, w_l, x_h, x_l, start=True):
                nc.tensor.matmul(ps, w_h, x_h, start=start, stop=False, skip_group_check=True)
                nc.tensor.matmul(ps, w_h, x_l, start=False, stop=False, skip_group_check=True)
                return nc.tensor.matmul(ps, w_l, x_h, start=False, stop=True, skip_group_check=True)

            def turn_inputs(b, f, r):
                pe.wait_ge(const_in, 16)
                pe.wait_ge(*f.at(b, f"tin{r}"))
                for i in range(2 * T):
                    ins = nc.tensor.transpose(b_front[:, i * P:(i + 1) * P], tin[:, i], ident)
                return ins

            def front0(b, k):
                if k == 9:
                    pe.wait_ge(*act_f1.at(b - 2, "v3"))
                    turn_inputs(b, dve_f0, 0).then_inc(*pe_f0("T0"))
                if k == 11:
                    pe.wait_ge(small_in, 16)
                    pe.wait_ge(*act_f0.at(b, "xfT"))
                    nc.tensor.matmul(b_front[:, 0:S], wq0, xaT[:], start=True, stop=True)
                    nc.tensor.matmul(b_front[:, S:2 * S], wk0, xaT[:], start=True, stop=True).then_inc(*pe_f0("qk0"))
                if k == 14:
                    pe.wait_ge(*dve_f0.at(b, "qsT"))
                    for t in range(T):
                        nc.tensor.matmul(b_front[:, t * P:(t + 1) * P], xaT[:, t * P:(t + 1) * P], wv0, start=True, stop=True)
                    for t in range(T):
                        ins = nc.tensor.transpose(b_front[:, S + t * P:S + (t + 1) * P], keT[:, t * P:(t + 1) * P], ident)
                    ins.then_inc(*pe_f0("vk0"))
                if k == 15:
                    pe.wait_ge(*act_f0.at(b, "vk"))
                    for t in range(T):
                        ins = nc.tensor.matmul(b_front[:, 0:P], vk[:, 0, t], vk[:, 1, t], start=(t == 0), stop=(t == T - 1))
                    ins.then_inc(*pe_f0("ctx"))
                if k == 16:
                    pe.wait_ge(*dve_f0.at(b, "ctxT"))
                    nc.tensor.matmul(b_front[:, 0:D], ctxT[:], wout0, start=True, stop=True).then_inc(*pe_f0("mix"))
                if k == 18:
                    pe.wait_ge(*act_f0.at(b, "mix"))
                    for t in range(T):
                        nc.tensor.matmul(b_front[:, t * D:(t + 1) * D], qsT[:, t * P:(t + 1) * P], mix[:], start=True, stop=False)
                        nc.tensor.matmul(b_front[:, t * D:(t + 1) * D], ones_row, b_out, start=False, stop=True)
                    for t in range(T):
                        ins = nc.tensor.matmul(b_front[:, S + t * E:S + (t + 1) * E], xfT[:, t * P:(t + 1) * P], router0,
                                               start=True, stop=True)
                    ins.then_inc(*pe_f0("out0"))

            def project_qk(ps, t, c):
                tok = slice(t * P, (t + 1) * P)
                return matmul3(ps[:], xa_h[:, tok], xa_l[:, tok], wqk_h[:, c:c + 512], wqk_l[:, c:c + 512])

            def project_v(ps, t, c):
                return nc.tensor.matmul(ps[:], xaT[:, t * P:(t + 1) * P], wv1[:, c:c + 512], start=True, stop=True)

            def turn_bank_free(b, name):
                m = TURNS.index(name)
                if m >= 3:
                    pe.wait_ge(*act_f1.at(b, TURNS[m - 3]))
                else:
                    pe.wait_ge(*(dve_heads.at(b - 1, f"sim{'AB'[m - 1]}{STEPS - 1}") if m else act_f1.at(b, "proj7")))

            def front1(b, k):
                if k == 24:
                    pe.wait_ge(*dve_f0.at(b + 1, "rt0"))
                    turn_inputs(b, dve_f1, 1).then_inc(*pe_f1("T1"))
                if k == 25:
                    pe.wait_ge(*act_f1.at(b, "xfT1"))
                    for t in range(T):
                        ins = nc.tensor.matmul(b_front[:, t * E:(t + 1) * E], xfT[:, t * P:(t + 1) * P], router1, start=True, stop=True)
                    ins.then_inc(*pe_f1("logit1"))
                if 26 <= k < 34:
                    n = k - 26
                    back = n - (3 if proj_bank(b, 1) is b_sim[0] else 1)
                    pe.wait_ge(*(act_f1.at(b, f"proj{back}") if back >= 0 else dve_f1.at(b, "rt1")))
                    if n == 0:
                        pe.wait_ge(wqk_lo, 2)
                    project_qk(proj_bank(b, n), n // 2 % 2, n // 4 * HD1 + n % 2 * 512).then_inc(*pe_f1(f"proj{n}"))
                if 34 <= k < 42:
                    n = k - 34
                    w, t, g = n // 4, n // 2 % 2, n % 2
                    turn_bank_free(b, f"qkT{n}")
                    pe.wait_ge(*unit.at(b, f"nrm{n}"))
                    for i in range(4):
                        hp = 4 * g + i
                        ins = nc.tensor.transpose(turn_bank(f"qkT{n}")[:, i * P:(i + 1) * P], qk[:, w, t, hp * P:(hp + 1) * P], ident)
                    ins.then_inc(*pe_f1(f"qkT{n}"))
                if 38 <= k < 42:
                    n = k - 38
                    turn_bank_free(b, f"v{n}")
                    if n == 0:
                        pe.wait_ge(wv_in, 16)
                    project_v(turn_bank(f"v{n}"), n // 2, n % 2 * 512).then_inc(*pe_f1(f"v{n}"))

            def expert_up(b, layer, e, name):
                if e == 0 and name == "g":
                    pe.wait_ge(up_lo[layer], 4)
                    pe.wait_ge(*(pool_f1.at(b, "xfl1") if layer else pool_f0.at(b, "xfl")))
                l1, b1, e1 = expert_before(b, layer, e)
                ps, free = {"g": (b_gate, "ga"), "u": (b_up, "hid")}[name]
                pe.wait_ge(*dve_moe[l1].at(b1, f"{free}{e1}"))
                c = HID if (name == "g") == (layer == 0) else 0
                for a in range(HB):
                    cs = slice(c + a * P, c + (a + 1) * P)
                    ins = matmul3(ps[:, a * S:(a + 1) * S], up_h[layer][:, e, cs], up_l[layer][:, e, cs],
                                  xf_h[layer][:], xf_l[layer][:])
                ins.then_inc(*pe_moe[layer](f"{name}{e}"))

            def shared_bank_free(b, steps):
                for p in steps:
                    for half in halves_at(p, 6):
                        pe.wait_ge(*dve_heads.at(b, f"pnT{half}"))
                    for half in halves_at(p, 8):
                        pe.wait_ge(*dve_heads.at(b, f"add{half}"))

            def expert_down(b, layer, e, p, h):
                if e == 0:
                    pe.wait_ge((dn0_in, dn1_in)[layer], 16)
                l1, b1, e1 = expert_before(b, layer, e)
                pe.wait_ge(*taken(b1, l1, e1))
                if h:
                    shared_bank_free(b - 1 + layer, [p - 1, p])
                pe.wait_ge(*dve_moe[layer].at(b, f"hid{e}"))
                for t in range(T):
                    for a in range(HB):
                        ins = nc.tensor.matmul(b_y[:, t * D:(t + 1) * D], th[e % 2][:, a * S + t * P:a * S + (t + 1) * P], down[layer][:, e, a],
                                               start=(a == 0), stop=(a == HB - 1), skip_group_check=True)
                ins.then_inc(*pe_moe[layer](f"dn{e}"))

            def outputs(b, p, m0, m1):
                for layer, e in experts_at(p - 1, m0, m1):
                    expert_down(b + 1 - layer, layer, e, p, m1)

            def gates(b, p, m0, m1):
                for layer, e in experts_at(p, m0, m1):
                    expert_up(b + 1 - layer, layer, e, "g")

            def ups(b, p, m0, m1):
                for layer, e in experts_at(p, m0, m1):
                    expert_up(b + 1 - layer, layer, e, "u")

            def scores(b, p, m0, m1):
                qt = p // HP
                toks = slice(qt * P, (qt + 1) * P)
                if halves_at(p, 6) + halves_at(p, 8):
                    shared_bank_free(b, [p - 2])
                    layer, e = [x for q in range(p - 1) for x in experts_at(q, m0, m1)][-1]
                    pe.wait_ge(*taken(b + 1 - layer, layer, e))
                for half in halves_at(p, 6):
                    pe.wait_ge(*pool_heads.at(b, f"pnl{4 * half + 3}"))
                    nc.tensor.transpose(b_y[0:NULL_ROWS, D:D + P], pn3[:].bitcast(F32), ident).then_inc(*pe_heads(f"pnT{half}"))
                for half in halves_at(p, 8):
                    pe.wait_ge(wout_in, 16)
                    pe.wait_ge(*act_heads.at(b, f"oT{half}"))
                    for i in range(4):
                        ins = nc.tensor.matmul(b_y[:, 0:D], oT[:, i], wout1[:, half % 2 * 4 + i], start=(i == 0), stop=(i == 3))
                    ins.then_inc(*pe_heads(f"op{half}"))
                if p < STEPS:
                    hp = p % HP
                    if p == 0:
                        pe.wait_ge(null_dve, 6)
                        pe.wait_ge(*act_f1.at(b, "v3"))
                    for i, ab in enumerate("AB"):
                        ch = slice(i * DH1, (i + 1) * DH1)
                        if p:
                            pe.wait_ge(*dve_heads.at(b, f"sim{ab}{p - 1}"))
                        else:
                            pe.wait_ge(*dve_heads.at(b - 1, f"sim{ab}{STEPS - 1}"))
                        n = NULL + P * (qt + 1)
                        nc.tensor.matmul(b_sim[i][:, 0:n], qT[ch, hp, toks], kT[ch, hp, 0:n], start=True, stop=True)\
                            .then_inc(*pe_heads(f"sim{ab}{p}"))

            def values(b, p, m0, m1):
                if 1 <= p <= STEPS:
                    p1 = p - 1
                    nc1 = p1 // HP + 1
                    pe.wait_ge(*(act_heads.at(b, f"prT{p1 - 1}") if p1 else act_heads.at(b - 1, f"prT{STEPS - 1}")))
                    pe.wait_ge(*dve_heads.at(b, f"norm{p1}"))
                    for i in range(2):
                        for c in range(nc1):
                            ins = nc.tensor.transpose(b_prT[:, (i * nc1 + c) * P:(i * nc1 + c + 1) * P],
                                                      prb[p1 % 2][:, i, NULL + c * P:NULL + (c + 1) * P], ident)
                    ins.then_inc(*pe_heads(f"prT{p1}"))
                if 3 <= p < STEPS + 3:
                    p3 = p - 3
                    q3 = p3 // HP
                    if p3 % 4 == 0:
                        pe.wait_ge(*(act_heads.at(b, f"oT{p3 // 4 - 1}") if p3 else act_heads.at(b - 1, f"oT{STEPS // 4 - 1}")))
                    if p3 == 0:
                        pe.wait_ge(*act_f1.at(b, "v3"))
                    pe.wait_ge(*act_heads.at(b, f"prT{p3}"))
                    at = p3 % 4 * P
                    for c in range(q3 + 1):
                        for i in range(2):
                            h = 2 * (p3 % HP) + i
                            ins = nc.tensor.matmul(b_pv[i * DH1:(i + 1) * DH1, at:at + P], v[:, c, h * DH1:(h + 1) * DH1],
                                                   prT[p3 % 3][:, i, c * P:(c + 1) * P], start=(p3 % 4 == 0 and c == 0),
                                                   stop=False, skip_group_check=True)
                    ins.then_inc(*pe_heads(f"pv{p3}"))
                for half in halves_at(p, 6):
                    pe.wait_ge(*dve_heads.at(b, f"pnT{half}"))
                    for i in range(4):
                        ins = nc.tensor.matmul(b_pv[:, i * P:(i + 1) * P], nvbd[:, half % 2, i * P:(i + 1) * P], pnT[:], start=False,
                                               stop=(i == 3), skip_group_check=True)
                    ins.then_inc(*pe_heads(f"pvn{half}"))

            for k in range(PIECES):
                front0(0, k)
            pe.wait_ge(null_dve, 4)
            nc.tensor.transpose(b_pv[:, 0:NULL * H1], nkw[:].rearrange("p a d -> p (a d)"), ident[0:NULL * H1, 0:NULL * H1])\
                .then_inc(null_pe, 1)
            front = fronts(front0, front1)
            all_rounds(pe, heads(scores), experts(gates), experts(outputs), experts(ups), front[0], heads(values), front[1])


def table(widths):
    out, at = {}, 0
    for name, n in widths:
        out[name] = (at, n)
        at += n
    return out, at


SMALL, SMALL_COLS = table([("wq0", P), ("wk0", P), ("wv0", P), ("wout0", D), ("router0", E), ("router1", E), ("b_out", D),
                           ("gamma0", 1), ("beta0", 1), ("rms", 1), ("gamma1", 1), ("qs2", 1), ("ks2", 1)])
CONST, CONST_COLS = table([("ident", P), ("ones", P), ("head_mask", P), ("iota8", E)])


def constants():
    c = np.zeros((P, CONST_COLS), np.float32)

    def put(name, a):
        at, n = CONST[name]
        c[:, at:at + n] = a

    row = np.arange(P)[:, None]
    put("ident", np.eye(P))
    put("ones", 1.0)
    put("head_mask", (row // DH0) == (np.arange(P)[None, :] // DH0))
    put("iota8", np.arange(E)[None, :])
    return c


def distances():
    d = P + NULL + np.arange(P)[:, None] - np.arange(KEYS)[None, :]
    return np.where(d < 0, np.float32(FAR), d.astype(np.float32))


def kernel(**inputs):
    import numpy as _np
    import concourse.bacc as _bacc
    from concourse import mybir as _mybir
    from concourse.bass_utils import run_bass_kernel_spmd as _run

    a = {k: _np.asarray(v) for k, v in inputs.items()}
    qkv0 = a["L0_attn_w_qkv"]
    parts = {
        "wq0": qkv0[:, 0:P], "wk0": qkv0[:, P:2 * P], "wv0": qkv0[:, 2 * P:3 * P], "wout0": a["L0_attn_w_out"],
        "router0": a["L0_ffn_w_router"].T, "router1": a["L1_ffn_gate_w"].T,
        "b_out": _np.broadcast_to(a["L0_attn_b_out"][None, :], (P, D)),
        "gamma0": a["L0_attn_gamma"].reshape(D, 1), "beta0": a["L0_attn_beta"].reshape(D, 1),
        "rms": a["L0_ffn_norm_scale"].reshape(D, 1), "gamma1": a["L1_attn_gamma"].reshape(D, 1),
        "qs2": _np.concatenate([a["L1_attn_q_scale"]] * 2).reshape(P, 1),
        "ks2": _np.concatenate([a["L1_attn_k_scale"]] * 2).reshape(P, 1),
    }
    null = a["L1_attn_null_kv"].reshape(H1, NULL, 2, DH1)
    null_k = null[:, :, 0].reshape(H1 * NULL, DH1)
    null_v = _np.zeros((HALF, NULL, T, HALF, DH1), null.dtype)
    for h in range(H1):
        null_v[h % HALF, :, h // HALF, h % HALF] = null[h, :, 1]
    arrays = {
        "x": a["L0_attn_x"],
        "w_small": _np.concatenate([parts[n] for n in SMALL], axis=1),
        "w_up0": a["L0_ffn_w_up"].transpose(2, 0, 1).reshape(D, -1),
        "w_dn0": a["L0_ffn_w_down"].reshape(E, D, HB, P).transpose(3, 0, 2, 1).reshape(P, -1),
        "w_qk1": _np.concatenate([a["L1_attn_w_q"], a["L1_attn_w_kv"][:, 0:HD1]], axis=1),
        "w_v1": a["L1_attn_w_kv"][:, HD1:2 * HD1],
        "w_out1": a["L1_attn_w_out"].reshape(HP, P, D).transpose(1, 0, 2).reshape(P, -1),
        "w_up1": a["L1_ffn_w13_weight"].transpose(2, 0, 1).reshape(D, -1),
        "w_dn1": a["L1_ffn_w2_weight"].reshape(E, D, HB, P).transpose(3, 0, 2, 1).reshape(P, -1),
        "null_k": _np.concatenate([null_k, null_k], axis=1),
        "null_v": null_v.reshape(HALF * NULL, -1),
        "consts": constants(),
        "distance": distances(),
    }
    arrays = {n: _np.ascontiguousarray(v) for n, v in arrays.items()}
    nc = _bacc.Bacc("TRN2", target_bir_lowering=False, num_devices=1)
    args = [nc.dram_tensor(n, v.shape, _mybir.dt.from_np(v.dtype), kind="ExternalInput").ap() for n, v in arrays.items()]
    args.append(nc.dram_tensor("result", (B, S, D), _mybir.dt.float32, kind="ExternalOutput").ap())
    build(nc, *args)
    r = _run(nc, [arrays], core_ids=[0])
    return r.results[0]["result"]
```
